# Optimizing a Trainium2 kernel written in Bass

```python
import numpy as np
import jax
import jax.numpy as jnp

def _softmax(x, axis=-1):
    return jax.nn.softmax(x, axis=axis)

def _gelu(x):
    return jax.nn.gelu(x, approximate=True)

def _silu(x):
    return jax.nn.silu(x)

def _sigmoid(x):
    return jax.nn.sigmoid(x)

def _layernorm(x, axis=-1, eps=1e-05):
    m = jnp.mean(x, axis=axis, keepdims=True)
    v = jnp.var(x, axis=axis, keepdims=True)
    return (x - m) / jnp.sqrt(v + eps)

def _scatter_add(tgt, idx, src, axis=0):
    return tgt.at[idx].add(src)

def _segment_sum(src, seg, n):
    return jax.ops.segment_sum(src, seg, n)
kernel_name = 'mk_sandwich_d1_jaxref_r8_8ae75c'

def setup_inputs(seed: int=0):
    np.random.seed(seed)
    _w = jnp.asarray

    def _L0_attn_setup():
        import math
        import jax, jax.numpy as jnp
        import numpy as np
        B, T, IN, HID, H, D = (8, 256, 128, 128, 8, 64)
        HD = H * D

        def _mlstm_forward(x, Wq, Wk, Wv, Wi, bi, Wf, bf, Wo, bo, W_out, ln_g, ln_b):
            Bb, Tt, _ = x.shape
            q = (x @ Wq.T).reshape(Bb, Tt, H, D)
            k = (x @ Wk.T).reshape(Bb, Tt, H, D) / math.sqrt(D)
            v = (x @ Wv.T).reshape(Bb, Tt, H, D)
            i_g = jnp.exp(x @ Wi.T + bi)
            f_g = jnp.exp(x @ Wf.T + bf)
            o_g = jax.nn.sigmoid(x @ Wo.T + bo).reshape(Bb, Tt, H, D)

            def step(carry, inp):
                C, n = carry
                qt, kt, vt, it, ft, ot = inp
                C = ft[:, :, None, None] * C + it[:, :, None, None] * (vt[:, :, :, None] * kt[:, :, None, :])
                n = ft[:, :, None] * n + it[:, :, None] * kt
                h = jnp.einsum('bhde,bhe->bhd', C, qt)
                denom = jnp.maximum(jnp.abs(jnp.sum(n * qt, axis=-1)), 1.0)
                h = h / denom[:, :, None] * ot
                return ((C, n), h)
            xs = tuple((jnp.moveaxis(a, 1, 0) for a in (q, k, v, i_g, f_g, o_g)))
            C0 = jnp.zeros((Bb, H, D, D), x.dtype)
            n0 = jnp.zeros((Bb, H, D), x.dtype)
            (C, n), hs = jax.lax.scan(step, (C0, n0), xs)
            hs = jnp.moveaxis(hs, 0, 1).reshape(Bb, Tt, HD)
            mu = jnp.mean(hs, axis=-1, keepdims=True)
            var = jnp.var(hs, axis=-1, keepdims=True)
            hn = (hs - mu) * jax.lax.rsqrt(var + 1e-05) * ln_g + ln_b
            out = hn @ W_out.T
            return (out, C, n)

        def _reference_tuple_inner(x, Wq, Wk, Wv, Wi, bi, Wf, bf, Wo, bo, W_out, ln_g, ln_b):
            out, C, n = _mlstm_forward(x, Wq, Wk, Wv, Wi, bi, Wf, bf, Wo, bo, W_out, ln_g, ln_b)
            return (out, (C, n))
        key = jax.random.key(seed)
        ks = jax.random.split(key, 13)
        s = 0.02
        gs = 0.001
        f32 = jnp.float32
        return {'x': jax.random.normal(ks[0], (B, T, IN), f32), 'Wq': jax.random.normal(ks[1], (HD, IN), f32) * s, 'Wk': jax.random.normal(ks[2], (HD, IN), f32) * s, 'Wv': jax.random.normal(ks[3], (HD, IN), f32) * s, 'Wi': jax.random.normal(ks[4], (H, IN), f32) * gs, 'bi': jnp.zeros((H,), f32), 'Wf': jax.random.normal(ks[5], (H, IN), f32) * gs, 'bf': jnp.zeros((H,), f32), 'Wo': jax.random.normal(ks[6], (HD, IN), f32) * s, 'bo': jnp.zeros((HD,), f32), 'W_out': jax.random.normal(ks[7], (HID, HD), f32) * s, 'ln_g': jnp.ones((HD,), f32), 'ln_b': jnp.zeros((HD,), f32)}
    _L0_attn_in = _L0_attn_setup()

    def _L0_ffn_setup():
        import jax, jax.numpy as jnp
        import numpy as np
        DIM = 128
        DEPTH = 2
        HEADS = 8
        DIM_HEAD = 64
        WINDOW = 64
        INNER = HEADS * DIM_HEAD
        HID = int(DIM * 4 * 2 / 3)
        B, N = (2, 1024)
        QK_SCALE = 8.0

        def shift_token(t):
            t1, t2 = jnp.split(t, 2, axis=-1)
            t2 = jnp.pad(t2, ((0, 0), (1, 0), (0, 0)))[:, :-1]
            return jnp.concatenate([t1, t2], axis=-1)

        def l2norm(t):
            return t / jnp.clip(jnp.linalg.norm(t, axis=-1, keepdims=True), 1e-12)

        def rotate_half(x):
            x1, x2 = jnp.split(x, 2, axis=-1)
            return jnp.concatenate([-x2, x1], axis=-1)

        def rotary_xpos(q, k):
            n = q.shape[-2]
            half_idx = jnp.arange(0, DIM_HEAD, 2, dtype=jnp.float32)
            inv_freq = 1.0 / 10000.0 ** (half_idx / DIM_HEAD)
            t = jnp.arange(n, dtype=jnp.float32)
            freqs = t[:, None] * inv_freq[None, :]
            freqs = jnp.concatenate([freqs, freqs], axis=-1)
            base = (half_idx + 0.4 * DIM_HEAD) / (1.4 * DIM_HEAD)
            power = (t - n // 2) / float(WINDOW // 2)
            scale = base[None, :] ** power[:, None]
            scale = jnp.concatenate([scale, scale], axis=-1)
            cos, sin = (jnp.cos(freqs), jnp.sin(freqs))
            q = q * cos * scale + rotate_half(q) * sin * scale
            k = k * cos / scale + rotate_half(k) * sin / scale
            return (q, k)

        def local_attention(q, k, v):
            b, h, n, d = q.shape
            w = n // WINDOW
            bq = q.reshape(b, h, w, WINDOW, d) * QK_SCALE
            bk = k.reshape(b, h, w, WINDOW, d)
            bv = v.reshape(b, h, w, WINDOW, d)

            def look_around(t):
                p = jnp.pad(t, ((0, 0), (0, 0), (1, 0), (0, 0), (0, 0)))
                return jnp.concatenate([p[:, :, :w], p[:, :, 1:]], axis=3)
            bk, bv = (look_around(bk), look_around(bv))
            bt = jnp.arange(n).reshape(w, WINDOW)
            btp = jnp.pad(bt, ((1, 0), (0, 0)), constant_values=-1)
            btk = jnp.concatenate([btp[:w], btp[1:]], axis=1)
            sim = jnp.einsum('bhwid,bhwjd->bhwij', bq, bk)
            i = bt[:, :, None]
            j = btk[:, None, :]
            mask = (i < j) | (i > j + WINDOW) | (j == -1)
            sim = jnp.where(mask, -jnp.finfo(sim.dtype).max, sim)
            attn = jax.nn.softmax(sim, axis=-1)
            out = jnp.einsum('bhwij,bhwjd->bhwid', attn, bv)
            return out.reshape(b, h, n, d)

        def _layer(x, wqkv, qs, ksc, wo, lg, lb, w1, b1, w2, b2):
            b, n, _ = x.shape
            h = shift_token(x)
            qkv = h @ wqkv
            q, k, v = jnp.split(qkv, 3, axis=-1)
            to_heads = lambda t: t.reshape(b, n, HEADS, DIM_HEAD).transpose(0, 2, 1, 3)
            q, k, v = (to_heads(q), to_heads(k), to_heads(v))
            q = l2norm(q) * qs
            k = l2norm(k) * ksc
            q, k = rotary_xpos(q, k)
            o = local_attention(q, k, v)
            o = o.transpose(0, 2, 1, 3).reshape(b, n, INNER)
            x = x + o @ wo
            h = shift_token(x)
            mu = h.mean(-1, keepdims=True)
            var = h.var(-1, keepdims=True)
            h = (h - mu) / jnp.sqrt(var + 1e-05) * lg + lb
            h = h @ w1 + b1
            a, g = jnp.split(h, 2, axis=-1)
            h = a * jax.nn.gelu(g, approximate=False)
            x = x + h @ w2 + b2
            return x
        key = jax.random.key(seed)
        ks = jax.random.split(key, 6)
        return {'x': jax.random.normal(ks[0], (B, N, DIM), jnp.float32), 'wqkv': jax.random.normal(ks[1], (DEPTH, DIM, 3 * INNER), jnp.float32) * 0.02, 'q_scale': jnp.ones((DEPTH, DIM_HEAD), jnp.float32), 'k_scale': jnp.ones((DEPTH, DIM_HEAD), jnp.float32), 'wo': jax.random.normal(ks[2], (DEPTH, INNER, DIM), jnp.float32) * 0.02, 'ln_g': jnp.ones((DEPTH, DIM), jnp.float32), 'ln_b': jnp.zeros((DEPTH, DIM), jnp.float32), 'w1': jax.random.normal(ks[3], (DEPTH, DIM, 2 * HID), jnp.float32) * 0.02, 'b1': jnp.zeros((DEPTH, 2 * HID), jnp.float32), 'w2': jax.random.normal(ks[4], (DEPTH, HID, DIM), jnp.float32) * 0.02, 'b2': jnp.zeros((DEPTH, DIM), jnp.float32)}
    _L0_ffn_in = _L0_ffn_setup()
    _d = {'L0_attn_x': _L0_attn_in['x'], 'L0_attn_Wq': _L0_attn_in['Wq'], 'L0_attn_Wk': _L0_attn_in['Wk'], 'L0_attn_Wv': _L0_attn_in['Wv'], 'L0_attn_Wi': _L0_attn_in['Wi'], 'L0_attn_bi': _L0_attn_in['bi'], 'L0_attn_Wf': _L0_attn_in['Wf'], 'L0_attn_bf': _L0_attn_in['bf'], 'L0_attn_Wo': _L0_attn_in['Wo'], 'L0_attn_bo': _L0_attn_in['bo'], 'L0_attn_W_out': _L0_attn_in['W_out'], 'L0_attn_ln_g': _L0_attn_in['ln_g'], 'L0_attn_ln_b': _L0_attn_in['ln_b'], 'L0_ffn_wqkv': _L0_ffn_in['wqkv'], 'L0_ffn_q_scale': _L0_ffn_in['q_scale'], 'L0_ffn_k_scale': _L0_ffn_in['k_scale'], 'L0_ffn_wo': _L0_ffn_in['wo'], 'L0_ffn_ln_g': _L0_ffn_in['ln_g'], 'L0_ffn_ln_b': _L0_ffn_in['ln_b'], 'L0_ffn_w1': _L0_ffn_in['w1'], 'L0_ffn_b1': _L0_ffn_in['b1'], 'L0_ffn_w2': _L0_ffn_in['w2'], 'L0_ffn_b2': _L0_ffn_in['b2']}
    _x0 = _d['L0_attn_x']
    _d['L0_attn_x'] = jax.random.normal(jax.random.fold_in(jax.random.key(seed), 1), (32, 256, 128), dtype=_x0.dtype)
    del _x0
    return _d

def reference(L0_attn_x, L0_attn_Wq, L0_attn_Wk, L0_attn_Wv, L0_attn_Wi, L0_attn_bi, L0_attn_Wf, L0_attn_bf, L0_attn_Wo, L0_attn_bo, L0_attn_W_out, L0_attn_ln_g, L0_attn_ln_b, L0_ffn_wqkv, L0_ffn_q_scale, L0_ffn_k_scale, L0_ffn_wo, L0_ffn_ln_g, L0_ffn_ln_b, L0_ffn_w1, L0_ffn_b1, L0_ffn_w2, L0_ffn_b2):

    def _L0_attn_ref(x, Wq, Wk, Wv, Wi, bi, Wf, bf, Wo, bo, W_out, ln_g, ln_b):
        import math
        import jax, jax.numpy as jnp
        import numpy as np
        B, T, IN, HID, H, D = (8, 256, 128, 128, 8, 64)
        HD = H * D

        def _mlstm_forward(x, Wq, Wk, Wv, Wi, bi, Wf, bf, Wo, bo, W_out, ln_g, ln_b):
            Bb, Tt, _ = x.shape
            q = (x @ Wq.T).reshape(Bb, Tt, H, D)
            k = (x @ Wk.T).reshape(Bb, Tt, H, D) / math.sqrt(D)
            v = (x @ Wv.T).reshape(Bb, Tt, H, D)
            i_g = jnp.exp(x @ Wi.T + bi)
            f_g = jnp.exp(x @ Wf.T + bf)
            o_g = jax.nn.sigmoid(x @ Wo.T + bo).reshape(Bb, Tt, H, D)

            def step(carry, inp):
                C, n = carry
                qt, kt, vt, it, ft, ot = inp
                C = ft[:, :, None, None] * C + it[:, :, None, None] * (vt[:, :, :, None] * kt[:, :, None, :])
                n = ft[:, :, None] * n + it[:, :, None] * kt
                h = jnp.einsum('bhde,bhe->bhd', C, qt)
                denom = jnp.maximum(jnp.abs(jnp.sum(n * qt, axis=-1)), 1.0)
                h = h / denom[:, :, None] * ot
                return ((C, n), h)
            xs = tuple((jnp.moveaxis(a, 1, 0) for a in (q, k, v, i_g, f_g, o_g)))
            C0 = jnp.zeros((Bb, H, D, D), x.dtype)
            n0 = jnp.zeros((Bb, H, D), x.dtype)
            (C, n), hs = jax.lax.scan(step, (C0, n0), xs)
            hs = jnp.moveaxis(hs, 0, 1).reshape(Bb, Tt, HD)
            mu = jnp.mean(hs, axis=-1, keepdims=True)
            var = jnp.var(hs, axis=-1, keepdims=True)
            hn = (hs - mu) * jax.lax.rsqrt(var + 1e-05) * ln_g + ln_b
            out = hn @ W_out.T
            return (out, C, n)

        def _reference_tuple_inner(x, Wq, Wk, Wv, Wi, bi, Wf, bf, Wo, bo, W_out, ln_g, ln_b):
            out, C, n = _mlstm_forward(x, Wq, Wk, Wv, Wi, bi, Wf, bf, Wo, bo, W_out, ln_g, ln_b)
            return (out, (C, n))
        return _reference_tuple_inner(x, Wq, Wk, Wv, Wi, bi, Wf, bf, Wo, bo, W_out, ln_g, ln_b)[0]

    def _L0_ffn_ref(x, wqkv, q_scale, k_scale, wo, ln_g, ln_b, w1, b1, w2, b2):
        import jax, jax.numpy as jnp
        import numpy as np
        DIM = 128
        DEPTH = 2
        HEADS = 8
        DIM_HEAD = 64
        WINDOW = 64
        INNER = HEADS * DIM_HEAD
        HID = int(DIM * 4 * 2 / 3)
        B, N = (2, 1024)
        QK_SCALE = 8.0

        def shift_token(t):
            t1, t2 = jnp.split(t, 2, axis=-1)
            t2 = jnp.pad(t2, ((0, 0), (1, 0), (0, 0)))[:, :-1]
            return jnp.concatenate([t1, t2], axis=-1)

        def l2norm(t):
            return t / jnp.clip(jnp.linalg.norm(t, axis=-1, keepdims=True), 1e-12)

        def rotate_half(x):
            x1, x2 = jnp.split(x, 2, axis=-1)
            return jnp.concatenate([-x2, x1], axis=-1)

        def rotary_xpos(q, k):
            n = q.shape[-2]
            half_idx = jnp.arange(0, DIM_HEAD, 2, dtype=jnp.float32)
            inv_freq = 1.0 / 10000.0 ** (half_idx / DIM_HEAD)
            t = jnp.arange(n, dtype=jnp.float32)
            freqs = t[:, None] * inv_freq[None, :]
            freqs = jnp.concatenate([freqs, freqs], axis=-1)
            base = (half_idx + 0.4 * DIM_HEAD) / (1.4 * DIM_HEAD)
            power = (t - n // 2) / float(WINDOW // 2)
            scale = base[None, :] ** power[:, None]
            scale = jnp.concatenate([scale, scale], axis=-1)
            cos, sin = (jnp.cos(freqs), jnp.sin(freqs))
            q = q * cos * scale + rotate_half(q) * sin * scale
            k = k * cos / scale + rotate_half(k) * sin / scale
            return (q, k)

        def local_attention(q, k, v):
            b, h, n, d = q.shape
            w = n // WINDOW
            bq = q.reshape(b, h, w, WINDOW, d) * QK_SCALE
            bk = k.reshape(b, h, w, WINDOW, d)
            bv = v.reshape(b, h, w, WINDOW, d)

            def look_around(t):
                p = jnp.pad(t, ((0, 0), (0, 0), (1, 0), (0, 0), (0, 0)))
                return jnp.concatenate([p[:, :, :w], p[:, :, 1:]], axis=3)
            bk, bv = (look_around(bk), look_around(bv))
            bt = jnp.arange(n).reshape(w, WINDOW)
            btp = jnp.pad(bt, ((1, 0), (0, 0)), constant_values=-1)
            btk = jnp.concatenate([btp[:w], btp[1:]], axis=1)
            sim = jnp.einsum('bhwid,bhwjd->bhwij', bq, bk)
            i = bt[:, :, None]
            j = btk[:, None, :]
            mask = (i < j) | (i > j + WINDOW) | (j == -1)
            sim = jnp.where(mask, -jnp.finfo(sim.dtype).max, sim)
            attn = jax.nn.softmax(sim, axis=-1)
            out = jnp.einsum('bhwij,bhwjd->bhwid', attn, bv)
            return out.reshape(b, h, n, d)

        def _layer(x, wqkv, qs, ksc, wo, lg, lb, w1, b1, w2, b2):
            b, n, _ = x.shape
            h = shift_token(x)
            qkv = h @ wqkv
            q, k, v = jnp.split(qkv, 3, axis=-1)
            to_heads = lambda t: t.reshape(b, n, HEADS, DIM_HEAD).transpose(0, 2, 1, 3)
            q, k, v = (to_heads(q), to_heads(k), to_heads(v))
            q = l2norm(q) * qs
            k = l2norm(k) * ksc
            q, k = rotary_xpos(q, k)
            o = local_attention(q, k, v)
            o = o.transpose(0, 2, 1, 3).reshape(b, n, INNER)
            x = x + o @ wo
            h = shift_token(x)
            mu = h.mean(-1, keepdims=True)
            var = h.var(-1, keepdims=True)
            h = (h - mu) / jnp.sqrt(var + 1e-05) * lg + lb
            h = h @ w1 + b1
            a, g = jnp.split(h, 2, axis=-1)
            h = a * jax.nn.gelu(g, approximate=False)
            x = x + h @ w2 + b2
            return x
        for l in range(DEPTH):
            x = _layer(x, wqkv[l], q_scale[l], k_scale[l], wo[l], ln_g[l], ln_b[l], w1[l], b1[l], w2[l], b2[l])
        return x
    x = L0_attn_x
    x = x + _layernorm(_L0_attn_ref(_layernorm(x, axis=-1), L0_attn_Wq, L0_attn_Wk, L0_attn_Wv, L0_attn_Wi, L0_attn_bi, L0_attn_Wf, L0_attn_bf, L0_attn_Wo, L0_attn_bo, L0_attn_W_out, L0_attn_ln_g, L0_attn_ln_b), axis=-1)
    x = x + _layernorm(_L0_ffn_ref(_layernorm(x, axis=-1), L0_ffn_wqkv, L0_ffn_q_scale, L0_ffn_k_scale, L0_ffn_wo, L0_ffn_ln_g, L0_ffn_ln_b, L0_ffn_w1, L0_ffn_b1, L0_ffn_w2, L0_ffn_b2), axis=-1)
    return x

_drawn_inputs = setup_inputs


def setup_inputs(seed=0):
    import zlib

    import numpy as np

    out = dict(_drawn_inputs(seed))
    spreads = {'L0_attn_bi': (0.0, 0.1),
     'L0_attn_bf': (0.0, 0.1),
     'L0_attn_bo': (0.0, 0.1),
     'L0_attn_ln_g': (1.0, 0.2),
     'L0_attn_ln_b': (0.0, 0.1),
     'L0_ffn_q_scale': (1.0, 0.6),
     'L0_ffn_k_scale': (1.0, 0.6),
     'L0_ffn_ln_g': (1.0, 0.6),
     'L0_ffn_ln_b': (0.0, 0.8),
     'L0_ffn_b1': (0.0, 0.8),
     'L0_ffn_b2': (0.0, 0.8)}
    factors = {'L0_attn_Wi': 2.715,
     'L0_ffn_wqkv': 3.988,
     'L0_ffn_wo': 3.961,
     'L0_ffn_w1': 7.543,
     'L0_ffn_w2': 7.408}
    for name, (base, spread) in spreads.items():
        noise = np.random.default_rng([zlib.crc32(name.encode()), seed]).standard_normal(out[name].shape)
        drawn = base * np.exp(spread * noise) if base else spread * noise
        out[name] = jnp.asarray(drawn.astype(out[name].dtype))
    for name, factor in factors.items():
        out[name] = (out[name] * factor).astype(out[name].dtype)
    return out
```

```python
import concourse.bass as bass
from concourse import mybir
from contextlib import ExitStack


F32 = mybir.dt.float32
BF16 = mybir.dt.bfloat16
ALU = mybir.AluOpType
ACT = mybir.ActivationFunctionType
AXX = mybir.AxisListType.X

P = 128
C = 128
SEQ = 256
NT = SEQ // P
H = 8
D = 64
HD = H * D
PAIRS = H // 2
WINDOW = 64
DEPTH = 2
HID = 341
HB = [(0, 128), (128, 128), (256, 85)]
DW = SEQ + P
KEYS = P + WINDOW
MASKED = -1.0e30
EPS = 1e-5
STREAMS = 2


class Count:

    def __init__(self, sem):
        self.sem, self.seen = sem, 0

    def next(self, n=1):
        self.seen += n
        return self.seen


def settle(engine, counts):
    for c in counts:
        if c.seen:
            engine.sem_inc(c.sem, -c.seen)


def block_kernel(nc, x, Wq, Wk, Wv, Wi, bi, Wf, bf, Wo, bo, W_out, lng, lnb,
                 wqkv, qsc, ksc, wo, lg, lb, w1, b1, w2, b2, rotary, out):
    ctx = ExitStack()
    with ctx:
        def sb(name, shape, dt=F32):
            return ctx.enter_context(nc.sbuf_tensor(name, shape, dt))

        def sem(name):
            return ctx.enter_context(nc.semaphore(name))

        ident = sb("ident", [P, P])
        ident_bf = sb("ident_bf", [P, P], BF16)
        band0 = sb("band0", [P, 2, P], BF16)
        band1 = sb("band1", [P, 2, KEYS], BF16)
        pick = sb("pick", [P, H, P], BF16)
        ones_bf = sb("ones_bf", [P, P], BF16)
        minus_half = sb("minus_half", [P, 4 * H])
        wqT = sb("wqT", [C, HD])
        wkT = sb("wkT", [C, HD])
        wvT = sb("wvT", [C, HD])
        woT = sb("woT", [C, HD])
        wiT = sb("wiT", [C, H])
        wfT = sb("wfT", [C, H])
        bi_c = sb("bi_c", [H, 1])
        bf_c = sb("bf_c", [H, 1])
        bo3 = sb("bo3", [P, HD], BF16)
        w_out = sb("w_out", [P, 4, C])
        out_bias = sb("out_bias", [P, C])
        wqkv_sb = sb("wqkv_sb", [C, DEPTH, 3 * HD])
        wo_sb = sb("wo_sb", [P, DEPTH, 4, C])
        w1_sb = sb("w1_sb", [C, DEPTH, 2 * HID])
        w2_sb = sb("w2_sb", [P, DEPTH, 3, C])
        b1_c = sb("b1_c", [P, DEPTH, 2, 3])
        b2_sb = sb("b2_sb", [P, DEPTH, C])
        rot = sb("rot", [P, DEPTH, NT, 2, 2, D])

        def per_stream(name, shape, dt=F32):
            return [sb(f"{name}{s}", shape, dt) for s in range(STREAMS)]

        x_in = per_stream("x_in", [P, NT, C])
        mid = per_stream("mid", [P, NT, C])
        xb = per_stream("xb", [P, NT, C])
        x1 = per_stream("x1", [P, NT, C])
        x1b = per_stream("x1b", [P, NT, C])
        xs = per_stream("xs", [P, NT, C])
        nrm = per_stream("nrm", [P, NT, C])
        y = x1b
        stats = per_stream("stats", [P, NT, 6])
        mv = per_stream("mv", [P, NT, 2])
        veps = per_stream("veps", [P, NT])
        rstd = per_stream("rstd", [P, NT])
        nT = per_stream("nT", [C, SEQ])
        sT = per_stream("sT", [C, SEQ])
        lin = per_stream("lin", [P, PAIRS, SEQ])
        bd = per_stream("bd", [P, PAIRS, 2, SEQ])
        v = per_stream("v", [P, NT, H, D + 1])
        prob = per_stream("prob", [P, H, P + SEQ])
        shared = per_stream("shared", [P, H * DW])
        work = per_stream("work", [P, H * DW])
        th = per_stream("th", [P, NT, HD])
        hs = per_stream("hs", [P, NT, HD])
        hT = per_stream("hT", [P, 4, SEQ])
        cum = [hs[s][0:H, 0, 0:SEQ] for s in range(STREAMS)]
        gi = [hs[s][0:H, 0, SEQ:2 * SEQ] for s in range(STREAMS)]
        rest = [hs[s][0:H, 1, 0:SEQ] for s in range(STREAMS)]
        mid_bf = per_stream("mid_bf", [H, SEQ], BF16)
        cum3 = per_stream("cum3", [P, SEQ], BF16)
        src_bias = per_stream("src_bias", [P, NT, H])
        rden = per_stream("rden", [P, NT, H])
        ss = per_stream("ss", [P, NT, 2, H])
        rs = per_stream("rs", [P, NT, 2, H])
        nbias = per_stream("nbias", [P, NT, H])
        smax = per_stream("smax", [P, NT, H])
        rsum = per_stream("rsum", [P, NT, H])
        rinv = per_stream("rinv", [P, NT, H])
        prod = [sb(f"prod{j}", [P, 2, H, D]) for j in range(2)]

        sqr = [hs[t][:, :, :].rearrange("p w (h d) -> p w h d", h=H) for t in range(NT)]

        def dec_v(s):
            return work[s][:, :].rearrange("p (h t) -> p h t", h=H)

        def wgt_v(s):
            return shared[s][:, :].rearrange("p (h t) -> p h t", h=H)

        def pt_v(s):
            return shared[s][:, :].rearrange("p (b h t) -> p b h t", b=3, h=H)

        def hid_v(s):
            return shared[s][:, 0:3 * SEQ].rearrange("p (b t) -> p b t", b=3)

        def gelu_v(s):
            return shared[s][:, 3 * SEQ:6 * SEQ].rearrange("p (b t) -> p b t", b=3)

        def rot_v(s):
            return work[s][:, 0:4 * HD].rearrange("p (t w h d) -> p t w h d", t=NT, w=2, h=H)

        class Ring:
            def __init__(self, name):
                self.banks = [ctx.enter_context(nc.psum_tensor(f"{name}{j}", [P, 512], F32)) for j in range(2)]
                self.to_act = Count(sem(f"{name}_ready_for_scalar"))
                self.to_dve = Count(sem(f"{name}_ready_for_vector"))
                self.evacuated = [sem(f"{name}{j}_evacuated") for j in range(2)]
                self.uses = [0, 0]
                self.act_banks, self.dve_banks = [], []

        proj, score, turn, acc = Ring("proj"), Ring("score"), Ring("turn"), Ring("acc")
        RINGS = (proj, score, turn, acc)

        load_s = sem("weights_loaded")
        set_d = sem("setup_vector_done")
        set_a = sem("setup_scalar_done")
        set_p = sem("setup_tensor_done")
        set_g = sem("setup_gpsimd_done")

        x_loaded = [Count(sem(f"x_loaded{s}")) for s in range(STREAMS)]
        x_free = [Count(sem(f"x_free{s}")) for s in range(STREAMS)]
        y_ready = [Count(sem(f"y_ready{s}")) for s in range(STREAMS)]
        y_stored = [Count(sem(f"y_stored{s}")) for s in range(STREAMS)]
        y_free = [Count(sem(f"y_free{s}")) for s in range(STREAMS)]
        x1_ready = [Count(sem(f"x1_ready{s}")) for s in range(STREAMS)]
        x1_pool = Count(sem("x1_ready_for_gpsimd"))
        shifted = [Count(sem(f"x1_shifted{s}")) for s in range(STREAMS)]
        half_kept = Count(sem("first_half_copied"))
        x1b_ready = Count(sem("x1_with_bias_ready"))
        stats_ready = Count(sem("stats_ready"))
        rstd_ready = Count(sem("rstd_ready"))
        nrm_ready = Count(sem("normalised_ready"))
        hn_ready = Count(sem("head_outputs_ready"))
        res_ready = Count(sem("residual_ready"))
        cum_ready = Count(sem("split_cumulative_ready"))
        cum_act = Count(sem("cumulative_middle_ready"))
        mid_moved = Count(sem("cumulative_middle_moved"))
        bias_ready = Count(sem("source_bias_ready"))
        dec_ready = Count(sem("decays_ready"))
        dec_masked = Count(sem("decays_masked"))
        sq_ready = Count(sem("squares_ready"))
        sq_free = [Count(sem(f"squares{t}_reduced")) for t in range(NT)]
        ss_ready = Count(sem("sums_of_squares_ready"))
        prod_ready = Count(sem("rotary_products_ready"))
        prod_free = [Count(sem(f"prod{j}_free")) for j in range(2)]
        rot_ready = Count(sem("rotated_ready"))
        max_ready = Count(sem("score_max_ready"))
        gelu_ready = Count(sem("gelu_ready"))
        v_step = Count(sem("vector_step"))
        a_step = Count(sem("scalar_step"))
        g_step = Count(sem("gpsimd_step"))

        def rows(ap, n=P):
            return ap.rearrange("(b p) c -> p b c", p=n)

        n_q, n_k = hs[0][:, 0, :], hs[0][:, 1, :]
        n_v, n_o = hs[1][:, 0, :], hs[1][:, 1, :]
        n_w = th[0][:, 0, :]
        n_i, n_f = nrm[0][0:H, 0, :], nrm[0][0:H, 1, :]
        lng_c = nrm[1][:, 0, 0:4]
        lnb_c = nrm[1][:, 0, 4:8]
        lb_c = nrm[1][:, 0, 8:8 + DEPTH]
        lg_c = nrm[1][:, 0, 16:16 + DEPTH]
        b1_n = nrm[1][:, 1, 0:6 * DEPTH].rearrange("p (l w b) -> p l w b", l=DEPTH, w=2)
        w1_n = prob[0][:, :, :].rearrange("p h t -> p (h t)")[:, 0:2 * 2 * HID].rearrange("p (l n) -> p l n", l=DEPTH)
        lnb_w = x_in[0][:, :, :].rearrange("p t c -> p (t c)")
        lnb_w2 = x_in[1][:, :, :].rearrange("p t c -> p (t c)")
        w_raw = shared[0][:, 0:4 * C].rearrange("p (b c) -> p b c", b=4)
        scales = shared[1][:, 0:DEPTH * 2 * D].rearrange("p (l w d) -> p l w d", l=DEPTH, w=2)
        tables = shared[1][:, 512:512 + NT * 4 * D].rearrange("p (t n) -> p t n", t=NT)
        bo_n = work[0][0:1, 0:HD]
        bo_r = work[0][0:1, HD:2 * HD]
        loads, setup_g = [0], [0]

        with nc.Block() as block:
            @block.sync
            def _(sp):
                def load(dst, src):
                    with nc.allow_non_contiguous_dma(reason="a few hundred words of biases, once"):
                        sp.dma_start(dst, src).then_inc(load_s, 16)
                    loads[0] += 16

                for dst, src in ((n_q, Wq), (n_k, Wk), (n_v, Wv), (n_o, Wo)):
                    load(dst.rearrange("p (b c) -> p b c", b=4), rows(src))
                load(n_w, W_out)
                load(n_i, Wi)
                load(n_f, Wf)
                load(bi_c[:, :], bi.rearrange("(p o) -> p o", o=1))
                load(bf_c[:, :], bf.rearrange("(p o) -> p o", o=1))
                load(bo_n, bo.rearrange("(o n) -> o n", o=1))
                load(lng_c, lng.rearrange("(b p) -> p b", p=P))
                load(lnb_c, lnb.rearrange("(b p) -> p b", p=P))
                load(lb_c, lb.rearrange("l p -> p l"))
                load(lg_c, lg.rearrange("l p -> p l"))
                load(tables, rotary.rearrange("(t p) n -> p t n", p=P))
                for l in range(DEPTH):
                    load(wqkv_sb[:, l, :], wqkv[l, :, :])
                    load(wo_sb[:, l, :, :], rows(wo[l, :, :]))
                    load(w1_n[:, l, :], w1[l, :, :])
                    for b, (at, n) in enumerate(HB):
                        load(w2_sb[0:n, l, b, :], w2[l, at:at + n, :])
                        for w in range(2):
                            a = w * HID + at
                            load(b1_n[0:n, l, w, b:b + 1], b1[l, a:a + n].rearrange("(p o) -> p o", o=1))
                    load(b2_sb[:, l, :], b2[l, :].partition_broadcast(P))
                    load(scales[:, l, 0, :], qsc[l, :].partition_broadcast(P))
                    load(scales[:, l, 1, :], ksc[l, :].partition_broadcast(P))

            @block.gpsimd
            def _(pool):
                g = nc.gpsimd
                n = [0]

                def link(ins):
                    n[0] += 1
                    ins.then_inc(set_g, 1)
                    pool.wait_ge(set_g, n[0])

                link(g.memset(ident[:, :], 0.0))
                link(g.affine_select(out=ident[:, :], in_=ident[:, :], compare_op=ALU.not_equal, fill=1.0,
                                     base=0, pattern=[[-1, P]], channel_multiplier=1))
                link(g.tensor_copy(ident_bf[:, :], ident[:, :]))
                link(g.memset(band0[:, :, :], 0.0))
                link(g.memset(band1[:, :, :], 0.0))
                link(g.affine_select(out=band0[:, :, :], in_=band0[:, :, :], compare_op=ALU.is_ge, fill=MASKED,
                                     base=0, pattern=[[0, 2], [-1, P]], channel_multiplier=1))
                link(g.affine_select(out=band0[:, :, :], in_=band0[:, :, :], compare_op=ALU.is_ge, fill=MASKED,
                                     base=WINDOW, pattern=[[0, 2], [1, P]], channel_multiplier=-1))
                link(g.affine_select(out=band1[:, :, :], in_=band1[:, :, :], compare_op=ALU.is_ge, fill=MASKED,
                                     base=P - WINDOW, pattern=[[0, 2], [-1, KEYS]], channel_multiplier=1))
                link(g.affine_select(out=band1[:, :, :], in_=band1[:, :, :], compare_op=ALU.is_ge, fill=MASKED,
                                     base=0, pattern=[[0, 2], [1, KEYS]], channel_multiplier=-1))
                link(g.memset(pick[:, :, :], 0.0))
                for part in range(3):
                    link(g.affine_select(out=pick[:, :, :], in_=pick[:, :, :], compare_op=ALU.not_equal, fill=1.0,
                                         base=-32 * part, pattern=[[-1, H], [0, P]], channel_multiplier=1))
                link(g.memset(ones_bf[:, :], 1.0))
                link(g.memset(minus_half[:, :], -0.5))
                link(g.memset(bo3[:, :], 0.0))
                for s in range(STREAMS):
                    link(g.memset(bd[s][:, :, :, :], 0.0))
                    link(g.memset(sT[s][:, 0:1], 0.0))
                    link(g.memset(cum3[s][:, :], 0.0))
                    link(g.memset(v[s][:, :, :, D:D + 1], 1.0))
                    link(g.memset(xs[s][:, :, :], 0.0))
                    if s:
                        link(g.memset(prob[s][:, :, P:P + WINDOW], 0.0))
                setup_g[0] = n[0]


            @block.tensor
            def _(pe):
                pe.wait_ge(load_s, loads[0])
                pe.wait_ge(set_g, setup_g[0])
                bank = [proj.banks[0], proj.banks[1], score.banks[0], score.banks[1], turn.banks[0]]
                for j, src in enumerate((n_q, n_k, n_v, n_o, n_w)):
                    for b in range(4):
                        last = nc.tensor.transpose(bank[j][:, b * P:(b + 1) * P], src[:, b * P:(b + 1) * P], ident[:, :])
                nc.tensor.transpose(turn.banks[1][:, 0:H], n_i, ident[0:H, 0:H])
                last = nc.tensor.transpose(turn.banks[1][:, H:2 * H], n_f, ident[0:H, 0:H])
                last.then_inc(set_p, 1)
                pe.wait_ge(set_d, 8)
                for b in range(4):
                    half = (lnb_w if b < 2 else lnb_w2)[:, (b % 2) * P:(b % 2 + 1) * P]
                    nc.tensor.matmul(acc.banks[0][:, 0:C], half, w_raw[:, b, :], start=(b == 0), stop=(b == 3))
                for l in range(DEPTH):
                    for w in range(2):
                        for b, (at, m) in enumerate(HB):
                            a = w * HID + at
                            last = nc.tensor.matmul(acc.banks[1][0:m, (l * 2 + w) * 3 + b:(l * 2 + w) * 3 + b + 1],
                                                    w1_n[:, l, a:a + m], lb_c[:, l:l + 1], start=True, stop=True)
                last.then_inc(set_p, 1)

            @block.scalar
            def _(act):
                act.wait_ge(set_p, 1)
                for dst, src in ((wqT, proj.banks[0]), (wkT, proj.banks[1]), (wvT, score.banks[0]), (woT, score.banks[1])):
                    nc.scalar.activation(dst[:, :], src[:, :], ACT.Copy).then_inc(set_a, 1)

            @block.vector
            def _(dve):
                V = nc.vector
                n = [0]

                def link(ins):
                    n[0] += 1
                    ins.then_inc(set_d, 1)
                    dve.wait_ge(set_d, n[0])

                dve.wait_ge(set_p, 1)
                link(V.tensor_copy(wiT[:, :], turn.banks[1][:, 0:H]))
                link(V.tensor_copy(wfT[:, :], turn.banks[1][:, H:2 * H]))
                link(V.tensor_copy(w_raw, turn.banks[0][:, :].rearrange("p (b c) -> p b c", b=4)))
                link(V.tensor_tensor(w_out[:, :, :], w_raw, lng_c.unsqueeze(2).broadcast_to([P, 4, C]), ALU.mult))
                for b in range(4):
                    half = (lnb_w if b < 2 else lnb_w2)[:, (b % 2) * P:(b % 2 + 1) * P]
                    link(V.tensor_copy(half, lnb_c[:, b:b + 1].broadcast_to([P, P])))
                for l in range(DEPTH):
                    link(V.tensor_scalar(w1_sb[:, l, :], w1_n[:, l, :], lg_c[:, l:l + 1], None, ALU.mult))
                for l in range(DEPTH):
                    for t in range(NT):
                        tab = tables[:, t, :].rearrange("p (w u d) -> p w u d", w=2, u=2)
                        sc = scales[:, l, :, :].unsqueeze(2).broadcast_to([P, 2, 2, D])
                        link(V.tensor_tensor(rot[:, l, t, :, :, :], tab, sc, ALU.mult))
                link(V.tensor_copy(bo3[0:1, :], bo_n))
                link(V.tensor_tensor(bo_r, bo_n, bo3[0:1, :], ALU.subtract))
                link(V.tensor_copy(bo3[32:33, :], bo_r))
                link(V.tensor_copy(mid_bf[0][0:1, :], bo_r[:, 0:SEQ]))
                link(V.tensor_copy(mid_bf[1][0:1, :], bo_r[:, SEQ:HD]))
                link(V.tensor_tensor(bo3[64:65, 0:SEQ], bo_r[:, 0:SEQ], mid_bf[0][0:1, :], ALU.subtract))
                link(V.tensor_tensor(bo3[64:65, SEQ:HD], bo_r[:, SEQ:HD], mid_bf[1][0:1, :], ALU.subtract))
                dve.wait_ge(set_p, 2)
                link(V.tensor_copy(out_bias[:, :], acc.banks[0][:, 0:C]))
                for l in range(DEPTH):
                    for b, (at, m) in enumerate(HB):
                        col = acc.banks[1][0:m, l * 6 + b:l * 6 + b + 4:3]
                        link(V.tensor_tensor(b1_c[0:m, l, :, b], b1_n[0:m, l, :, b], col, ALU.add))
                link(V.memset(prob[0][:, :, P:P + WINDOW], 0.0))

        TURNS = x.shape[0] // STREAMS
        xv = x.rearrange("b (t p) c -> b p t c", p=P)
        ov = out.rearrange("b (t p) c -> b p t c", p=P)

        with nc.Block() as block:
            @block.tensor
            def _(pe):
                T = nc.tensor
                at = {r: 0 for r in RINGS}

                class Use:

                    def __init__(self, ring, j):
                        self.tile, self.sem, self.value = ring.banks[j], ring.evacuated[j], ring.uses[j] + 1

                def claim(ring, to_act=False, to_dve=False):
                    j = at[ring] % 2
                    at[ring] += 1
                    pe.wait_ge(ring.evacuated[j], ring.uses[j] + 1)
                    ring.uses[j] += 1
                    if to_act:
                        ring.act_banks.append(j)
                    if to_dve:
                        ring.dve_banks.append(j)
                    return Use(ring, j)

                def wait_evacuated(uses):
                    for u in {u.sem.name: u for u in sorted(uses, key=lambda u: u.value)}.values():
                        pe.wait_ge(u.sem, u.value)

                made = [dict() for _ in range(STREAMS)]

                def turn_tile(s, src, ready, n, name):
                    use = claim(turn, to_act=True)
                    b = use.tile
                    if ready is None:
                        wait_evacuated(made[s]["residual"])
                    else:
                        pe.wait_ge(ready.sem, ready.next(n))
                    made[s][name] = [use]
                    for t in range(NT):
                        last = T.transpose(b[:, t * P:(t + 1) * P], src[:, t, :], ident[:, :])
                    last.then_inc(turn.to_act.sem, 1)

                def gate_products(s):
                    use = claim(turn, to_dve=True)
                    b = use.tile
                    wait_evacuated(made[s]["nT"])
                    made[s]["gates"] = [use]
                    T.matmul(b[0:H, 0:SEQ], wiT[:, :], nT[s][:, :], start=True, stop=True)
                    T.matmul(b[0:H, SEQ:2 * SEQ], wfT[:, :], nT[s][:, :], start=True, stop=True)\
                     .then_inc(turn.to_dve.sem, 1)

                def gates_turned(s):
                    use = claim(turn, to_dve=True)
                    b = use.tile
                    wait_evacuated(made[s]["gates"])
                    for t in range(NT):
                        last = T.transpose(b[:, t * H:(t + 1) * H], gi[s][:, t * P:(t + 1) * P], ident[0:H, 0:H])
                    last.then_inc(turn.to_dve.sem, 1)

                def mlstm_projections(s):
                    made[s]["heads"], made[s]["v"] = [], []
                    for w, is_q in ((wqT, True), (wkT, False)):
                        for g2 in range(2):
                            use = claim(proj, to_act=is_q, to_dve=not is_q)
                            b = use.tile
                            made[s]["heads"].append(use)
                            for e in range(2):
                                p2 = 2 * g2 + e
                                last = T.matmul(b[:, e * SEQ:(e + 1) * SEQ], w[:, p2 * P:(p2 + 1) * P], nT[s][:, :],
                                                start=True, stop=True)
                            last.then_inc((proj.to_act if is_q else proj.to_dve).sem, 1)
                    for w in (wvT, woT):
                        for t in range(NT):
                            use = claim(proj, to_act=True)
                            b = use.tile
                            made[s]["v"].append(use)
                            gate = w is woT
                            last = T.matmul(b[:, :], nT[s][:, t * P:(t + 1) * P], w[:, :], start=True, stop=not gate)
                            if gate:
                                last = T.matmul(b[:, :], ones_bf[:, :], bo3[:, :], start=False, stop=True)
                            last.then_inc(proj.to_act.sem, 1)

                def spread_gates(s):
                    pe.wait_ge(cum_ready.sem, cum_ready.next())
                    pe.wait_ge(mid_moved.sem, mid_moved.next())
                    for p2 in range(PAIRS):
                        use = claim(proj, to_act=True)
                        b = use.tile
                        for e in range(2):
                            last = T.matmul(b[:, e * SEQ:(e + 1) * SEQ], pick[:, 2 * p2 + e, :], cum3[s][:, :],
                                            start=True, stop=True)
                        last.then_inc(proj.to_act.sem, 1)

                def mlstm_scores(s):
                    wait_evacuated(made[s]["heads"])
                    made[s]["weights"] = []
                    for p2 in range(PAIRS):
                        use = claim(score, to_dve=True)
                        b = use.tile
                        made[s]["weights"].append(use)
                        T.matmul(b[:, :].rearrange("p (e t) -> p e t", e=2), lin[s][:, p2, 0:P], bd[s][:, p2, :, :],
                                 start=True, stop=True).then_inc(score.to_dve.sem, 1)
                    for g2 in range(2):
                        use = claim(score, to_dve=True)
                        b = use.tile
                        made[s]["weights"].append(use)
                        for e in range(2):
                            p2 = 2 * g2 + e
                            last = T.matmul(b[:, e * SEQ:(e + 1) * SEQ].rearrange("p (e t) -> p e t", e=2),
                                            lin[s][:, p2, P:SEQ], bd[s][:, p2, :, P:SEQ], start=True, stop=True)
                        last.then_inc(score.to_dve.sem, 1)

                def mlstm_values(s):
                    wgt = wgt_v(s)
                    wait_evacuated(made[s]["v"])
                    wait_evacuated(made[s]["weights"][:PAIRS])
                    for t in range(NT):
                        for g2 in range(2):
                            use = claim(acc, to_dve=True)
                            b = use.tile
                            if t == 1:
                                wait_evacuated(made[s]["weights"][PAIRS + g2:PAIRS + g2 + 1])
                            for j in range(4):
                                h = 4 * g2 + j
                                o = b[:, j * (D + 1):(j + 1) * (D + 1)]
                                last = T.matmul(o, wgt[:, h, t * P:(t + 1) * P], v[s][:, 0, h, :], start=True, stop=t == 0)
                                if t == 1:
                                    last = T.matmul(o, wgt[:, h, SEQ:DW], v[s][:, 1, h, :], start=False, stop=True)
                            last.then_inc(acc.to_dve.sem, 1)

                def features_T(s, src, ready):
                    made[s]["hT"] = []
                    for t in range(NT):
                        use = claim(turn, to_act=True)
                        b = use.tile
                        made[s]["hT"].append(use)
                        if ready is None:
                            wait_evacuated(made[s]["outputs"][t:t + 1])
                        else:
                            pe.wait_ge(ready.sem, ready.next())
                        for k in range(4):
                            last = T.transpose(b[:, k * P:(k + 1) * P], src[:, t, k * P:(k + 1) * P], ident[:, :])
                        last.then_inc(turn.to_act.sem, 1)

                def from_heads(s, w):
                    use = claim(acc, to_dve=True)
                    b = use.tile
                    for t in range(NT):
                        wait_evacuated(made[s]["hT"][t:t + 1])
                        for k in range(4):
                            last = T.matmul(b[:, t * C:(t + 1) * C], hT[s][:, k, t * P:(t + 1) * P], w[:, k, :],
                                            start=(k == 0), stop=(k == 3))
                    last.then_inc(acc.to_dve.sem, 1)

                def attention_projections(l, s):
                    wait_evacuated(made[s]["sT"])
                    made[s]["v"] = []
                    for t in range(NT):
                        for w in range(3):
                            use = claim(proj, to_act=True, to_dve=w < 2)
                            b = use.tile
                            if w == 2:
                                made[s]["v"].append(use)
                            T.matmul(b[:, :], sT[s][:, t * P:(t + 1) * P], wqkv_sb[:, l, w * HD:(w + 1) * HD],
                                     start=True, stop=True).then_inc(proj.to_act.sem, 1)

                def rotated_T(s):
                    r = rot_v(s)
                    made[s]["heads"] = []
                    for t in range(NT):
                        pe.wait_ge(rot_ready.sem, rot_ready.next())
                        for w in range(2):
                            use = claim(turn, to_act=w == 0, to_dve=w == 1)
                            b = use.tile
                            made[s]["heads"].append(use)
                            flat = r[:, t, w, :, :].rearrange("p h d -> p (h d)")
                            for k in range(4):
                                last = T.transpose(b[:, k * P:(k + 1) * P], flat[:, k * P:(k + 1) * P], ident[:, :])
                            last.then_inc((turn.to_act if w == 0 else turn.to_dve).sem, 1)

                def attention_scores(s):
                    wait_evacuated(made[s]["heads"])
                    made[s]["prob"] = []
                    for g2 in range(2):
                        use = claim(score, to_act=True, to_dve=True)
                        b = use.tile
                        made[s]["prob"].append(use)
                        for e in range(2):
                            p2 = 2 * g2 + e
                            o = b[:, e * SEQ:(e + 1) * SEQ].rearrange("p (e t) -> p e t", e=2)
                            T.matmul(o, lin[s][:, p2, 0:P], bd[s][:, p2, :, 0:P], start=True, stop=False)
                            last = T.matmul(o, ident_bf[:, :], band0[:, :, :], start=False, stop=True)
                        last.then_inc(score.to_dve.sem, 1)
                    for p2 in range(PAIRS):
                        use = claim(score, to_act=True, to_dve=True)
                        b = use.tile
                        made[s]["prob"].append(use)
                        o = b[:, 0:2 * KEYS].rearrange("p (e t) -> p e t", e=2)
                        T.matmul(o, lin[s][:, p2, P:SEQ], bd[s][:, p2, :, WINDOW:SEQ], start=True, stop=False)
                        T.matmul(o, ident_bf[:, :], band1[:, :, :], start=False, stop=True).then_inc(score.to_dve.sem, 1)

                def probs_turned(s):
                    made[s]["pt"] = []
                    for k in range(6):
                        blk, h0 = k // 2, 4 * (k % 2)
                        if blk == 0:
                            wait_evacuated(made[s]["prob"][k:k + 1])
                        if blk == 1:
                            wait_evacuated(made[s]["prob"][2 + h0 // 2:4 + h0 // 2])
                        use = claim(turn, to_act=k % 2 == 0, to_dve=k % 2 == 1)
                        b = use.tile
                        made[s]["pt"].append(use)
                        for j in range(4):
                            last = T.transpose(b[:, j * P:(j + 1) * P], prob[s][:, h0 + j, blk * P:(blk + 1) * P], ident[:, :])
                        last.then_inc((turn.to_act if k % 2 == 0 else turn.to_dve).sem, 1)

                def attention_values(s):
                    pt = pt_v(s)
                    wait_evacuated(made[s]["v"])
                    made[s]["outputs"] = []
                    for t in range(NT):
                        use = claim(acc, to_dve=True)
                        b = use.tile
                        made[s]["outputs"].append(use)
                        wait_evacuated(made[s]["pt"][0:2] if t == 0 else made[s]["pt"][2:6])
                        for h in range(H):
                            o = b[:, h * D:(h + 1) * D]
                            last = T.matmul(o, pt[:, t, h, :], v[s][:, 0, h, 0:D], start=True, stop=t == 0)
                            if t == 1:
                                last = T.matmul(o, pt[:, 2, h, :], v[s][:, 1, h, 0:D], start=False, stop=True)
                        last.then_inc(acc.to_dve.sem, 1)

                def mlp_up(l, s):
                    wait_evacuated(made[s]["nT"])
                    made[s]["hidden"] = []
                    for k, (a, m) in enumerate(HB):
                        use = claim(proj, to_act=True, to_dve=True)
                        b = use.tile
                        made[s]["hidden"].append(use)
                        T.matmul(b[0:m, 0:SEQ], w1_sb[:, l, HID + a:HID + a + m], nT[s][:, :], start=True, stop=True)
                        T.matmul(b[0:m, SEQ:2 * SEQ], w1_sb[:, l, a:a + m], nT[s][:, :], start=True, stop=True)\
                         .then_inc(proj.to_act.sem, 1)

                def mlp_down(l, s):
                    hd = hid_v(s)
                    use = claim(acc, to_dve=True)
                    b = use.tile
                    made[s]["residual"] = [use]
                    wait_evacuated(made[s]["hidden"])
                    for t in range(NT):
                        for k, (a, m) in enumerate(HB):
                            last = T.matmul(b[:, t * C:(t + 1) * C], hd[0:m, k, t * P:(t + 1) * P], w2_sb[0:m, l, k, :],
                                            start=(k == 0), stop=(k == 2))
                    last.then_inc(acc.to_dve.sem, 1)

                for r in RINGS:
                    for c in r.evacuated:
                        pe.sem_inc(c, 1)
                with pe.Fori(0, TURNS) as i:
                    for s in range(STREAMS):
                        turn_tile(s, nrm[s], nrm_ready, NT, "nT")
                    for s in range(STREAMS):
                        gate_products(s)
                    for s in range(STREAMS):
                        gates_turned(s)
                    for s in range(STREAMS):
                        mlstm_projections(s)
                        spread_gates(s)
                        mlstm_scores(s)
                        mlstm_values(s)
                    for s in range(STREAMS):
                        features_T(s, hs[s], hn_ready)
                    for s in range(STREAMS):
                        from_heads(s, w_out)
                    for l in range(DEPTH):
                        for s in range(STREAMS):
                            turn_tile(s, xb[s], res_ready if l == 0 else None, NT, "sT")
                        for s in range(STREAMS):
                            attention_projections(l, s)
                        for s in range(STREAMS):
                            rotated_T(s)
                        for s in range(STREAMS):
                            attention_scores(s)
                        for s in range(STREAMS):
                            probs_turned(s)
                        for s in range(STREAMS):
                            attention_values(s)
                        for s in range(STREAMS):
                            features_T(s, th[s], None)
                        for s in range(STREAMS):
                            from_heads(s, wo_sb[:, l, :, :])
                        for s in range(STREAMS):
                            turn_tile(s, nrm[s], nrm_ready, NT, "nT")
                        for s in range(STREAMS):
                            mlp_up(l, s)
                        for s in range(STREAMS):
                            mlp_down(l, s)
                    settle(pe, [nrm_ready, hn_ready, cum_ready, mid_moved, rot_ready, res_ready])
                    for r in RINGS:
                        for c, n in zip(r.evacuated, r.uses):
                            pe.sem_inc(c, -n)
                        assert r.uses[0] == r.uses[1]

            @block.sync
            def _(sp):
                def load_x(turn_no, s):
                    sp.dma_start(x_in[s][:, :, :], xv[bass.ds(turn_no * STREAMS + s, 1), :, :, :]
                                 .rearrange("o p t c -> p (o t) c")).then_inc(x_loaded[s].sem, 16)

                def shift(s):
                    sp.wait_ge(x1_ready[s].sem, x1_ready[s].next())
                    sp.dma_start(xs[s][1:P, :, D:C], x1[s][0:P - 1, :, D:C]).then_inc(shifted[s].sem, 16)
                    sp.dma_start(xs[s][0:1, 1, D:C], x1[s][P - 1:P, 0, D:C]).then_inc(shifted[s].sem, 16)

                def turn_of(i, more):
                    if more:
                        for s in range(STREAMS):
                            sp.wait_ge(x_free[s].sem, x_free[s].next())
                            load_x(i + 1, s)
                    for l in range(DEPTH):
                        for s in range(STREAMS):
                            shift(s)
                    for s in range(STREAMS):
                        sp.wait_ge(y_ready[s].sem, y_ready[s].next())
                        sp.dma_start(ov[bass.ds(i * STREAMS + s, 1), :, :, :].rearrange("o p t c -> p (o t) c"),
                                     y[s][:, :, :]).then_inc(y_stored[s].sem, 16)
                    for s in range(STREAMS):
                        sp.wait_ge(y_stored[s].sem, y_stored[s].next(16))
                        sp.sem_inc(y_free[s].sem, 1)
                    settle(sp, [*x_free, *x1_ready, *y_ready, *y_stored])
                    for c in (*x_free, *x1_ready, *y_ready, *y_stored):
                        c.seen = 0

                for s in range(STREAMS):
                    load_x(0, s)
                    sp.sem_inc(y_free[s].sem, 1)
                with sp.Fori(0, TURNS - 1) as i:
                    turn_of(i, True)
                turn_of(TURNS - 1, False)

            @block.gpsimd
            def _(pool):
                g = nc.gpsimd

                def link(ins):
                    ins.then_inc(g_step.sem, 1)
                    pool.wait_ge(g_step.sem, g_step.next())

                def inverse_std(s):
                    pool.wait_ge(stats_ready.sem, stats_ready.next())
                    link(g.tensor_scalar(veps[s][:, :], mv[s][:, :, 1], EPS, None, ALU.add))
                    g.tensor_tensor(rstd[s][:, :], veps[s][:, :], minus_half[:, 0:NT], ALU.pow).then_inc(rstd_ready.sem, 1)

                def mask_decays(s):
                    dec = dec_v(s)
                    pool.wait_ge(dec_ready.sem, dec_ready.next())
                    for t in range(NT):
                        part = dec[:, :, 0:P] if t == 0 else dec[:, :, SEQ:SEQ + P]
                        g.affine_select(out=part, in_=part, compare_op=ALU.is_ge, fill=0.0, base=0,
                                        pattern=[[0, H], [1, P]], channel_multiplier=-1).then_inc(dec_masked.sem, 1)

                def rotate(s, t):
                    r = rot_v(s)
                    for w in range(2):
                        pool.wait_ge(prod_ready.sem, prod_ready.next())
                        pr = prod[w]
                        for half in range(2):
                            a, b = half * 32, 32 - half * 32
                            g.tensor_tensor(r[:, t, w, :, a:a + 32], pr[:, 0, :, a:a + 32], pr[:, 1, :, b:b + 32],
                                            ALU.add).then_inc(g_step.sem, 1)
                            g_step.next()
                        pool.wait_ge(g_step.sem, g_step.seen)
                        pool.sem_inc(prod_free[w].sem, 1)

                def inverse_norms(s, t):
                    pool.wait_ge(ss_ready.sem, ss_ready.next())
                    link(g.tensor_tensor(rs[s][:, t, :, :].rearrange("p w h -> p (w h)"),
                                         ss[s][:, t, :, :].rearrange("p w h -> p (w h)"),
                                         minus_half[:, 0:2 * H], ALU.pow))

                def scale_k(s, t):
                    r = rot_v(s)
                    g.tensor_tensor(r[:, t, 1, :, :], r[:, t, 1, :, :],
                                    rs[s][:, t, 1, :].unsqueeze(2).broadcast_to([P, H, D]), ALU.mult)\
                     .then_inc(rot_ready.sem, 1)

                def mlp_inputs(l, s):
                    pool.wait_ge(x1_pool.sem, x1_pool.next())
                    g.tensor_copy(xs[s][:, :, 0:D], x1[s][:, :, 0:D]).then_inc(half_kept.sem, 1)
                    if l == 0:
                        pool.wait_ge(y_free[s].sem, y_free[s].next())
                    g.tensor_tensor(x1b[s][:, :, :], x1[s][:, :, :],
                                    b2_sb[:, l, :].unsqueeze(1).broadcast_to([P, NT, C]), ALU.add)\
                     .then_inc(x1b_ready.sem, 1)

                with pool.Fori(0, TURNS) as i:
                    for s in range(STREAMS):
                        inverse_std(s)
                    for s in range(STREAMS):
                        mask_decays(s)
                    for s in range(STREAMS):
                        inverse_std(s)
                    for s in range(STREAMS):
                        inverse_std(s)
                    for s in range(STREAMS):
                        inverse_std(s)
                    for l in range(DEPTH):
                        for s in range(STREAMS):
                            for t in range(NT):
                                rotate(s, t)
                                inverse_norms(s, t)
                                scale_k(s, t)
                        for s in range(STREAMS):
                            mlp_inputs(l, s)
                        for s in range(STREAMS):
                            inverse_std(s)
                    for s in range(STREAMS):
                        inverse_std(s)
                    settle(pool, [stats_ready, dec_ready, prod_ready, ss_ready, x1_pool, g_step] + y_free)

            @block.scalar
            def _(act):
                A = nc.scalar

                def bank(ring):
                    j = ring.act_banks.pop(0)
                    return ring.banks[j], ring.evacuated[j]

                def normal_T(s):
                    b, free = bank(turn)
                    act.wait_ge(turn.to_act.sem, turn.to_act.next())
                    ins = A.activation(nT[s][:, :], b[:, 0:SEQ], ACT.Copy)
                    ins.then_inc(free, 1)

                def move_middle(s):
                    act.wait_ge(cum_act.sem, cum_act.next())
                    A.activation(cum3[s][32:32 + H, :], mid_bf[s][:, :], ACT.Copy).then_inc(mid_moved.sem, 1)

                def mlstm_heads(s):
                    for g2 in range(2):
                        b, free = bank(proj)
                        act.wait_ge(proj.to_act.sem, proj.to_act.next())
                        src = b[:, :].rearrange("p (a t) -> p a t", a=2)
                        for e in range(2):
                            ins = A.activation(bd[s][e * D:(e + 1) * D, 2 * g2:2 * g2 + 2, e, :],
                                               src[e * D:(e + 1) * D, :, :], ACT.Copy)
                        ins.then_inc(free, 1)
                    for t in range(NT):
                        b, free = bank(proj)
                        act.wait_ge(proj.to_act.sem, proj.to_act.next())
                        ins = A.activation(v[s][:, t, :, 0:D], b[:, :].rearrange("p (h d) -> p h d", h=H), ACT.Copy)
                        ins.then_inc(free, 1)
                    for t in range(NT):
                        b, free = bank(proj)
                        act.wait_ge(proj.to_act.sem, proj.to_act.next())
                        ins = A.activation(th[s][:, t, :], b[:, :], ACT.Tanh, scale=0.5)
                        ins.then_inc(free, 1)

                def decays(s):
                    dec = dec_v(s)
                    act.wait_ge(bias_ready.sem, bias_ready.next())
                    for p2 in range(PAIRS):
                        b, free = bank(proj)
                        act.wait_ge(proj.to_act.sem, proj.to_act.next())
                        src = b[:, :].rearrange("p (e t) -> p e t", e=2)
                        for e in range(2):
                            h = 2 * p2 + e
                            A.activation(dec[:, h, 0:SEQ], src[:, e, :], ACT.Exp, bias=src_bias[s][:, 0, h:h + 1])
                            ins = A.activation(dec[:, h, SEQ:DW], src[:, e, P:SEQ], ACT.Exp,
                                               bias=src_bias[s][:, 1, h:h + 1])
                        if p2 < PAIRS - 1:
                            ins.then_inc(free, 1)
                    ins.then_inc(a_step.sem, 1)
                    act.wait_ge(a_step.sem, a_step.next())
                    act.sem_inc(free, 1)
                    act.sem_inc(dec_ready.sem, 1)

                def outputs_T(s, t):
                    b, free = bank(turn)
                    act.wait_ge(turn.to_act.sem, turn.to_act.next())
                    ins = A.activation(hT[s][:, :, t * P:(t + 1) * P], b[:, :].rearrange("p (b t) -> p b t", b=4), ACT.Copy)
                    ins.then_inc(free, 1)

                def shifted_T(s):
                    b, free = bank(turn)
                    act.wait_ge(turn.to_act.sem, turn.to_act.next())
                    A.activation(sT[s][0:D, :], b[0:D, 0:SEQ], ACT.Copy)
                    ins = A.activation(sT[s][D:C, 1:SEQ], b[D:C, 0:SEQ - 1], ACT.Copy)
                    ins.then_inc(free, 1)

                def squares(s, t):
                    sq = sqr[t]
                    act.wait_ge(sq_free[t].sem, sq_free[t].next())
                    for w in range(2):
                        b, free = bank(proj)
                        act.wait_ge(proj.to_act.sem, proj.to_act.next())
                        A.activation(sq[:, w, :, :], b[:, :].rearrange("p (h d) -> p h d", h=H), ACT.Square)\
                         .then_inc(sq_ready.sem, 1)
                    b, free = bank(proj)
                    act.wait_ge(proj.to_act.sem, proj.to_act.next())
                    ins = A.activation(v[s][:, t, :, 0:D], b[:, :].rearrange("p (h d) -> p h d", h=H), ACT.Copy)
                    ins.then_inc(free, 1)

                def q_T(s, t):
                    b, free = bank(turn)
                    act.wait_ge(turn.to_act.sem, turn.to_act.next())
                    ins = A.activation(lin[s][:, :, t * P:(t + 1) * P], b[:, :].rearrange("p (b t) -> p b t", b=4), ACT.Copy)
                    ins.then_inc(free, 1)

                def softmax(s):
                    for g2 in range(2):
                        b, free = bank(score)
                        act.wait_ge(max_ready.sem, max_ready.next())
                        for j in range(4):
                            h = 4 * g2 + j
                            ins = A.activation(prob[s][:, h, 0:P], b[:, j * P:(j + 1) * P], ACT.Exp,
                                               scale=rs[s][:, 0, 0, h:h + 1], bias=nbias[s][:, 0, h:h + 1],
                                               accum_out=rsum[s][:, 0, h:h + 1])
                        ins.then_inc(free, 1)
                    for p2 in range(PAIRS):
                        b, free = bank(score)
                        act.wait_ge(max_ready.sem, max_ready.next())
                        for e in range(2):
                            h = 2 * p2 + e
                            ins = A.activation(prob[s][:, h, P + WINDOW:P + SEQ], b[:, e * KEYS:(e + 1) * KEYS], ACT.Exp,
                                               scale=rs[s][:, 1, 0, h:h + 1], bias=nbias[s][:, 1, h:h + 1],
                                               accum_out=rsum[s][:, 1, h:h + 1])
                        ins.then_inc(free, 1)

                def probs_T(s):
                    pt = pt_v(s)
                    for k in range(6):
                        if k % 2 == 0:
                            b, free = bank(turn)
                            act.wait_ge(turn.to_act.sem, turn.to_act.next())
                            ins = A.activation(pt[:, k // 2, 4 * (k % 2):4 * (k % 2) + 4, :],
                                               b[:, :].rearrange("p (h t) -> p h t", h=4), ACT.Copy)
                            ins.then_inc(free, 1)

                def gelu(l, s):
                    gl = gelu_v(s)
                    for k, (at, m) in enumerate(HB):
                        b, free = bank(proj)
                        act.wait_ge(proj.to_act.sem, proj.to_act.next())
                        A.activation(gl[0:m, k, :], b[0:m, 0:SEQ], ACT.Gelu,
                                     bias=b1_c[0:m, l, 1, k:k + 1]).then_inc(gelu_ready.sem, 1)

                for c in sq_free:
                    act.sem_inc(c.sem, 1)
                with act.Fori(0, TURNS) as i:
                    for s in range(STREAMS):
                        normal_T(s)
                    for s in range(STREAMS):
                        move_middle(s)
                    for s in range(STREAMS):
                        mlstm_heads(s)
                        decays(s)
                    for s in range(STREAMS):
                        for t in range(NT):
                            outputs_T(s, t)
                    for l in range(DEPTH):
                        for s in range(STREAMS):
                            shifted_T(s)
                        for s in range(STREAMS):
                            for t in range(NT):
                                squares(s, t)
                        for s in range(STREAMS):
                            for t in range(NT):
                                q_T(s, t)
                        for s in range(STREAMS):
                            softmax(s)
                        for s in range(STREAMS):
                            probs_T(s)
                        for s in range(STREAMS):
                            for t in range(NT):
                                outputs_T(s, t)
                        for s in range(STREAMS):
                            normal_T(s)
                        for s in range(STREAMS):
                            gelu(l, s)
                    settle(act, [r.to_act for r in RINGS] + [cum_act, bias_ready, max_ready, a_step] + sq_free)

            @block.vector
            def _(dve):
                V = nc.vector

                def link(ins):
                    ins.then_inc(v_step.sem, 1)
                    dve.wait_ge(v_step.sem, v_step.next())

                def bank(ring):
                    j = ring.dve_banks.pop(0)
                    return ring.banks[j], ring.evacuated[j]

                def stats_of(s, src):
                    for t in range(NT):
                        ins = V.bn_stats(stats[s][:, t, :], src[:, t, :])
                        ins.then_inc(v_step.sem, 1)
                        v_step.next()
                    dve.wait_ge(v_step.sem, v_step.seen)
                    for t in range(NT):
                        ins = V.bn_aggr(mv[s][:, t, :], stats[s][:, t, :])
                        if t < NT - 1:
                            ins.then_inc(v_step.sem, 1)
                            v_step.next()
                    link(ins)
                    dve.sem_inc(stats_ready.sem, 1)

                def normalise(s, dst, src, ready, link_it=False):
                    dve.wait_ge(rstd_ready.sem, rstd_ready.next())
                    for t in range(NT):
                        ins = V.tensor_scalar(dst[:, t, :], src[:, t, :], mv[s][:, t, 0:1], rstd[s][:, t:t + 1],
                                              ALU.subtract, ALU.mult)
                        if ready is not None:
                            ins.then_inc(ready.sem, 1)
                        if link_it:
                            ins.then_inc(v_step.sem, 1)
                            v_step.next()
                    if link_it:
                        dve.wait_ge(v_step.sem, v_step.seen)

                def gates(s):
                    b, free = bank(turn)
                    dve.wait_ge(turn.to_dve.sem, turn.to_dve.next())
                    link(V.tensor_tensor_scan(cum[s][:, :], bf_c[:, 0:1].broadcast_to([H, SEQ]), b[0:H, SEQ:2 * SEQ],
                                              0.0, ALU.add, ALU.add))
                    ins = V.scalar_tensor_tensor(gi[s][:, :], b[0:H, 0:SEQ], bi_c[:, 0:1], cum[s][:, :],
                                                 ALU.add, ALU.subtract)
                    ins.then_inc(free, 1)
                    link(V.tensor_copy(cum3[s][0:H, :], cum[s][:, :]))
                    link(V.tensor_tensor(rest[s][:, :], cum[s][:, :], cum3[s][0:H, :], ALU.subtract))
                    link(V.tensor_copy(mid_bf[s][:, :], rest[s][:, :]))
                    dve.sem_inc(cum_act.sem, 1)
                    V.tensor_tensor(cum3[s][64:64 + H, :], rest[s][:, :], mid_bf[s][:, :], ALU.subtract)\
                     .then_inc(cum_ready.sem, 1)

                def source_bias(s):
                    b, free = bank(turn)
                    dve.wait_ge(turn.to_dve.sem, turn.to_dve.next())
                    link(V.tensor_copy(src_bias[s][:, :, :], b[:, 0:NT * H].rearrange("p (t h) -> p t h", t=NT)))
                    dve.sem_inc(free, 1)
                    dve.sem_inc(bias_ready.sem, 1)

                def mlstm_k(s):
                    for g2 in range(2):
                        b, free = bank(proj)
                        dve.wait_ge(proj.to_dve.sem, proj.to_dve.next())
                        ins = V.tensor_scalar(lin[s][:, 2 * g2:2 * g2 + 2, :], b[:, :].rearrange("p (a t) -> p a t", a=2),
                                              D ** -0.5, None, ALU.mult)
                        ins.then_inc(free, 1)

                def weigh(s):
                    dec, wgt = dec_v(s), wgt_v(s)
                    dve.wait_ge(dec_masked.sem, dec_masked.next(NT))
                    for p2 in range(PAIRS):
                        b, free = bank(score)
                        dve.wait_ge(score.to_dve.sem, score.to_dve.next())
                        ins = V.tensor_tensor(wgt[:, 2 * p2:2 * p2 + 2, 0:SEQ], b[:, :].rearrange("p (e t) -> p e t", e=2),
                                              dec[:, 2 * p2:2 * p2 + 2, 0:SEQ], ALU.mult)
                        ins.then_inc(free, 1)
                    for g2 in range(2):
                        b, free = bank(score)
                        dve.wait_ge(score.to_dve.sem, score.to_dve.next())
                        ins = V.tensor_tensor(wgt[:, 4 * g2:4 * g2 + 4, SEQ:DW], b[:, :].rearrange("p (e t) -> p e t", e=4),
                                              dec[:, 4 * g2:4 * g2 + 4, SEQ:DW], ALU.mult)
                        ins.then_inc(free, 1)

                def head_outputs(s, t):
                    for g2 in range(2):
                        b, free = bank(acc)
                        dve.wait_ge(acc.to_dve.sem, acc.to_dve.next())
                        src = b[:, 0:4 * (D + 1)].rearrange("p (h d) -> p h d", h=4)
                        rd = rden[s][:, t, 4 * g2:4 * g2 + 4]
                        o = hs[s][:, t, 256 * g2:256 * g2 + 256].rearrange("p (h d) -> p h d", h=4)
                        link(V.tensor_scalar(rd, src[:, :, D], -1.0, 1.0, ALU.mult, ALU.max))
                        link(V.tensor_tensor(rd, src[:, :, D], rd, ALU.max))
                        link(V.reciprocal(rd, rd))
                        ins = V.scalar_tensor_tensor(o, th[s][:, t, 256 * g2:256 * g2 + 256].rearrange("p (h d) -> p h d", h=4),
                                                     1.0, src[:, :, 0:D], ALU.add, ALU.mult)
                        link(ins)
                        dve.sem_inc(free, 1)
                        link(V.scalar_tensor_tensor(o, o, 0.5, rd.unsqueeze(2).broadcast_to([P, 4, D]), ALU.mult, ALU.mult))

                def project_out(s):
                    b, free = bank(acc)
                    dve.wait_ge(acc.to_dve.sem, acc.to_dve.next())
                    ins = V.tensor_tensor(x1[s][:, :, :], b[:, 0:SEQ].rearrange("p (t c) -> p t c", t=NT),
                                          out_bias[:, :].unsqueeze(1).broadcast_to([P, NT, C]), ALU.add)
                    link(ins)
                    dve.sem_inc(free, 1)
                    stats_of(s, x1[s])

                def mlstm_residual(s):
                    normalise(s, x1[s], x1[s], None, link_it=True)
                    ins = V.tensor_tensor(mid[s][:, :, :], x1[s][:, :, :], x_in[s][:, :, :], ALU.add)
                    link(ins)
                    dve.sem_inc(x_free[s].sem, 1)
                    stats_of(s, mid[s])

                def rotary_products(l, s, t):
                    def announce(w, step, free):
                        dve.wait_ge(v_step.sem, step)
                        dve.sem_inc(prod_ready.sem, 1)
                        dve.sem_inc(free, 1)

                    made = []
                    for w in range(2):
                        b, free = bank(proj)
                        dve.wait_ge(sq_ready.sem, sq_ready.next())
                        dve.wait_ge(prod_free[w].sem, prod_free[w].next())
                        src = b[:, :].rearrange("p (h d) -> p h d", h=H).unsqueeze(1).broadcast_to([P, 2, H, D])
                        tab = rot[:, l, t, w, :, :].unsqueeze(2).broadcast_to([P, 2, H, D])
                        V.tensor_tensor(prod[w][:, :, :, :], src, tab, ALU.mult).then_inc(v_step.sem, 1)
                        made.append((w, v_step.next(), free))
                        if w:
                            announce(*made[0])
                    V.tensor_reduce(ss[s][:, t, :, :], sqr[t][:, :, :, :], axis=AXX, op=ALU.add)\
                     .then_inc(v_step.sem, 1)
                    reduced = v_step.next()
                    announce(*made[1])
                    dve.wait_ge(v_step.sem, reduced)
                    dve.sem_inc(sq_free[t].sem, 1)
                    V.tensor_scalar(ss[s][:, t, :, :], ss[s][:, t, :, :], 1e-24, None, ALU.max)\
                     .then_inc(ss_ready.sem, 1)

                def k_T(s, t):
                    b, free = bank(turn)
                    dve.wait_ge(turn.to_dve.sem, turn.to_dve.next())
                    src = b[:, :].rearrange("p (b t) -> p b t", b=4)
                    for e in range(2):
                        ins = V.tensor_copy(bd[s][e * D:(e + 1) * D, :, e, t * P:(t + 1) * P], src[e * D:(e + 1) * D, :, :])
                    ins.then_inc(free, 1)

                def maxima(s, t, h, n, view):
                    dve.wait_ge(score.to_dve.sem, score.to_dve.next())
                    link(V.tensor_reduce(smax[s][:, t, h:h + n], view, axis=AXX, op=ALU.max))
                    V.scalar_tensor_tensor(nbias[s][:, t, h:h + n], smax[s][:, t, h:h + n], -1.0,
                                           rs[s][:, t, 0, h:h + n], ALU.mult, ALU.mult).then_inc(max_ready.sem, 1)

                def score_max(s):
                    for g2 in range(2):
                        b, _ = bank(score)
                        maxima(s, 0, 4 * g2, 4, b[:, :].rearrange("p (h t) -> p h t", h=4))
                    for p2 in range(PAIRS):
                        b, _ = bank(score)
                        maxima(s, 1, 2 * p2, 2, b[:, 0:2 * KEYS].rearrange("p (h t) -> p h t", h=2))

                def probs_T(s):
                    pt = pt_v(s)
                    for k in range(6):
                        if k % 2:
                            b, free = bank(turn)
                            dve.wait_ge(turn.to_dve.sem, turn.to_dve.next())
                            ins = V.tensor_copy(pt[:, k // 2, 4 * (k % 2):4 * (k % 2) + 4, :],
                                                b[:, :].rearrange("p (h t) -> p h t", h=4))
                            ins.then_inc(free, 1)

                def attention_out(s, t):
                    b, free = bank(acc)
                    dve.wait_ge(acc.to_dve.sem, acc.to_dve.next())
                    link(V.reciprocal(rinv[s][:, t, :], rsum[s][:, t, :]))
                    ins = V.tensor_tensor(th[s][:, t, :].rearrange("p (h d) -> p h d", h=H),
                                          b[:, :].rearrange("p (h d) -> p h d", h=H),
                                          rinv[s][:, t, :].unsqueeze(2).broadcast_to([P, H, D]), ALU.mult)
                    ins.then_inc(free, 1)

                def attention_residual(s):
                    b, free = bank(acc)
                    dve.wait_ge(acc.to_dve.sem, acc.to_dve.next())
                    ins = V.tensor_tensor(x1[s][:, :, :], b[:, 0:SEQ].rearrange("p (t c) -> p t c", t=NT),
                                          xb[s][:, :, :], ALU.add)
                    link(ins)
                    dve.sem_inc(x1_ready[s].sem, 1)
                    dve.sem_inc(x1_pool.sem, 1)
                    dve.sem_inc(free, 1)

                def shifted_stats(s):
                    dve.wait_ge(half_kept.sem, half_kept.next())
                    dve.wait_ge(shifted[s].sem, shifted[s].next(32))
                    stats_of(s, xs[s])

                def hidden(l, s):
                    hd, gl = hid_v(s), gelu_v(s)
                    for k, (at, m) in enumerate(HB):
                        b, free = bank(proj)
                        dve.wait_ge(gelu_ready.sem, gelu_ready.next())
                        ins = V.scalar_tensor_tensor(hd[0:m, k, :], b[0:m, SEQ:2 * SEQ], b1_c[0:m, l, 0, k:k + 1],
                                                     gl[0:m, k, :], ALU.add, ALU.mult)
                        ins.then_inc(free, 1)

                def mlp_residual(l, s):
                    b, free = bank(acc)
                    dve.wait_ge(acc.to_dve.sem, acc.to_dve.next())
                    dve.wait_ge(x1b_ready.sem, x1b_ready.next())
                    ins = V.tensor_tensor(xb[s][:, :, :], b[:, 0:SEQ].rearrange("p (t c) -> p t c", t=NT),
                                          x1b[s][:, :, :], ALU.add)
                    link(ins)
                    dve.sem_inc(free, 1)

                for c in prod_free:
                    dve.sem_inc(c.sem, 1)
                with dve.Fori(0, TURNS) as i:
                    for s in range(STREAMS):
                        dve.wait_ge(x_loaded[s].sem, x_loaded[s].next(16))
                        stats_of(s, x_in[s])
                    for s in range(STREAMS):
                        normalise(s, nrm[s], x_in[s], nrm_ready)
                    for s in range(STREAMS):
                        gates(s)
                    for s in range(STREAMS):
                        source_bias(s)
                    for s in range(STREAMS):
                        mlstm_k(s)
                        weigh(s)
                        for t in range(NT):
                            head_outputs(s, t)
                        stats_of(s, hs[s])
                    for s in range(STREAMS):
                        normalise(s, hs[s], hs[s], hn_ready)
                    for s in range(STREAMS):
                        project_out(s)
                    for s in range(STREAMS):
                        mlstm_residual(s)
                    for s in range(STREAMS):
                        normalise(s, xb[s], mid[s], res_ready)
                    for l in range(DEPTH):
                        for s in range(STREAMS):
                            for t in range(NT):
                                rotary_products(l, s, t)
                        for s in range(STREAMS):
                            for t in range(NT):
                                k_T(s, t)
                        for s in range(STREAMS):
                            score_max(s)
                        for s in range(STREAMS):
                            probs_T(s)
                        for s in range(STREAMS):
                            for t in range(NT):
                                attention_out(s, t)
                        for s in range(STREAMS):
                            attention_residual(s)
                        for s in range(STREAMS):
                            shifted_stats(s)
                        for s in range(STREAMS):
                            normalise(s, nrm[s], xs[s], nrm_ready)
                        for s in range(STREAMS):
                            hidden(l, s)
                        for s in range(STREAMS):
                            mlp_residual(l, s)
                    for s in range(STREAMS):
                        stats_of(s, xb[s])
                    for s in range(STREAMS):
                        normalise(s, x1[s], xb[s], None, link_it=True)
                        V.tensor_tensor(y[s][:, :, :], x1[s][:, :, :], mid[s][:, :, :], ALU.add)\
                         .then_inc(y_ready[s].sem, 1)
                    settle(dve, [r.to_dve for r in RINGS] + x_loaded + shifted + prod_free +
                           [rstd_ready, v_step, dec_masked, sq_ready, half_kept, gelu_ready, x1b_ready])


_INS = ["L0_attn_x", "L0_attn_Wq", "L0_attn_Wk", "L0_attn_Wv", "L0_attn_Wi", "L0_attn_bi", "L0_attn_Wf", "L0_attn_bf",
        "L0_attn_Wo", "L0_attn_bo", "L0_attn_W_out", "L0_attn_ln_g", "L0_attn_ln_b", "L0_ffn_wqkv", "L0_ffn_q_scale",
        "L0_ffn_k_scale", "L0_ffn_wo", "L0_ffn_ln_g", "L0_ffn_ln_b", "L0_ffn_w1", "L0_ffn_b1", "L0_ffn_w2", "L0_ffn_b2"]


def rotary_factors():
    import numpy as np

    half = np.arange(0, D, 2, dtype=np.float32)
    inv_freq = (np.float32(1.0) / np.float32(10000.0) ** (half / np.float32(D))).astype(np.float32)
    t = np.arange(SEQ, dtype=np.float32)
    freqs = np.concatenate([t[:, None] * inv_freq[None, :]] * 2, axis=-1)
    base = ((half + np.float32(0.4 * D)) / np.float32(1.4 * D)).astype(np.float32)
    power = ((t - SEQ // 2) / np.float32(WINDOW // 2)).astype(np.float32)
    scale = np.concatenate([base[None, :].astype(np.float64) ** power[:, None]] * 2, axis=-1)
    cos, sin = np.cos(freqs.astype(np.float64)), np.sin(freqs.astype(np.float64))
    sign = np.concatenate([np.ones(D // 2), -np.ones(D // 2)])
    q = np.stack([cos * scale, sin * scale * sign], axis=1) * 8.0
    k = np.stack([cos / scale, sin / scale * sign], axis=1)
    return np.ascontiguousarray(np.stack([q, k], axis=1).reshape(SEQ, 4 * D).astype(np.float32))


def kernel(**inputs):
    import numpy as _np
    import concourse.bacc as _bacc
    from concourse import mybir as _mybir
    from concourse.bass_utils import run_bass_kernel_spmd as _run

    nc = _bacc.Bacc("TRN2", target_bir_lowering=False, num_devices=1)
    arrays, args = {}, []
    for name in _INS + ["rotary"]:
        a = rotary_factors() if name == "rotary" else _np.ascontiguousarray(inputs[name])
        arrays[f"in_{name}_dram"] = a
        args.append(nc.dram_tensor(f"in_{name}_dram", a.shape, _mybir.dt.from_np(a.dtype), kind="ExternalInput").ap())
    shape = arrays["in_L0_attn_x_dram"].shape
    args.append(nc.dram_tensor("out_dram", shape, _mybir.dt.float32, kind="ExternalOutput").ap())
    block_kernel(nc, *args)
    r = _run(nc, [arrays], core_ids=[0])
    return r.results[0]["out_dram"]
```

```python
import concourse.bass as bass
from concourse import mybir
from contextlib import ExitStack


F32 = mybir.dt.float32
BF16 = mybir.dt.bfloat16
ALU = mybir.AluOpType
ACT = mybir.ActivationFunctionType
AXX = mybir.AxisListType.X

P = 128
C = 128
SEQ = 256
NT = SEQ // P
H = 8
D = 64
HD = H * D
PAIRS = H // 2
WINDOW = 64
DEPTH = 2
HID = 341
HB = [(0, 128), (128, 128), (256, 85)]
DW = SEQ + P
KEYS = P + WINDOW
MASKED = -1.0e30
EPS = 1e-5
MLSTM = 0
LAYERS = (1, 2)

PARTS = {
    "mlstm": (MLSTM, {
        "x_stats":        (None, None,    1,    0),
        "x_norm":         (None, None,    5, None),
        "x_turn":         (   5,    3, None, None),
        "gates":          (   8,    8,   11, None),
        "heads_q":        (  13,   10, None, None),
        "gate_bias":      (  15, None,   18, None),
        "heads_k":        (  19, None,   20, None),
        "heads_v":        (  23,   16, None, None),
        "heads_o":        (  30,   22, None, None),
        "decays0":        (  32,   23, None,    7),
        "decays1":        (  34,   25, None,    8),
        "weights0":       (  37, None,   35, None),
        "weights1":       (  40, None,   38, None),
        "weights2":       (  42, None,   39, None),
        "heads_out0":     (  45, None,   44, None),
        "heads_out1":     (  48, None,   47,   11),
        "outputs_norm":   (None, None,   49, None),
        "outputs0":       (  52,   38, None, None),
        "outputs1":       (  54,   39, None, None),
        "mlstm_project":  (  56, None,   55,   13),
        "mlstm_residual": (None, None,   57,   14),
        "mlstm_out":      (None, None,   59, None),
    }),
    "front1": (1, {
        "pass_front":     (None, None,   10, None),
        "layer_in":       (  20,   14, None, None),
        "project0":       (  36,   27,   32,    9),
        "project1":       (  38,   28,   36,   10),
        "keep":           (None, None,   41, None),
        "rotated0":       (  47,   33,   46, None),
        "rotated1":       (  51,   35,   51, None),
        "scores0":        (  55,   40,   53, None),
        "scores1":        (  57,   41,   56, None),
        "scores2":        (  58,   42,   58, None),
    }),
    "back1": (1, {
        "pass_back":      (None, None,    9, None),
        "probs0":         (  11,    7,   12, None),
        "probs1":         (  12,    9,   14, None),
        "probs2":         (  14,   11,   15, None),
        "values0":        (  17, None,   21, None),
        "values1":        (  22, None,   24, None),
        "outputs0":       (  24,   18, None, None),
        "outputs1":       (  27,   19, None, None),
        "residual":       (  28, None,   27,    5),
        "shifted_stats":  (None, None,   29,    6),
        "shifted_norm":   (None, None,   31, None),
        "mlp_in":         (  39,   29, None, None),
        "mlp_up0":        (  41,   30,   40, None),
        "mlp_up1":        (  43,   31,   42, None),
        "mlp_up2":        (  46,   32,   45, None),
        "mlp_down":       (  50, None,   50, None),
    }),
    "front2": (2, {
        "pass_front":     (None, None,    4, None),
        "layer_in":       (   9,    6, None, None),
        "project0":       (  16,   12,   17,    3),
        "project1":       (  25,   17,   23,    4),
        "keep":           (None, None,   25, None),
        "rotated0":       (  31,   24,   30, None),
        "rotated1":       (  35,   26,   33, None),
        "scores0":        (  44,   34,   43, None),
        "scores1":        (  49,   36,   48, None),
        "scores2":        (  53,   37,   52, None),
    }),
    "back2": (2, {
        "pass_back":      (None, None,    0, None),
        "probs0":         (   0,    0,    2, None),
        "probs1":         (   1,    1,    3, None),
        "probs2":         (   2,    2,    6, None),
        "values0":        (   3, None,    7, None),
        "values1":        (   4, None,    8, None),
        "outputs0":       (   6,    4, None, None),
        "outputs1":       (   7,    5, None, None),
        "residual":       (  10, None,   13,    1),
        "shifted_stats":  (None, None,   16,    2),
        "shifted_norm":   (None, None,   19, None),
        "mlp_in":         (  18,   13, None, None),
        "mlp_up0":        (  21,   15,   22, None),
        "mlp_up1":        (  26,   20,   26, None),
        "mlp_up2":        (  29,   21,   28, None),
        "mlp_down":       (  33, None,   34, None),
        "final_stats":    (None, None,   37,   12),
        "final":          (None, None,   54, None),
    }),
}
TENSOR, SCALAR, VECTOR, GPSIMD = range(4)


def schedule(parts, engine):
    order = []
    for part in parts:
        lane, stages = PARTS[part]
        order += [(places[engine], lane, name) for name, places in stages.items() if places[engine] is not None]
    return [(lane, name) for _, lane, name in sorted(order)]


FULL_TURN = tuple(PARTS)
FIRST_TURNS = [FULL_TURN[:n] for n in range(1, len(PARTS))]
LAST_TURNS = [FULL_TURN[n:] for n in range(1, len(PARTS))]


class Count:

    def __init__(self, sem):
        self.sem, self.seen = sem, 0

    def next(self, n=1):
        self.seen += n
        return self.seen


def settle(engine, counts):
    for c in counts:
        if c.seen:
            engine.sem_inc(c.sem, -c.seen)
            c.seen = 0


def block_kernel(nc, x, Wq, Wk, Wv, Wi, bi, Wf, bf, Wo, bo, W_out, lng, lnb,
                 wqkv, qsc, ksc, wo, lg, lb, w1, b1, w2, b2, rotary, out):
    ctx = ExitStack()
    with ctx:
        def sb(name, shape, dt=F32):
            return ctx.enter_context(nc.sbuf_tensor(name, shape, dt))

        def sem(name):
            return ctx.enter_context(nc.semaphore(name))

        ident = sb("ident", [P, P])
        ident_bf = sb("ident_bf", [P, P], BF16)
        band0 = sb("band0", [P, 2, P], BF16)
        band1 = sb("band1", [P, 2, KEYS], BF16)
        pick = sb("pick", [P, H, P], BF16)
        ones_bf = sb("ones_bf", [P, P], BF16)
        minus_half = sb("minus_half", [P, 4 * H])
        wqT = sb("wqT", [C, HD])
        wkT = sb("wkT", [C, HD])
        wvT = sb("wvT", [C, HD])
        woT = sb("woT", [C, HD])
        wiT = sb("wiT", [C, H])
        wfT = sb("wfT", [C, H])
        bi_c = sb("bi_c", [H, 1])
        bf_c = sb("bf_c", [H, 1])
        bo3 = sb("bo3", [P, HD], BF16)
        w_out = sb("w_out", [P, 4, C])
        out_bias = sb("out_bias", [P, C])
        wqkv_sb = sb("wqkv_sb", [C, DEPTH, 3 * HD])
        wo_sb = sb("wo_sb", [P, DEPTH, 4, C])
        w1_sb = sb("w1_sb", [C, DEPTH, 2 * HID])
        w2_sb = sb("w2_sb", [P, DEPTH, 3, C])
        b1_c = sb("b1_c", [P, DEPTH, 2, 3])
        b2_sb = sb("b2_sb", [P, DEPTH, C])
        rot = sb("rot", [P, DEPTH, NT, 2, 2, D])

        def lanes(name, shape, dt=F32, of=(MLSTM, *LAYERS)):
            return {s: sb(f"{name}{s}", shape, dt) for s in of}

        x1 = lanes("x1", [P, NT, C])
        nrm = lanes("nrm", [P, NT, C])
        passed = [sb(f"passed{n}", [P, NT, C]) for n in range(len(PARTS))]
        stats = lanes("stats", [P, NT, 6])
        mv = lanes("mv", [P, NT, 2])
        veps = lanes("veps", [P, NT])
        rstd = lanes("rstd", [P, NT])
        nT = lanes("nT", [C, SEQ])
        lin = lanes("lin", [P, PAIRS, SEQ])
        bd = lanes("bd", [P, PAIRS, 2, SEQ])
        v = lanes("v", [P, NT, H, D + 1])
        x_in = sb("x_in", [P, NT, C])
        work = sb("work", [P, H, DW])
        th = sb("th", [P, NT, HD])
        hs = sb("hs", [P, NT, HD])
        cum = hs[0:H, 0, 0:SEQ]
        gi = hs[0:H, 0, SEQ:2 * SEQ]
        rest = hs[0:H, 1, 0:SEQ]
        mid_bf = sb("mid_bf", [H, SEQ], BF16)
        cum3 = sb("cum3", [P, SEQ], BF16)
        src_bias = sb("src_bias", [P, NT, H])
        rden = sb("rden", [P, NT, H])
        xb = lanes("xb", [P, NT, C], of=LAYERS)
        xr = lanes("xr", [P, NT, C], of=LAYERS)
        x1b = lanes("x1b", [P, NT, C], of=LAYERS)
        xs = lanes("xs", [P, NT, C], of=LAYERS)
        sT = lanes("sT", [C, SEQ], of=LAYERS)
        prob = lanes("prob", [P, H * (P + SEQ)], of=LAYERS)
        ss = lanes("ss", [P, NT, 2, H], of=LAYERS)
        rs = lanes("rs", [P, NT, 2, H], of=LAYERS)
        nbias = lanes("nbias", [P, NT, H], of=LAYERS)
        smax = lanes("smax", [P, NT, H], of=LAYERS)
        rsum = lanes("rsum", [P, NT, H], of=LAYERS)
        rinv = lanes("rinv", [P, NT, H], of=LAYERS)
        y = x1b[2]
        prod = [sb(f"prod{j}", [P, 2, H, D]) for j in range(2)]
        sqr = [sb(f"sqr{t}", [P, 2, H, D]) for t in range(NT)]
        rotr = [sb(f"rotr{t}", [P, 2, H, D]) for t in range(NT)]
        pt = sb("pt", [P, 3, H, P])

        prob0 = {s: prob[s][:, 0:H * P].rearrange("p (h t) -> p h t", h=H) for s in LAYERS}
        prob1 = {s: prob[s][:, H * P:3 * H * P].rearrange("p (h t) -> p h t", h=H) for s in LAYERS}
        o_sb = {s: lin[s][:, :, :].rearrange("p a (b t) -> p (a b t)", b=2).rearrange("p (t n) -> p t n", t=NT)
                for s in LAYERS}
        hT = {s: prob[s][:, 0:4 * SEQ].rearrange("p (b t) -> p b t", b=4) for s in LAYERS}
        hT[MLSTM] = lin[MLSTM]
        hid = {s: prob[s][:, 0:3 * SEQ].rearrange("p (b t) -> p b t", b=3) for s in LAYERS}
        gel = {s: lin[s][:, 0:3, :] for s in LAYERS}

        class Ring:
            def __init__(self, name):
                self.banks = [ctx.enter_context(nc.psum_tensor(f"{name}{j}", [P, 512], F32)) for j in range(2)]
                self.to_act = Count(sem(f"{name}_ready_for_scalar"))
                self.to_dve = Count(sem(f"{name}_ready_for_vector"))
                self.evacuated = [sem(f"{name}{j}_evacuated") for j in range(2)]
                self.uses = [0, 0]
                self.act_banks, self.dve_banks = [], []

        proj, score, turn, acc = Ring("proj"), Ring("score"), Ring("turn"), Ring("acc")
        RINGS = (proj, score, turn, acc)

        load_s = sem("weights_loaded")
        set_d = sem("setup_vector_done")
        set_a = sem("setup_scalar_done")
        set_p = sem("setup_tensor_done")
        set_g = sem("setup_gpsimd_done")

        x_loaded = Count(sem("x_loaded"))
        x_free = Count(sem("x_free"))
        y_ready = Count(sem("y_ready"))
        y_stored = Count(sem("y_stored"))
        y_free = Count(sem("y_free"))
        x1_ready = {s: Count(sem(f"x1_ready{s}")) for s in LAYERS}
        x1_pool = {s: Count(sem(f"x1_ready_for_gpsimd{s}")) for s in LAYERS}
        shifted = {s: Count(sem(f"x1_shifted{s}")) for s in LAYERS}
        half_kept = {s: Count(sem(f"first_half_copied{s}")) for s in LAYERS}
        x1b_ready = {s: Count(sem(f"x1_with_bias_ready{s}")) for s in LAYERS}
        stats_ready = {s: Count(sem(f"stats_ready{s}")) for s in (MLSTM, *LAYERS)}
        rstd_ready = {s: Count(sem(f"rstd_ready{s}")) for s in (MLSTM, *LAYERS)}
        nrm_ready = {s: Count(sem(f"normalised_ready{s}")) for s in (MLSTM, *LAYERS)}
        hn_ready = Count(sem("head_outputs_ready"))
        res_ready = {s: Count(sem(f"residual{s}_ready")) for s in LAYERS}
        cum_ready = Count(sem("split_cumulative_ready"))
        cum_act = Count(sem("cumulative_middle_ready"))
        mid_moved = Count(sem("cumulative_middle_moved"))
        bias_ready = Count(sem("source_bias_ready"))
        dec_ready = Count(sem("decays_ready"))
        dec_masked = Count(sem("decays_masked"))
        sq_ready = {s: Count(sem(f"squares_ready{s}")) for s in LAYERS}
        ss_ready = {s: Count(sem(f"sums_of_squares_ready{s}")) for s in LAYERS}
        prod_ready = {s: Count(sem(f"rotary_products_ready{s}")) for s in LAYERS}
        prod_free = [Count(sem(f"prod{j}_free")) for j in range(2)]
        rot_ready = {s: Count(sem(f"rotated_ready{s}")) for s in LAYERS}
        max_ready = {s: Count(sem(f"score_max_ready{s}")) for s in LAYERS}
        gelu_ready = {s: Count(sem(f"gelu_ready{s}")) for s in LAYERS}
        v_step = Count(sem("vector_step"))
        a_step = Count(sem("scalar_step"))
        g_step = Count(sem("gpsimd_step"))

        def rows(ap, n=P):
            return ap.rearrange("(b p) c -> p b c", p=n)

        n_q, n_k, n_v, n_o, n_w = (prob[1][:, j * HD:(j + 1) * HD] for j in range(5))
        w_raw = prob[1][:, 5 * HD:6 * HD].rearrange("p (b c) -> p b c", b=4)
        w1_n = prob[2][:, 0:2 * 2 * HID].rearrange("p (l n) -> p l n", l=DEPTH)
        tables = prob[2][:, 4 * HID:4 * HID + NT * 4 * D].rearrange("p (t n) -> p t n", t=NT)
        scales = prob[2][:, 4 * HID + NT * 4 * D:4 * HID + NT * 4 * D + DEPTH * 2 * D]\
            .rearrange("p (l w d) -> p l w d", l=DEPTH, w=2)
        n_i, n_f = nrm[0][0:H, 0, :], nrm[0][0:H, 1, :]
        lng_c = nrm[1][:, 0, 0:4]
        lnb_c = nrm[1][:, 0, 4:8]
        lb_c = nrm[1][:, 0, 8:8 + DEPTH]
        lg_c = nrm[1][:, 0, 16:16 + DEPTH]
        b1_n = nrm[1][:, 1, 0:6 * DEPTH].rearrange("p (l w b) -> p l w b", l=DEPTH, w=2)
        lnb_w = x1[1][:, :, :].rearrange("p t c -> p (t c)")
        lnb_w2 = x1[2][:, :, :].rearrange("p t c -> p (t c)")
        bo_n = work[0:1, 0:2, 0:SEQ]
        bo_r = work[0:1, 2:4, 0:SEQ]
        loads, setup_g = [0], [0]

        with nc.Block() as block:
            @block.sync
            def _(sp):
                def load(dst, src):
                    with nc.allow_non_contiguous_dma(reason="a few hundred words of biases, once"):
                        sp.dma_start(dst, src).then_inc(load_s, 16)
                    loads[0] += 16

                for dst, src in ((n_q, Wq), (n_k, Wk), (n_v, Wv), (n_o, Wo)):
                    load(dst.rearrange("p (b c) -> p b c", b=4), rows(src))
                load(n_w, W_out)
                load(n_i, Wi)
                load(n_f, Wf)
                load(bi_c[:, :], bi.rearrange("(p o) -> p o", o=1))
                load(bf_c[:, :], bf.rearrange("(p o) -> p o", o=1))
                load(bo_n, bo.rearrange("(o a n) -> o a n", o=1, a=2))
                load(lng_c, lng.rearrange("(b p) -> p b", p=P))
                load(lnb_c, lnb.rearrange("(b p) -> p b", p=P))
                load(lb_c, lb.rearrange("l p -> p l"))
                load(lg_c, lg.rearrange("l p -> p l"))
                load(tables, rotary.rearrange("(t p) n -> p t n", p=P))
                for l in range(DEPTH):
                    load(wqkv_sb[:, l, :], wqkv[l, :, :])
                    load(wo_sb[:, l, :, :], rows(wo[l, :, :]))
                    load(w1_n[:, l, :], w1[l, :, :])
                    for b, (at, n) in enumerate(HB):
                        load(w2_sb[0:n, l, b, :], w2[l, at:at + n, :])
                        for w in range(2):
                            a = w * HID + at
                            load(b1_n[0:n, l, w, b:b + 1], b1[l, a:a + n].rearrange("(p o) -> p o", o=1))
                    load(b2_sb[:, l, :], b2[l, :].partition_broadcast(P))
                    load(scales[:, l, 0, :], qsc[l, :].partition_broadcast(P))
                    load(scales[:, l, 1, :], ksc[l, :].partition_broadcast(P))

            @block.gpsimd
            def _(pool):
                g = nc.gpsimd
                n = [0]

                def link(ins):
                    n[0] += 1
                    ins.then_inc(set_g, 1)
                    pool.wait_ge(set_g, n[0])

                link(g.memset(ident[:, :], 0.0))
                link(g.affine_select(out=ident[:, :], in_=ident[:, :], compare_op=ALU.not_equal, fill=1.0,
                                     base=0, pattern=[[-1, P]], channel_multiplier=1))
                link(g.tensor_copy(ident_bf[:, :], ident[:, :]))
                link(g.memset(band0[:, :, :], 0.0))
                link(g.memset(band1[:, :, :], 0.0))
                link(g.affine_select(out=band0[:, :, :], in_=band0[:, :, :], compare_op=ALU.is_ge, fill=MASKED,
                                     base=0, pattern=[[0, 2], [-1, P]], channel_multiplier=1))
                link(g.affine_select(out=band0[:, :, :], in_=band0[:, :, :], compare_op=ALU.is_ge, fill=MASKED,
                                     base=WINDOW, pattern=[[0, 2], [1, P]], channel_multiplier=-1))
                link(g.affine_select(out=band1[:, :, :], in_=band1[:, :, :], compare_op=ALU.is_ge, fill=MASKED,
                                     base=P - WINDOW, pattern=[[0, 2], [-1, KEYS]], channel_multiplier=1))
                link(g.affine_select(out=band1[:, :, :], in_=band1[:, :, :], compare_op=ALU.is_ge, fill=MASKED,
                                     base=0, pattern=[[0, 2], [1, KEYS]], channel_multiplier=-1))
                link(g.memset(pick[:, :, :], 0.0))
                for part in range(3):
                    link(g.affine_select(out=pick[:, :, :], in_=pick[:, :, :], compare_op=ALU.not_equal, fill=1.0,
                                         base=-32 * part, pattern=[[-1, H], [0, P]], channel_multiplier=1))
                link(g.memset(ones_bf[:, :], 1.0))
                link(g.memset(minus_half[:, :], -0.5))
                link(g.memset(bo3[:, :], 0.0))
                for s in (MLSTM, *LAYERS):
                    link(g.memset(bd[s][:, :, :, :], 0.0))
                    link(g.memset(v[s][:, :, :, D:D + 1], 1.0))
                for s in LAYERS:
                    link(g.memset(sT[s][:, 0:1], 0.0))
                    link(g.memset(xs[s][:, :, :], 0.0))
                link(g.memset(cum3[:, :], 0.0))
                setup_g[0] = n[0]


            @block.tensor
            def _(pe):
                pe.wait_ge(load_s, loads[0])
                pe.wait_ge(set_g, setup_g[0])
                bank = [proj.banks[0], proj.banks[1], score.banks[0], score.banks[1], turn.banks[0]]
                for j, src in enumerate((n_q, n_k, n_v, n_o, n_w)):
                    for b in range(4):
                        last = nc.tensor.transpose(bank[j][:, b * P:(b + 1) * P], src[:, b * P:(b + 1) * P], ident[:, :])
                nc.tensor.transpose(turn.banks[1][:, 0:H], n_i, ident[0:H, 0:H])
                last = nc.tensor.transpose(turn.banks[1][:, H:2 * H], n_f, ident[0:H, 0:H])
                last.then_inc(set_p, 1)
                pe.wait_ge(set_d, 8)
                for b in range(4):
                    half = (lnb_w if b < 2 else lnb_w2)[:, (b % 2) * P:(b % 2 + 1) * P]
                    nc.tensor.matmul(acc.banks[0][:, 0:C], half, w_raw[:, b, :], start=(b == 0), stop=(b == 3))
                for l in range(DEPTH):
                    for w in range(2):
                        for b, (at, m) in enumerate(HB):
                            a = w * HID + at
                            last = nc.tensor.matmul(acc.banks[1][0:m, (l * 2 + w) * 3 + b:(l * 2 + w) * 3 + b + 1],
                                                    w1_n[:, l, a:a + m], lb_c[:, l:l + 1], start=True, stop=True)
                last.then_inc(set_p, 1)

            @block.scalar
            def _(act):
                act.wait_ge(set_p, 1)
                for dst, src in ((wqT, proj.banks[0]), (wkT, proj.banks[1]), (wvT, score.banks[0]), (woT, score.banks[1])):
                    nc.scalar.activation(dst[:, :], src[:, :], ACT.Copy).then_inc(set_a, 1)

            @block.vector
            def _(dve):
                V = nc.vector
                n = [0]

                def link(ins):
                    n[0] += 1
                    ins.then_inc(set_d, 1)
                    dve.wait_ge(set_d, n[0])

                dve.wait_ge(set_p, 1)
                link(V.tensor_copy(wiT[:, :], turn.banks[1][:, 0:H]))
                link(V.tensor_copy(wfT[:, :], turn.banks[1][:, H:2 * H]))
                link(V.tensor_copy(w_raw, turn.banks[0][:, :].rearrange("p (b c) -> p b c", b=4)))
                link(V.tensor_tensor(w_out[:, :, :], w_raw, lng_c.unsqueeze(2).broadcast_to([P, 4, C]), ALU.mult))
                for b in range(4):
                    half = (lnb_w if b < 2 else lnb_w2)[:, (b % 2) * P:(b % 2 + 1) * P]
                    link(V.tensor_copy(half, lnb_c[:, b:b + 1].broadcast_to([P, P])))
                for l in range(DEPTH):
                    link(V.tensor_scalar(w1_sb[:, l, :], w1_n[:, l, :], lg_c[:, l:l + 1], None, ALU.mult))
                for l in range(DEPTH):
                    for t in range(NT):
                        tab = tables[:, t, :].rearrange("p (w u d) -> p w u d", w=2, u=2)
                        sc = scales[:, l, :, :].unsqueeze(2).broadcast_to([P, 2, 2, D])
                        link(V.tensor_tensor(rot[:, l, t, :, :, :], tab, sc, ALU.mult))
                def halves(ap):
                    return ap.rearrange("o (a n) -> o a n", a=2)

                link(V.tensor_copy(halves(bo3[0:1, :]), bo_n))
                link(V.tensor_tensor(bo_r, bo_n, halves(bo3[0:1, :]), ALU.subtract))
                link(V.tensor_copy(halves(bo3[32:33, :]), bo_r))
                for a in range(2):
                    link(V.tensor_copy(mid_bf[0:1, :], bo_r[:, a, :]))
                    link(V.tensor_tensor(bo3[64:65, a * SEQ:(a + 1) * SEQ], bo_r[:, a, :], mid_bf[0:1, :], ALU.subtract))
                dve.wait_ge(set_p, 2)
                link(V.tensor_copy(out_bias[:, :], acc.banks[0][:, 0:C]))
                for l in range(DEPTH):
                    for b, (at, m) in enumerate(HB):
                        col = acc.banks[1][0:m, l * 6 + b:l * 6 + b + 4:3]
                        link(V.tensor_tensor(b1_c[0:m, l, :, b], b1_n[0:m, l, :, b], col, ALU.add))
                for s in LAYERS:
                    link(V.memset(prob1[s][:, :, 0:WINDOW], 0.0))

        SEQS = x.shape[0]
        FULL = SEQS - len(FIRST_TURNS)

        def walk(which, engine, stages, settle_turn):
            def turn_of(parts):
                for lane, name in schedule(parts, which):
                    stages[name](lane)
                settle_turn()

            for parts in FIRST_TURNS:
                turn_of(parts)
            with engine.Fori(0, FULL):
                turn_of(FULL_TURN)
            for parts in LAST_TURNS:
                turn_of(parts)
        xv = x.rearrange("b (t p) c -> b p t c", p=P)
        ov = out.rearrange("b (t p) c -> b p t c", p=P)

        with nc.Block() as block:
            @block.tensor
            def _(pe):
                T = nc.tensor
                at = {r: 0 for r in RINGS}

                class Use:

                    def __init__(self, ring, j):
                        self.tile, self.sem, self.value = ring.banks[j], ring.evacuated[j], ring.uses[j] + 1

                def claim(ring, to_act=False, to_dve=False):
                    j = at[ring] % 2
                    at[ring] += 1
                    pe.wait_ge(ring.evacuated[j], ring.uses[j] + 1)
                    ring.uses[j] += 1
                    if to_act:
                        ring.act_banks.append(j)
                    if to_dve:
                        ring.dve_banks.append(j)
                    return Use(ring, j)

                def wait_evacuated(uses):
                    for u in {u.sem.name: u for u in sorted(uses, key=lambda u: u.value)}.values():
                        pe.wait_ge(u.sem, u.value)

                made = {s: {} for s in (MLSTM, *LAYERS)}

                def turn_tile(s, src, ready, name):
                    use = claim(turn, to_act=True)
                    b = use.tile
                    pe.wait_ge(ready.sem, ready.next())
                    made[s][name] = [use]
                    for t in range(NT):
                        last = T.transpose(b[:, t * P:(t + 1) * P], src[:, t, :], ident[:, :])
                    last.then_inc(turn.to_act.sem, 1)

                def gate_products(s):
                    use = claim(turn, to_dve=True)
                    b = use.tile
                    wait_evacuated(made[s]["nT"])
                    made[s]["gates"] = [use]
                    T.matmul(b[0:H, 0:SEQ], wiT[:, :], nT[s][:, :], start=True, stop=True)
                    T.matmul(b[0:H, SEQ:2 * SEQ], wfT[:, :], nT[s][:, :], start=True, stop=True)\
                     .then_inc(turn.to_dve.sem, 1)

                def gates_turned(s):
                    use = claim(acc, to_dve=True)
                    b = use.tile
                    wait_evacuated(made[s]["gates"])
                    for t in range(NT):
                        last = T.transpose(b[:, t * H:(t + 1) * H], gi[:, t * P:(t + 1) * P], ident[0:H, 0:H])
                    last.then_inc(acc.to_dve.sem, 1)

                def mlstm_feature_heads(s, w, is_q):
                    if is_q:
                        made[s]["heads"] = []
                    for g2 in range(2):
                        use = claim(proj, to_act=is_q, to_dve=not is_q)
                        b = use.tile
                        made[s]["heads"].append(use)
                        for e in range(2):
                            p2 = 2 * g2 + e
                            last = T.matmul(b[:, e * SEQ:(e + 1) * SEQ], w[:, p2 * P:(p2 + 1) * P], nT[s][:, :],
                                            start=True, stop=True)
                        last.then_inc((proj.to_act if is_q else proj.to_dve).sem, 1)

                def mlstm_token_heads(s, w, gate):
                    if not gate:
                        made[s]["v"] = []
                    for t in range(NT):
                        use = claim(proj, to_act=True)
                        b = use.tile
                        made[s]["v"].append(use)
                        last = T.matmul(b[:, :], nT[s][:, t * P:(t + 1) * P], w[:, :], start=True, stop=not gate)
                        if gate:
                            last = T.matmul(b[:, :], ones_bf[:, :], bo3[:, :], start=False, stop=True)
                        last.then_inc(proj.to_act.sem, 1)

                def spread_gates(s, pairs):
                    if pairs[0] == 0:
                        pe.wait_ge(cum_ready.sem, cum_ready.next())
                        pe.wait_ge(mid_moved.sem, mid_moved.next())
                    for p2 in pairs:
                        use = claim(proj, to_act=True)
                        b = use.tile
                        for e in range(2):
                            last = T.matmul(b[:, e * SEQ:(e + 1) * SEQ], pick[:, 2 * p2 + e, :], cum3[:, :],
                                            start=True, stop=True)
                        last.then_inc(proj.to_act.sem, 1)

                def mlstm_scores0(s, pairs):
                    if pairs[0] == 0:
                        wait_evacuated(made[s]["heads"])
                        made[s]["weights"] = []
                    for p2 in pairs:
                        use = claim(score, to_dve=True)
                        b = use.tile
                        made[s]["weights"].append(use)
                        T.matmul(b[:, :].rearrange("p (e t) -> p e t", e=2), lin[s][:, p2, 0:P], bd[s][:, p2, :, :],
                                 start=True, stop=True).then_inc(score.to_dve.sem, 1)

                def mlstm_scores1(s):
                    for g2 in range(2):
                        use = claim(score, to_dve=True)
                        b = use.tile
                        made[s]["weights"].append(use)
                        for e in range(2):
                            p2 = 2 * g2 + e
                            last = T.matmul(b[:, e * SEQ:(e + 1) * SEQ].rearrange("p (e t) -> p e t", e=2),
                                            lin[s][:, p2, P:SEQ], bd[s][:, p2, :, P:SEQ], start=True, stop=True)
                        last.then_inc(score.to_dve.sem, 1)

                def mlstm_values(s, t):
                    if t == 0:
                        wait_evacuated(made[s]["v"])
                        wait_evacuated(made[s]["weights"][:PAIRS])
                    for g2 in range(2):
                        use = claim(acc, to_dve=True)
                        b = use.tile
                        if t == 1:
                            wait_evacuated(made[s]["weights"][PAIRS + g2:PAIRS + g2 + 1])
                        for j in range(4):
                            h = 4 * g2 + j
                            o = b[:, j * (D + 1):(j + 1) * (D + 1)]
                            last = T.matmul(o, work[:, h, t * P:(t + 1) * P], v[s][:, 0, h, :], start=True, stop=t == 0)
                            if t == 1:
                                last = T.matmul(o, work[:, h, SEQ:DW], v[s][:, 1, h, :], start=False, stop=True)
                        last.then_inc(acc.to_dve.sem, 1)

                def features_T(s, src, ready, t):
                    if t == 0:
                        made[s]["hT"] = []
                    use = claim(turn, to_act=True)
                    b = use.tile
                    made[s]["hT"].append(use)
                    if ready is None:
                        wait_evacuated(made[s]["outputs"][t:t + 1])
                    elif t == 0:
                        pe.wait_ge(ready.sem, ready.next())
                    for k in range(4):
                        last = T.transpose(b[:, k * P:(k + 1) * P], src[:, t, k * P:(k + 1) * P], ident[:, :])
                    last.then_inc(turn.to_act.sem, 1)

                def outputs_T(s, t):
                    if s == MLSTM:
                        features_T(s, hs, hn_ready, t)
                    else:
                        features_T(s, o_sb[s], None, t)

                def from_heads(s, w):
                    use = claim(acc, to_dve=True)
                    b = use.tile
                    for t in range(NT):
                        wait_evacuated(made[s]["hT"][t:t + 1])
                        for k in range(4):
                            last = T.matmul(b[:, t * C:(t + 1) * C], hT[s][:, k, t * P:(t + 1) * P], w[:, k, :],
                                            start=(k == 0), stop=(k == 3))
                    last.then_inc(acc.to_dve.sem, 1)

                def attention_projections(s, t):
                    l = s - 1
                    if t == 0:
                        wait_evacuated(made[s]["sT"])
                        made[s]["v"] = []
                    for w in range(3):
                        use = claim(proj, to_act=True, to_dve=w < 2)
                        b = use.tile
                        if w == 2:
                            made[s]["v"].append(use)
                        T.matmul(b[:, :], sT[s][:, t * P:(t + 1) * P], wqkv_sb[:, l, w * HD:(w + 1) * HD],
                                 start=True, stop=True).then_inc(proj.to_act.sem, 1)

                def rotated_T(s, t):
                    if t == 0:
                        wait_evacuated(made[s].get("hidden", []))
                        made[s]["heads"] = []
                    pe.wait_ge(rot_ready[s].sem, rot_ready[s].next())
                    for w in range(2):
                        use = claim(turn, to_act=w == 0, to_dve=w == 1)
                        b = use.tile
                        made[s]["heads"].append(use)
                        flat = rotr[t][:, w, :, :].rearrange("p h d -> p (h d)")
                        for k in range(4):
                            last = T.transpose(b[:, k * P:(k + 1) * P], flat[:, k * P:(k + 1) * P], ident[:, :])
                        last.then_inc((turn.to_act if w == 0 else turn.to_dve).sem, 1)

                def attention_scores0(s):
                    wait_evacuated(made[s]["heads"])
                    made[s]["prob"] = []
                    for g2 in range(2):
                        use = claim(score, to_act=True, to_dve=True)
                        b = use.tile
                        made[s]["prob"].append(use)
                        for e in range(2):
                            p2 = 2 * g2 + e
                            o = b[:, e * SEQ:(e + 1) * SEQ].rearrange("p (e t) -> p e t", e=2)
                            T.matmul(o, lin[s][:, p2, 0:P], bd[s][:, p2, :, 0:P], start=True, stop=False)
                            last = T.matmul(o, ident_bf[:, :], band0[:, :, :], start=False, stop=True)
                        last.then_inc(score.to_dve.sem, 1)

                def attention_scores1(s, pairs):
                    for p2 in pairs:
                        use = claim(score, to_act=True, to_dve=True)
                        b = use.tile
                        made[s]["prob"].append(use)
                        o = b[:, 0:2 * KEYS].rearrange("p (e t) -> p e t", e=2)
                        T.matmul(o, lin[s][:, p2, P:SEQ], bd[s][:, p2, :, WINDOW:SEQ], start=True, stop=False)
                        T.matmul(o, ident_bf[:, :], band1[:, :, :], start=False, stop=True).then_inc(score.to_dve.sem, 1)

                def probs_turned(s, ks):
                    if ks[0] == 0:
                        made[s]["pt"] = []
                    for k in ks:
                        blk, h0 = k // 2, 4 * (k % 2)
                        src = prob0[s] if blk == 0 else prob1[s][:, :, (blk - 1) * P:blk * P]
                        if blk == 0:
                            wait_evacuated(made[s]["prob"][k:k + 1])
                        if blk == 1:
                            wait_evacuated(made[s]["prob"][2 + h0 // 2:4 + h0 // 2])
                        use = claim(turn, to_act=k % 2 == 0, to_dve=k % 2 == 1)
                        b = use.tile
                        made[s]["pt"].append(use)
                        for j in range(4):
                            last = T.transpose(b[:, j * P:(j + 1) * P], src[:, h0 + j, :], ident[:, :])
                        last.then_inc((turn.to_act if k % 2 == 0 else turn.to_dve).sem, 1)

                def attention_values(s, t):
                    if t == 0:
                        wait_evacuated(made[s]["v"])
                        made[s]["outputs"] = []
                    use = claim(acc, to_dve=True)
                    b = use.tile
                    made[s]["outputs"].append(use)
                    wait_evacuated(made[s]["pt"][0:2] if t == 0 else made[s]["pt"][2:6])
                    for h in range(H):
                        o = b[:, h * D:(h + 1) * D]
                        last = T.matmul(o, pt[:, t, h, :], v[s][:, 0, h, 0:D], start=True, stop=t == 0)
                        if t == 1:
                            last = T.matmul(o, pt[:, 2, h, :], v[s][:, 1, h, 0:D], start=False, stop=True)
                    last.then_inc(acc.to_dve.sem, 1)

                def mlp_up(s, k):
                    l = s - 1
                    a, m = HB[k]
                    if k == 0:
                        wait_evacuated(made[s]["nT"])
                        made[s]["hidden"] = []
                    use = claim(proj, to_act=True, to_dve=True)
                    b = use.tile
                    made[s]["hidden"].append(use)
                    T.matmul(b[0:m, 0:SEQ], w1_sb[:, l, HID + a:HID + a + m], nT[s][:, :], start=True, stop=True)
                    T.matmul(b[0:m, SEQ:2 * SEQ], w1_sb[:, l, a:a + m], nT[s][:, :], start=True, stop=True)\
                     .then_inc(proj.to_act.sem, 1)

                def mlp_down(s):
                    l = s - 1
                    hd = hid[s]
                    use = claim(acc, to_dve=True)
                    b = use.tile
                    wait_evacuated(made[s]["hidden"])
                    for t in range(NT):
                        for k, (a, m) in enumerate(HB):
                            last = T.matmul(b[:, t * C:(t + 1) * C], hd[0:m, k, t * P:(t + 1) * P], w2_sb[0:m, l, k, :],
                                            start=(k == 0), stop=(k == 2))
                    last.then_inc(acc.to_dve.sem, 1)

                for r in RINGS:
                    for c in r.evacuated:
                        pe.sem_inc(c, 1)

                def settle_turn():
                    settle(pe, [*nrm_ready.values(), hn_ready, cum_ready, mid_moved, *rot_ready.values(), *res_ready.values()])
                    for r in RINGS:
                        for j in range(2):
                            if r.uses[j]:
                                pe.sem_inc(r.evacuated[j], -r.uses[j])
                                r.uses[j] = 0
                    for tiles in made.values():
                        for u in (u for uses in tiles.values() for u in uses):
                            u.value = 1

                walk(TENSOR, pe, {
                    "x_turn": lambda s: turn_tile(s, nrm[s], nrm_ready[s], "nT"),
                    "gates": gate_products,
                    "gate_bias": gates_turned,
                    "heads_q": lambda s: mlstm_feature_heads(s, wqT, True),
                    "heads_k": lambda s: mlstm_feature_heads(s, wkT, False),
                    "heads_v": lambda s: mlstm_token_heads(s, wvT, False),
                    "heads_o": lambda s: mlstm_token_heads(s, woT, True),
                    "decays0": lambda s: spread_gates(s, (0, 1)),
                    "decays1": lambda s: spread_gates(s, (2, 3)),
                    "weights0": lambda s: mlstm_scores0(s, (0, 1)),
                    "weights1": lambda s: mlstm_scores0(s, (2, 3)),
                    "weights2": mlstm_scores1,
                    "heads_out0": lambda s: mlstm_values(s, 0),
                    "heads_out1": lambda s: mlstm_values(s, 1),
                    "outputs0": lambda s: outputs_T(s, 0),
                    "outputs1": lambda s: outputs_T(s, 1),
                    "mlstm_project": lambda s: from_heads(s, w_out),
                    "layer_in": lambda s: turn_tile(s, xb[s], res_ready[s], "sT"),
                    "project0": lambda s: attention_projections(s, 0),
                    "project1": lambda s: attention_projections(s, 1),
                    "rotated0": lambda s: rotated_T(s, 0),
                    "rotated1": lambda s: rotated_T(s, 1),
                    "scores0": attention_scores0,
                    "scores1": lambda s: attention_scores1(s, (0, 1)),
                    "scores2": lambda s: attention_scores1(s, (2, 3)),
                    "probs0": lambda s: probs_turned(s, (0, 1)),
                    "probs1": lambda s: probs_turned(s, (2, 3)),
                    "probs2": lambda s: probs_turned(s, (4, 5)),
                    "values0": lambda s: attention_values(s, 0),
                    "values1": lambda s: attention_values(s, 1),
                    "residual": lambda s: from_heads(s, wo_sb[:, s - 1, :, :]),
                    "mlp_in": lambda s: turn_tile(s, nrm[s], nrm_ready[s], "nT"),
                    "mlp_up0": lambda s: mlp_up(s, 0),
                    "mlp_up1": lambda s: mlp_up(s, 1),
                    "mlp_up2": lambda s: mlp_up(s, 2),
                    "mlp_down": mlp_down,
                }, settle_turn)

            @block.sync
            def _(sp):
                def load_x(n):
                    sp.dma_start(x_in[:, :, :], xv[bass.ds(n, 1), :, :, :].rearrange("o p t c -> p (o t) c"))\
                      .then_inc(x_loaded.sem, 16)

                def shift(s):
                    sp.wait_ge(x1_ready[s].sem, x1_ready[s].next())
                    sp.dma_start(xs[s][1:P, :, D:C], x1[s][0:P - 1, :, D:C]).then_inc(shifted[s].sem, 16)
                    sp.dma_start(xs[s][0:1, 1, D:C], x1[s][P - 1:P, 0, D:C]).then_inc(shifted[s].sem, 16)

                def turn_of(parts, n, more):
                    if "back2" in parts:
                        shift(2)
                    if "back1" in parts:
                        shift(1)
                    if "back2" in parts:
                        sp.wait_ge(y_ready.sem, y_ready.next())
                        sp.dma_start(ov[bass.ds(n, 1), :, :, :].rearrange("o p t c -> p (o t) c"), y[:, :, :])\
                          .then_inc(y_stored.sem, 16)
                        sp.wait_ge(y_stored.sem, y_stored.next(16))
                        sp.sem_inc(y_free.sem, 1)
                    if more is not None:
                        sp.wait_ge(x_free.sem, x_free.next())
                        load_x(more)
                    settle(sp, [x_free, *x1_ready.values(), y_ready, y_stored])

                load_x(0)
                sp.sem_inc(y_free.sem, 1)
                for n, parts in enumerate(FIRST_TURNS):
                    turn_of(parts, None, n + 1)
                lead = len(FIRST_TURNS)
                if FULL > 1:
                    with sp.Fori(0, FULL - 1) as i:
                        turn_of(FULL_TURN, i, i + lead + 1)
                turn_of(FULL_TURN, FULL - 1, None)
                for n, parts in enumerate(LAST_TURNS):
                    turn_of(parts, FULL + n, None)

            @block.gpsimd
            def _(pool):
                g = nc.gpsimd

                def link(ins):
                    ins.then_inc(g_step.sem, 1)
                    pool.wait_ge(g_step.sem, g_step.next())

                def inverse_std(s):
                    pool.wait_ge(stats_ready[s].sem, stats_ready[s].next())
                    link(g.tensor_scalar(veps[s][:, :], mv[s][:, :, 1], EPS, None, ALU.add))
                    g.tensor_tensor(rstd[s][:, :], veps[s][:, :], minus_half[:, 0:NT], ALU.pow).then_inc(rstd_ready[s].sem, 1)

                def mask_decays(s, a):
                    pool.wait_ge(dec_ready.sem, dec_ready.next())
                    for t in range(NT):
                        part = work[:, a:a + 4, 0:P] if t == 0 else work[:, a:a + 4, SEQ:SEQ + P]
                        g.affine_select(out=part, in_=part, compare_op=ALU.is_ge, fill=0.0, base=0,
                                        pattern=[[0, 4], [1, P]], channel_multiplier=-1).then_inc(dec_masked.sem, 1)

                def rotate(s, t):
                    r = rotr[t]
                    for w in range(2):
                        pool.wait_ge(prod_ready[s].sem, prod_ready[s].next())
                        pr = prod[w]
                        for half in range(2):
                            a, b = half * 32, 32 - half * 32
                            g.tensor_tensor(r[:, w, :, a:a + 32], pr[:, 0, :, a:a + 32], pr[:, 1, :, b:b + 32],
                                            ALU.add).then_inc(g_step.sem, 1)
                            g_step.next()
                        pool.wait_ge(g_step.sem, g_step.seen)
                        pool.sem_inc(prod_free[w].sem, 1)

                def inverse_norms(s, t):
                    pool.wait_ge(ss_ready[s].sem, ss_ready[s].next())
                    link(g.tensor_tensor(rs[s][:, t, :, :].rearrange("p w h -> p (w h)"),
                                         ss[s][:, t, :, :].rearrange("p w h -> p (w h)"),
                                         minus_half[:, 0:2 * H], ALU.pow))

                def scale_k(s, t):
                    r = rotr[t]
                    g.tensor_tensor(r[:, 1, :, :], r[:, 1, :, :],
                                    rs[s][:, t, 1, :].unsqueeze(2).broadcast_to([P, H, D]), ALU.mult)\
                     .then_inc(rot_ready[s].sem, 1)

                def mlp_inputs(s):
                    l = s - 1
                    pool.wait_ge(x1_pool[s].sem, x1_pool[s].next())
                    g.tensor_copy(xs[s][:, :, 0:D], x1[s][:, :, 0:D]).then_inc(half_kept[s].sem, 1)
                    if s == 2:
                        pool.wait_ge(y_free.sem, y_free.next())
                    g.tensor_tensor(x1b[s][:, :, :], x1[s][:, :, :],
                                    b2_sb[:, l, :].unsqueeze(1).broadcast_to([P, NT, C]), ALU.add)\
                     .then_inc(x1b_ready[s].sem, 1)

                def rotate_tile(t):
                    def steps(s):
                        rotate(s, t)
                        inverse_norms(s, t)
                        scale_k(s, t)
                    return steps

                walk(GPSIMD, pool, {
                    "x_stats": inverse_std,
                    "decays0": lambda s: mask_decays(s, 0),
                    "decays1": lambda s: mask_decays(s, 4),
                    "heads_out1": inverse_std,
                    "mlstm_project": inverse_std,
                    "mlstm_residual": inverse_std,
                    "project0": rotate_tile(0),
                    "project1": rotate_tile(1),
                    "residual": mlp_inputs,
                    "shifted_stats": inverse_std,
                    "final_stats": inverse_std,
                }, lambda: settle(pool, [*stats_ready.values(), *prod_ready.values(), *ss_ready.values(), *x1_pool.values(),
                                  dec_ready, y_free, g_step]))

            @block.scalar
            def _(act):
                A = nc.scalar

                def bank(ring):
                    j = ring.act_banks.pop(0)
                    return ring.banks[j], ring.evacuated[j]

                def normal_T(s):
                    b, free = bank(turn)
                    act.wait_ge(turn.to_act.sem, turn.to_act.next())
                    ins = A.activation(nT[s][:, :], b[:, 0:SEQ], ACT.Copy)
                    ins.then_inc(free, 1)

                def move_middle(s):
                    act.wait_ge(cum_act.sem, cum_act.next())
                    A.activation(cum3[32:32 + H, :], mid_bf[:, :], ACT.Copy).then_inc(mid_moved.sem, 1)

                def mlstm_q(s):
                    for g2 in range(2):
                        b, free = bank(proj)
                        act.wait_ge(proj.to_act.sem, proj.to_act.next())
                        src = b[:, :].rearrange("p (a t) -> p a t", a=2)
                        for e in range(2):
                            ins = A.activation(bd[s][e * D:(e + 1) * D, 2 * g2:2 * g2 + 2, e, :],
                                               src[e * D:(e + 1) * D, :, :], ACT.Copy)
                        ins.then_inc(free, 1)

                def mlstm_v(s):
                    for t in range(NT):
                        b, free = bank(proj)
                        act.wait_ge(proj.to_act.sem, proj.to_act.next())
                        ins = A.activation(v[s][:, t, :, 0:D], b[:, :].rearrange("p (h d) -> p h d", h=H), ACT.Copy)
                        ins.then_inc(free, 1)

                def mlstm_gate(s):
                    for t in range(NT):
                        b, free = bank(proj)
                        act.wait_ge(proj.to_act.sem, proj.to_act.next())
                        ins = A.activation(th[:, t, :], b[:, :], ACT.Tanh, scale=0.5)
                        ins.then_inc(free, 1)

                def decays(s, pairs):
                    if pairs[0] == 0:
                        act.wait_ge(bias_ready.sem, bias_ready.next())
                    for p2 in pairs:
                        b, free = bank(proj)
                        act.wait_ge(proj.to_act.sem, proj.to_act.next())
                        src = b[:, :].rearrange("p (e t) -> p e t", e=2)
                        for e in range(2):
                            h = 2 * p2 + e
                            A.activation(work[:, h, 0:SEQ], src[:, e, :], ACT.Exp, bias=src_bias[:, 0, h:h + 1])
                            ins = A.activation(work[:, h, SEQ:DW], src[:, e, P:SEQ], ACT.Exp,
                                               bias=src_bias[:, 1, h:h + 1])
                        if p2 < pairs[-1]:
                            ins.then_inc(free, 1)
                    ins.then_inc(a_step.sem, 1)
                    act.wait_ge(a_step.sem, a_step.next())
                    act.sem_inc(free, 1)
                    act.sem_inc(dec_ready.sem, 1)

                def outputs_T(s, t):
                    b, free = bank(turn)
                    act.wait_ge(turn.to_act.sem, turn.to_act.next())
                    ins = A.activation(hT[s][:, :, t * P:(t + 1) * P], b[:, :].rearrange("p (b t) -> p b t", b=4), ACT.Copy)
                    ins.then_inc(free, 1)

                def shifted_T(s):
                    b, free = bank(turn)
                    act.wait_ge(turn.to_act.sem, turn.to_act.next())
                    A.activation(sT[s][0:D, :], b[0:D, 0:SEQ], ACT.Copy)
                    ins = A.activation(sT[s][D:C, 1:SEQ], b[D:C, 0:SEQ - 1], ACT.Copy)
                    ins.then_inc(free, 1)

                def squares(s, t):
                    sq = sqr[t]
                    for w in range(2):
                        b, free = bank(proj)
                        act.wait_ge(proj.to_act.sem, proj.to_act.next())
                        A.activation(sq[:, w, :, :], b[:, :].rearrange("p (h d) -> p h d", h=H), ACT.Square)\
                         .then_inc(sq_ready[s].sem, 1)
                    b, free = bank(proj)
                    act.wait_ge(proj.to_act.sem, proj.to_act.next())
                    ins = A.activation(v[s][:, t, :, 0:D], b[:, :].rearrange("p (h d) -> p h d", h=H), ACT.Copy)
                    ins.then_inc(free, 1)

                def q_T(s, t):
                    b, free = bank(turn)
                    act.wait_ge(turn.to_act.sem, turn.to_act.next())
                    ins = A.activation(lin[s][:, :, t * P:(t + 1) * P], b[:, :].rearrange("p (b t) -> p b t", b=4), ACT.Copy)
                    ins.then_inc(free, 1)

                def softmax0(s):
                    for g2 in range(2):
                        b, free = bank(score)
                        act.wait_ge(max_ready[s].sem, max_ready[s].next())
                        for j in range(4):
                            h = 4 * g2 + j
                            ins = A.activation(prob0[s][:, h, :], b[:, j * P:(j + 1) * P], ACT.Exp,
                                               scale=rs[s][:, 0, 0, h:h + 1], bias=nbias[s][:, 0, h:h + 1],
                                               accum_out=rsum[s][:, 0, h:h + 1])
                        ins.then_inc(free, 1)

                def softmax1(s, pairs):
                    for p2 in pairs:
                        b, free = bank(score)
                        act.wait_ge(max_ready[s].sem, max_ready[s].next())
                        for e in range(2):
                            h = 2 * p2 + e
                            ins = A.activation(prob1[s][:, h, WINDOW:SEQ], b[:, e * KEYS:(e + 1) * KEYS], ACT.Exp,
                                               scale=rs[s][:, 1, 0, h:h + 1], bias=nbias[s][:, 1, h:h + 1],
                                               accum_out=rsum[s][:, 1, h:h + 1])
                        ins.then_inc(free, 1)

                def probs_T(s, ks):
                    for k in ks:
                        if k % 2 == 0:
                            b, free = bank(turn)
                            act.wait_ge(turn.to_act.sem, turn.to_act.next())
                            ins = A.activation(pt[:, k // 2, 4 * (k % 2):4 * (k % 2) + 4, :],
                                               b[:, :].rearrange("p (h t) -> p h t", h=4), ACT.Copy)
                            ins.then_inc(free, 1)

                def gelu(s, k):
                    m = HB[k][1]
                    b, free = bank(proj)
                    act.wait_ge(proj.to_act.sem, proj.to_act.next())
                    A.activation(gel[s][0:m, k, :], b[0:m, 0:SEQ], ACT.Gelu,
                                 bias=b1_c[0:m, s - 1, 1, k:k + 1]).then_inc(gelu_ready[s].sem, 1)

                walk(SCALAR, act, {
                    "x_turn": normal_T,
                    "gates": move_middle,
                    "heads_q": mlstm_q,
                    "heads_v": mlstm_v,
                    "heads_o": mlstm_gate,
                    "decays0": lambda s: decays(s, (0, 1)),
                    "decays1": lambda s: decays(s, (2, 3)),
                    "outputs0": lambda s: outputs_T(s, 0),
                    "outputs1": lambda s: outputs_T(s, 1),
                    "layer_in": shifted_T,
                    "project0": lambda s: squares(s, 0),
                    "project1": lambda s: squares(s, 1),
                    "rotated0": lambda s: q_T(s, 0),
                    "rotated1": lambda s: q_T(s, 1),
                    "scores0": softmax0,
                    "scores1": lambda s: softmax1(s, (0, 1)),
                    "scores2": lambda s: softmax1(s, (2, 3)),
                    "probs0": lambda s: probs_T(s, (0, 1)),
                    "probs1": lambda s: probs_T(s, (2, 3)),
                    "probs2": lambda s: probs_T(s, (4, 5)),
                    "mlp_in": normal_T,
                    "mlp_up0": lambda s: gelu(s, 0),
                    "mlp_up1": lambda s: gelu(s, 1),
                    "mlp_up2": lambda s: gelu(s, 2),
                }, lambda: settle(act, [r.to_act for r in RINGS] + [cum_act, bias_ready, *max_ready.values(), a_step]))

            @block.vector
            def _(dve):
                V = nc.vector

                def link(ins):
                    ins.then_inc(v_step.sem, 1)
                    dve.wait_ge(v_step.sem, v_step.next())

                def bank(ring):
                    j = ring.dve_banks.pop(0)
                    return ring.banks[j], ring.evacuated[j]

                def stats_of(s, src):
                    for t in range(NT):
                        ins = V.bn_stats(stats[s][:, t, :], src[:, t, :])
                        ins.then_inc(v_step.sem, 1)
                        v_step.next()
                    dve.wait_ge(v_step.sem, v_step.seen)
                    for t in range(NT):
                        ins = V.bn_aggr(mv[s][:, t, :], stats[s][:, t, :])
                        if t < NT - 1:
                            ins.then_inc(v_step.sem, 1)
                            v_step.next()
                    link(ins)
                    dve.sem_inc(stats_ready[s].sem, 1)

                def normalise(s, dst, src, ready, link_it=False):
                    dve.wait_ge(rstd_ready[s].sem, rstd_ready[s].next())
                    for t in range(NT):
                        ins = V.tensor_scalar(dst[:, t, :], src[:, t, :], mv[s][:, t, 0:1], rstd[s][:, t:t + 1],
                                              ALU.subtract, ALU.mult)
                        if ready is not None and t == NT - 1:
                            ins.then_inc(ready.sem, 1)
                        if link_it:
                            ins.then_inc(v_step.sem, 1)
                            v_step.next()
                    if link_it:
                        dve.wait_ge(v_step.sem, v_step.seen)

                def gates(s):
                    b, free = bank(turn)
                    dve.wait_ge(turn.to_dve.sem, turn.to_dve.next())
                    link(V.tensor_tensor_scan(cum, bf_c[:, 0:1].broadcast_to([H, SEQ]), b[0:H, SEQ:2 * SEQ],
                                              0.0, ALU.add, ALU.add))
                    ins = V.scalar_tensor_tensor(gi, b[0:H, 0:SEQ], bi_c[:, 0:1], cum,
                                                 ALU.add, ALU.subtract)
                    ins.then_inc(free, 1)
                    link(V.tensor_copy(cum3[0:H, :], cum))
                    link(V.tensor_tensor(rest, cum, cum3[0:H, :], ALU.subtract))
                    link(V.tensor_copy(mid_bf[:, :], rest))
                    dve.sem_inc(cum_act.sem, 1)
                    V.tensor_tensor(cum3[64:64 + H, :], rest, mid_bf[:, :], ALU.subtract)\
                     .then_inc(cum_ready.sem, 1)

                def source_bias(s):
                    b, free = bank(acc)
                    dve.wait_ge(acc.to_dve.sem, acc.to_dve.next())
                    link(V.tensor_copy(src_bias[:, :, :], b[:, 0:NT * H].rearrange("p (t h) -> p t h", t=NT)))
                    dve.sem_inc(free, 1)
                    dve.sem_inc(bias_ready.sem, 1)

                def mlstm_k(s):
                    for g2 in range(2):
                        b, free = bank(proj)
                        dve.wait_ge(proj.to_dve.sem, proj.to_dve.next())
                        ins = V.tensor_scalar(lin[s][:, 2 * g2:2 * g2 + 2, :], b[:, :].rearrange("p (a t) -> p a t", a=2),
                                              D ** -0.5, None, ALU.mult)
                        ins.then_inc(free, 1)

                def weigh0(s, pairs):
                    dve.wait_ge(dec_masked.sem, dec_masked.next(NT))
                    for p2 in pairs:
                        b, free = bank(score)
                        dve.wait_ge(score.to_dve.sem, score.to_dve.next())
                        part = work[:, 2 * p2:2 * p2 + 2, 0:SEQ]
                        V.tensor_tensor(part, b[:, :].rearrange("p (e t) -> p e t", e=2), part, ALU.mult)\
                         .then_inc(free, 1)

                def weigh1(s):
                    for g2 in range(2):
                        b, free = bank(score)
                        dve.wait_ge(score.to_dve.sem, score.to_dve.next())
                        part = work[:, 4 * g2:4 * g2 + 4, SEQ:DW]
                        V.tensor_tensor(part, b[:, :].rearrange("p (e t) -> p e t", e=4), part, ALU.mult)\
                         .then_inc(free, 1)

                def head_outputs(s, t):
                    for g2 in range(2):
                        b, free = bank(acc)
                        dve.wait_ge(acc.to_dve.sem, acc.to_dve.next())
                        src = b[:, 0:4 * (D + 1)].rearrange("p (h d) -> p h d", h=4)
                        rd = rden[:, t, 4 * g2:4 * g2 + 4]
                        o = hs[:, t, 256 * g2:256 * g2 + 256].rearrange("p (h d) -> p h d", h=4)
                        link(V.tensor_scalar(rd, src[:, :, D], -1.0, 1.0, ALU.mult, ALU.max))
                        link(V.tensor_tensor(rd, src[:, :, D], rd, ALU.max))
                        link(V.reciprocal(rd, rd))
                        ins = V.scalar_tensor_tensor(o, th[:, t, 256 * g2:256 * g2 + 256].rearrange("p (h d) -> p h d", h=4),
                                                     1.0, src[:, :, 0:D], ALU.add, ALU.mult)
                        link(ins)
                        dve.sem_inc(free, 1)
                        link(V.scalar_tensor_tensor(o, o, 0.5, rd.unsqueeze(2).broadcast_to([P, 4, D]), ALU.mult, ALU.mult))

                def project_out(s):
                    b, free = bank(acc)
                    dve.wait_ge(acc.to_dve.sem, acc.to_dve.next())
                    ins = V.tensor_tensor(x1[s][:, :, :], b[:, 0:SEQ].rearrange("p (t c) -> p t c", t=NT),
                                          out_bias[:, :].unsqueeze(1).broadcast_to([P, NT, C]), ALU.add)
                    link(ins)
                    dve.sem_inc(free, 1)
                    stats_of(s, x1[s])

                def mlstm_residual(s):
                    normalise(s, x1[s], x1[s], None, link_it=True)
                    ins = V.tensor_tensor(passed[0][:, :, :], x1[s][:, :, :], x_in[:, :, :], ALU.add)
                    link(ins)
                    dve.sem_inc(x_free.sem, 1)
                    stats_of(s, passed[0])

                def rotary_products(s, t):
                    l = s - 1
                    def announce(w, step, free):
                        dve.wait_ge(v_step.sem, step)
                        dve.sem_inc(prod_ready[s].sem, 1)
                        dve.sem_inc(free, 1)

                    made = []
                    for w in range(2):
                        b, free = bank(proj)
                        dve.wait_ge(sq_ready[s].sem, sq_ready[s].next())
                        dve.wait_ge(prod_free[w].sem, prod_free[w].next())
                        src = b[:, :].rearrange("p (h d) -> p h d", h=H).unsqueeze(1).broadcast_to([P, 2, H, D])
                        tab = rot[:, l, t, w, :, :].unsqueeze(2).broadcast_to([P, 2, H, D])
                        V.tensor_tensor(prod[w][:, :, :, :], src, tab, ALU.mult).then_inc(v_step.sem, 1)
                        made.append((w, v_step.next(), free))
                        if w:
                            announce(*made[0])
                    V.tensor_reduce(ss[s][:, t, :, :], sqr[t][:, :, :, :], axis=AXX, op=ALU.add)\
                     .then_inc(v_step.sem, 1)
                    reduced = v_step.next()
                    announce(*made[1])
                    dve.wait_ge(v_step.sem, reduced)
                    V.tensor_scalar(ss[s][:, t, :, :], ss[s][:, t, :, :], 1e-24, None, ALU.max)\
                     .then_inc(ss_ready[s].sem, 1)

                def k_T(s, t):
                    b, free = bank(turn)
                    dve.wait_ge(turn.to_dve.sem, turn.to_dve.next())
                    src = b[:, :].rearrange("p (b t) -> p b t", b=4)
                    for e in range(2):
                        ins = V.tensor_copy(bd[s][e * D:(e + 1) * D, :, e, t * P:(t + 1) * P], src[e * D:(e + 1) * D, :, :])
                    ins.then_inc(free, 1)

                def maxima(s, t, h, n, view):
                    dve.wait_ge(score.to_dve.sem, score.to_dve.next())
                    link(V.tensor_reduce(smax[s][:, t, h:h + n], view, axis=AXX, op=ALU.max))
                    V.scalar_tensor_tensor(nbias[s][:, t, h:h + n], smax[s][:, t, h:h + n], -1.0,
                                           rs[s][:, t, 0, h:h + n], ALU.mult, ALU.mult).then_inc(max_ready[s].sem, 1)

                def score_max0(s):
                    for g2 in range(2):
                        b, _ = bank(score)
                        maxima(s, 0, 4 * g2, 4, b[:, :].rearrange("p (h t) -> p h t", h=4))

                def score_max1(s, pairs):
                    for p2 in pairs:
                        b, _ = bank(score)
                        maxima(s, 1, 2 * p2, 2, b[:, 0:2 * KEYS].rearrange("p (h t) -> p h t", h=2))

                def probs_T(s, ks):
                    for k in ks:
                        if k % 2:
                            b, free = bank(turn)
                            dve.wait_ge(turn.to_dve.sem, turn.to_dve.next())
                            ins = V.tensor_copy(pt[:, k // 2, 4 * (k % 2):4 * (k % 2) + 4, :],
                                                b[:, :].rearrange("p (h t) -> p h t", h=4))
                            ins.then_inc(free, 1)

                def attention_out(s, t):
                    b, free = bank(acc)
                    dve.wait_ge(acc.to_dve.sem, acc.to_dve.next())
                    link(V.reciprocal(rinv[s][:, t, :], rsum[s][:, t, :]))
                    ins = V.tensor_tensor(o_sb[s][:, t, :].rearrange("p (h d) -> p h d", h=H),
                                          b[:, :].rearrange("p (h d) -> p h d", h=H),
                                          rinv[s][:, t, :].unsqueeze(2).broadcast_to([P, H, D]), ALU.mult)
                    ins.then_inc(free, 1)

                def attention_residual(s):
                    b, free = bank(acc)
                    dve.wait_ge(acc.to_dve.sem, acc.to_dve.next())
                    ins = V.tensor_tensor(x1[s][:, :, :], b[:, 0:SEQ].rearrange("p (t c) -> p t c", t=NT),
                                          xr[s][:, :, :], ALU.add)
                    link(ins)
                    dve.sem_inc(x1_ready[s].sem, 1)
                    dve.sem_inc(x1_pool[s].sem, 1)
                    dve.sem_inc(free, 1)

                def stats_of_shifted(s):
                    dve.wait_ge(half_kept[s].sem, half_kept[s].next())
                    dve.wait_ge(shifted[s].sem, shifted[s].next(32))
                    stats_of(s, xs[s])

                def hidden(s, k):
                    m = HB[k][1]
                    b, free = bank(proj)
                    dve.wait_ge(gelu_ready[s].sem, gelu_ready[s].next())
                    V.scalar_tensor_tensor(hid[s][0:m, k, :], b[0:m, SEQ:2 * SEQ], b1_c[0:m, s - 1, 0, k:k + 1],
                                           gel[s][0:m, k, :], ALU.add, ALU.mult).then_inc(free, 1)

                def mlp_residual(s):
                    b, free = bank(acc)
                    dve.wait_ge(acc.to_dve.sem, acc.to_dve.next())
                    dve.wait_ge(x1b_ready[s].sem, x1b_ready[s].next())
                    dst = xb[2] if s == 1 else x1[2]
                    link(V.tensor_tensor(dst[:, :, :], b[:, 0:SEQ].rearrange("p (t c) -> p t c", t=NT),
                                         x1b[s][:, :, :], ALU.add))
                    dve.sem_inc(free, 1)
                    if s == 1:
                        dve.sem_inc(res_ready[2].sem, 1)

                def pass_on(n):
                    link(V.tensor_copy(passed[n][:, :, :], passed[n - 1][:, :, :]))

                def keep(s):
                    link(V.tensor_copy(xr[s][:, :, :], xb[s][:, :, :]))

                def x_stats(s):
                    dve.wait_ge(x_loaded.sem, x_loaded.next(16))
                    stats_of(s, x_in)

                def last_head_outputs(s):
                    head_outputs(s, 1)
                    stats_of(s, hs)

                def final(s):
                    normalise(s, x1[s], x1[s], None, link_it=True)
                    link(V.tensor_tensor(y[:, :, :], x1[s][:, :, :], passed[-1][:, :, :], ALU.add))
                    dve.sem_inc(y_ready.sem, 1)

                for c in prod_free:
                    dve.sem_inc(c.sem, 1)
                walk(VECTOR, dve, {
                    "x_stats": x_stats,
                    "x_norm": lambda s: normalise(s, nrm[s], x_in, nrm_ready[s]),
                    "gates": gates,
                    "gate_bias": source_bias,
                    "heads_k": mlstm_k,
                    "weights0": lambda s: weigh0(s, (0, 1)),
                    "weights1": lambda s: weigh0(s, (2, 3)),
                    "weights2": weigh1,
                    "heads_out0": lambda s: head_outputs(s, 0),
                    "heads_out1": last_head_outputs,
                    "outputs_norm": lambda s: normalise(s, hs, hs, hn_ready),
                    "mlstm_project": project_out,
                    "mlstm_residual": mlstm_residual,
                    "mlstm_out": lambda s: normalise(s, xb[1], passed[0], res_ready[1]),
                    "pass_front": lambda s: pass_on(2 * s - 1),
                    "pass_back": lambda s: pass_on(2 * s),
                    "keep": keep,
                    "project0": lambda s: rotary_products(s, 0),
                    "project1": lambda s: rotary_products(s, 1),
                    "rotated0": lambda s: k_T(s, 0),
                    "rotated1": lambda s: k_T(s, 1),
                    "scores0": score_max0,
                    "scores1": lambda s: score_max1(s, (0, 1)),
                    "scores2": lambda s: score_max1(s, (2, 3)),
                    "probs0": lambda s: probs_T(s, (0, 1)),
                    "probs1": lambda s: probs_T(s, (2, 3)),
                    "probs2": lambda s: probs_T(s, (4, 5)),
                    "values0": lambda s: attention_out(s, 0),
                    "values1": lambda s: attention_out(s, 1),
                    "residual": attention_residual,
                    "shifted_stats": stats_of_shifted,
                    "shifted_norm": lambda s: normalise(s, nrm[s], xs[s], nrm_ready[s]),
                    "mlp_up0": lambda s: hidden(s, 0),
                    "mlp_up1": lambda s: hidden(s, 1),
                    "mlp_up2": lambda s: hidden(s, 2),
                    "mlp_down": mlp_residual,
                    "final_stats": lambda s: stats_of(s, x1[s]),
                    "final": final,
                }, lambda: settle(dve, [r.to_dve for r in RINGS] + [x_loaded] + [*shifted.values()] + prod_free +
                                  [*rstd_ready.values(), *sq_ready.values(), *half_kept.values(), *gelu_ready.values(),
                                   *x1b_ready.values(), v_step, dec_masked]))


_INS = ["L0_attn_x", "L0_attn_Wq", "L0_attn_Wk", "L0_attn_Wv", "L0_attn_Wi", "L0_attn_bi", "L0_attn_Wf", "L0_attn_bf",
        "L0_attn_Wo", "L0_attn_bo", "L0_attn_W_out", "L0_attn_ln_g", "L0_attn_ln_b", "L0_ffn_wqkv", "L0_ffn_q_scale",
        "L0_ffn_k_scale", "L0_ffn_wo", "L0_ffn_ln_g", "L0_ffn_ln_b", "L0_ffn_w1", "L0_ffn_b1", "L0_ffn_w2", "L0_ffn_b2"]


def rotary_factors():
    import numpy as np

    half = np.arange(0, D, 2, dtype=np.float32)
    inv_freq = (np.float32(1.0) / np.float32(10000.0) ** (half / np.float32(D))).astype(np.float32)
    t = np.arange(SEQ, dtype=np.float32)
    freqs = np.concatenate([t[:, None] * inv_freq[None, :]] * 2, axis=-1)
    base = ((half + np.float32(0.4 * D)) / np.float32(1.4 * D)).astype(np.float32)
    power = ((t - SEQ // 2) / np.float32(WINDOW // 2)).astype(np.float32)
    scale = np.concatenate([base[None, :].astype(np.float64) ** power[:, None]] * 2, axis=-1)
    cos, sin = np.cos(freqs.astype(np.float64)), np.sin(freqs.astype(np.float64))
    sign = np.concatenate([np.ones(D // 2), -np.ones(D // 2)])
    q = np.stack([cos * scale, sin * scale * sign], axis=1) * 8.0
    k = np.stack([cos / scale, sin / scale * sign], axis=1)
    return np.ascontiguousarray(np.stack([q, k], axis=1).reshape(SEQ, 4 * D).astype(np.float32))


def kernel(**inputs):
    import numpy as _np
    import concourse.bacc as _bacc
    from concourse import mybir as _mybir
    from concourse.bass_utils import run_bass_kernel_spmd as _run

    nc = _bacc.Bacc("TRN2", target_bir_lowering=False, num_devices=1)
    arrays, args = {}, []
    for name in _INS + ["rotary"]:
        a = rotary_factors() if name == "rotary" else _np.ascontiguousarray(inputs[name])
        arrays[f"in_{name}_dram"] = a
        args.append(nc.dram_tensor(f"in_{name}_dram", a.shape, _mybir.dt.from_np(a.dtype), kind="ExternalInput").ap())
    shape = arrays["in_L0_attn_x_dram"].shape
    args.append(nc.dram_tensor("out_dram", shape, _mybir.dt.float32, kind="ExternalOutput").ap())
    block_kernel(nc, *args)
    r = _run(nc, [arrays], core_ids=[0])
    return r.results[0]["out_dram"]
```

```python
import concourse.bass as bass
from concourse import mybir
from contextlib import ExitStack


F32 = mybir.dt.float32
BF16 = mybir.dt.bfloat16
ALU = mybir.AluOpType
ACT = mybir.ActivationFunctionType
AXX = mybir.AxisListType.X

P = 128
C = 128
SEQ = 256
NT = SEQ // P
H = 8
D = 64
HD = H * D
PAIRS = H // 2
WINDOW = 64
DEPTH = 2
HID = 341
HB = [(0, 128), (128, 128), (256, 85)]
DW = SEQ + P
KEYS = P + WINDOW
MASKED = -1.0e30
EPS = 1e-5
FG = 32
MLSTM = 0
LAYERS = (1, 2)

PARTS = {
    "mlstm": (MLSTM, {
        "x_stats":        (None, None,    6,    0),
        "x_norm":         (None, None,    8, None),
        "x_turn":         (   8,    6, None, None),
        "gates":          (  10,    8,   11, None),
        "heads_q":        (  14,   10, None, None),
        "gate_bias":      (  16, None,   18, None),
        "heads_k":        (  15, None,   16, None),
        "heads_v":        (  30,   23, None, None),
        "heads_o":        (  36,   28, None, None),
        "decays0":        (  32,   25, None,    9),
        "decays1":        (  39,   30, None,   10),
        "weights0":       (  42, None,   34, None),
        "weights1":       (  45, None,   37, None),
        "weights2":       (  50, None,   39, None),
        "heads_out0":     (  48, None,   43, None),
        "heads_out1":     (  54, None,   46, None),
        "heads_out2":     (  57, None,   49, None),
        "heads_out3":     (  58, None,   51,   15),
        "outputs_norm":   (None, None,   54, None),
        "outputs0":       (  67,   49, None, None),
        "outputs1":       (  68,   50, None, None),
        "mlstm_project":  (  70, None,   60,   17),
        "mlstm_residual": (None, None,   64,   18),
        "mlstm_out":      (None, None,   67, None),
    }),
    "front1": (1, {
        "pass_front":     (None, None,   21, None),
        "layer_in":       (  21,   17, None, None),
        "query0":         (  37,   29,   31,   11),
        "key0":           (  41,   31,   33,   12),
        "value0":         (  43,   32, None, None),
        "query1":         (  44,   34,   36,   13),
        "key1":           (  47,   36,   38,   14),
        "value1":         (  51,   38, None, None),
        "keep":           (None, None,   57, None),
        "rotated0":       (  60,   43, None, None),
        "rotated1":       (  62,   47, None, None),
        "scores0":        (  66,   51,   58, None),
        "scores1":        (  69,   52,   59, None),
        "scores2":        (  71,   53,   62, None),
        "scores3":        (  72,   54,   63, None),
        "scores4":        (  73,   55,   65, None),
        "scores5":        (  74,   56,   66, None),
    }),
    "back1": (1, {
        "pass_back":      (None, None,    5, None),
        "probs0":         (   6,    4,   10, None),
        "probs1":         (  13,   11,   14, None),
        "probs2":         (  17,   12,   19, None),
        "values0":        (  22, None,   23, None),
        "values1":        (  25, None,   26, None),
        "outputs0":       (  27,   20, None, None),
        "outputs1":       (  29,   22, None, None),
        "residual":       (  33, None,   29,    7),
        "shifted_stats":  (None, None,   30,    8),
        "shifted_norm":   (None, None,   32, None),
        "mlp_in":         (  46,   35, None, None),
        "mlp_up0":        (  49,   37,   40, None),
        "mlp_up1":        (  53,   39,   45, None),
        "mlp_up2":        (  55,   40,   47, None),
        "mlp_down":       (  64, None,   56, None),
    }),
    "front2": (2, {
        "pass_front":     (None, None,    4, None),
        "layer_in":       (   4,    3, None, None),
        "query0":         (   9,    9,   13,    3),
        "key0":           (  18,   13,   20,    4),
        "value0":         (  28,   21, None, None),
        "query1":         (  23,   16,   24,    5),
        "key1":           (  24,   18,   25,    6),
        "value1":         (  34,   26, None, None),
        "keep":           (None, None,   35, None),
        "rotated0":       (  35,   27, None, None),
        "rotated1":       (  40,   33, None, None),
        "scores0":        (  52,   41,   44, None),
        "scores1":        (  56,   42,   48, None),
        "scores2":        (  59,   44,   50, None),
        "scores3":        (  61,   45,   52, None),
        "scores4":        (  63,   46,   53, None),
        "scores5":        (  65,   48,   55, None),
    }),
    "back2": (2, {
        "pass_back":      (None, None,    0, None),
        "probs0":         (   0,    0,    1, None),
        "probs1":         (   1,    1,    2, None),
        "probs2":         (   2,    2,    3, None),
        "values0":        (   3, None,    7, None),
        "values1":        (   5, None,    9, None),
        "outputs0":       (   7,    5, None, None),
        "outputs1":       (  11,    7, None, None),
        "residual":       (  12, None,   12,    1),
        "shifted_stats":  (None, None,   15,    2),
        "shifted_norm":   (None, None,   17, None),
        "mlp_in":         (  19,   14, None, None),
        "mlp_up0":        (  20,   15,   22, None),
        "mlp_up1":        (  26,   19,   27, None),
        "mlp_up2":        (  31,   24,   28, None),
        "mlp_down":       (  38, None,   41, None),
        "final_stats":    (None, None,   42,   16),
        "final":          (None, None,   61, None),
    }),
}
TENSOR, SCALAR, VECTOR, GPSIMD = range(4)


def schedule(parts, engine):
    order = []
    for part in parts:
        lane, stages = PARTS[part]
        order += [(places[engine], lane, name) for name, places in stages.items() if places[engine] is not None]
    return [(lane, name) for _, lane, name in sorted(order)]


FULL_TURN = tuple(PARTS)
FIRST_TURNS = [FULL_TURN[:n] for n in range(1, len(PARTS))]
LAST_TURNS = [FULL_TURN[n:] for n in range(1, len(PARTS))]


class Count:

    def __init__(self, sem):
        self.sem, self.seen = sem, 0

    def next(self, n=1):
        self.seen += n
        return self.seen


def settle(engine, counts):
    for c in counts:
        if c.seen:
            engine.sem_inc(c.sem, -c.seen)
            c.seen = 0


def block_kernel(nc, x, Wq, Wk, Wv, Wi, bi, Wf, bf, Wo, bo, W_out, lng, lnb,
                 wqkv, qsc, ksc, wo, lg, lb, w1, b1, w2, b2, rotary, out):
    ctx = ExitStack()
    with ctx:
        def sb(name, shape, dt=F32):
            return ctx.enter_context(nc.sbuf_tensor(name, shape, dt))

        def sem(name):
            return ctx.enter_context(nc.semaphore(name))

        ident = sb("ident", [P, P])
        ident_bf = sb("ident_bf", [P, P], BF16)
        band0 = sb("band0", [P, 2, P], BF16)
        band1 = sb("band1", [P, 2, KEYS], BF16)
        pick = sb("pick", [P, H, P], BF16)
        ones_bf = sb("ones_bf", [P, P], BF16)
        minus_half = sb("minus_half", [P, 4 * H])
        wqT = sb("wqT", [C, HD])
        wkT = sb("wkT", [C, HD])
        wvT = sb("wvT", [C, HD])
        woT = sb("woT", [C, HD])
        gate_w = sb("gate_w", [C, FG + H])
        bi_c = sb("bi_c", [H, 1])
        bf_c = sb("bf_c", [FG + H, 1])
        bo3 = sb("bo3", [P, HD], BF16)
        w_out = sb("w_out", [P, 4, C])
        out_bias = sb("out_bias", [P, C])
        wqkv_sb = sb("wqkv_sb", [C, DEPTH, 3 * HD])
        wo_sb = sb("wo_sb", [P, DEPTH, 4, C])
        w1_sb = sb("w1_sb", [C, DEPTH, 2 * HID])
        w2_sb = sb("w2_sb", [P, DEPTH, 3, C])
        b1_c = sb("b1_c", [P, DEPTH, 2, 3])
        b2_sb = sb("b2_sb", [P, DEPTH, C])
        rot = sb("rot", [P, DEPTH, NT, 2, 2, D])

        def lanes(name, shape, dt=F32, of=(MLSTM, *LAYERS)):
            return {s: sb(f"{name}{s}", shape, dt) for s in of}

        x1 = lanes("x1", [P, NT, C])
        nrm = lanes("nrm", [P, NT, C])
        passed = [sb(f"passed{n}", [P, NT, C]) for n in range(len(PARTS))]
        stats = lanes("stats", [P, NT, 6])
        mv = lanes("mv", [P, NT, 2])
        veps = lanes("veps", [P, NT])
        rstd = lanes("rstd", [P, NT])
        nT = lanes("nT", [C, SEQ])
        lin = lanes("lin", [P, PAIRS, SEQ])
        bd = lanes("bd", [P, PAIRS, 2, SEQ])
        v = lanes("v", [P, NT, H, D + 1])
        x_in = sb("x_in", [P, NT, C])
        work = sb("work", [P, H, DW])
        th = sb("th", [P, NT, HD])
        hs = sb("hs", [P, NT, HD])
        cum = hs[0:H, 0, 0:SEQ]
        gi = hs[0:H, 0, SEQ:2 * SEQ]
        rest = hs[0:H, 1, 0:SEQ]
        mid_bf = sb("mid_bf", [H, SEQ], BF16)
        cum3 = sb("cum3", [P, SEQ], BF16)
        src_bias = sb("src_bias", [P, NT, H])
        rden = sb("rden", [P, NT, H])
        xb = lanes("xb", [P, NT, C], of=LAYERS)
        xr = lanes("xr", [P, NT, C], of=LAYERS)
        x1b = lanes("x1b", [P, NT, C], of=LAYERS)
        xs = lanes("xs", [P, NT, C], of=LAYERS)
        sT = lanes("sT", [C, SEQ], of=LAYERS)
        prob = lanes("prob", [P, H * (P + SEQ)], of=LAYERS)
        ss = lanes("ss", [P, NT, 2, H], of=LAYERS)
        rs = lanes("rs", [P, NT, 2, H], of=LAYERS)
        nbias = lanes("nbias", [P, NT, H], of=LAYERS)
        smax = lanes("smax", [P, NT, H], of=LAYERS)
        rsum = lanes("rsum", [P, NT, H], of=LAYERS)
        rinv = lanes("rinv", [P, NT, H], of=LAYERS)
        y = x1b[2]
        prod = [sb(f"prod{j}", [P, 2, H, D]) for j in range(2)]
        sqr = [sb(f"sqr{t}", [P, 2, H, D]) for t in range(NT)]
        rotr = [sb(f"rotr{t}", [P, 2, H, D]) for t in range(NT)]
        pt = sb("pt", [P, 3, H, P])

        prob0 = {s: prob[s][:, 0:H * P].rearrange("p (h t) -> p h t", h=H) for s in LAYERS}
        prob1 = {s: prob[s][:, H * P:3 * H * P].rearrange("p (h t) -> p h t", h=H) for s in LAYERS}
        o_sb = {s: lin[s][:, :, :].rearrange("p a (b t) -> p (a b t)", b=2).rearrange("p (t n) -> p t n", t=NT)
                for s in LAYERS}
        hT = {s: prob[s][:, 0:4 * SEQ].rearrange("p (b t) -> p b t", b=4) for s in LAYERS}
        hT[MLSTM] = lin[MLSTM]
        hid = {s: prob[s][:, 0:3 * SEQ].rearrange("p (b t) -> p b t", b=3) for s in LAYERS}
        gel = {s: lin[s][:, 0:3, :] for s in LAYERS}

        class Ring:
            def __init__(self, name):
                self.banks = [ctx.enter_context(nc.psum_tensor(f"{name}{j}", [P, 512], F32)) for j in range(2)]
                self.to_act = Count(sem(f"{name}_ready_for_scalar"))
                self.to_dve = Count(sem(f"{name}_ready_for_vector"))
                self.evacuated = [sem(f"{name}{j}_evacuated") for j in range(2)]
                self.uses = [0, 0]
                self.act_banks, self.dve_banks = [], []

        proj, score, turn, acc = Ring("proj"), Ring("score"), Ring("turn"), Ring("acc")
        RINGS = (proj, score, turn, acc)

        load_s = sem("weights_loaded")
        set_d = sem("setup_vector_done")
        set_a = sem("setup_scalar_done")
        set_p = sem("setup_tensor_done")
        set_g = sem("setup_gpsimd_done")

        x_loaded = Count(sem("x_loaded"))
        x_free = Count(sem("x_free"))
        y_ready = Count(sem("y_ready"))
        y_stored = Count(sem("y_stored"))
        y_free = Count(sem("y_free"))
        x1_ready = {s: Count(sem(f"x1_ready{s}")) for s in LAYERS}
        x1_pool = {s: Count(sem(f"x1_ready_for_gpsimd{s}")) for s in LAYERS}
        shifted = {s: Count(sem(f"x1_shifted{s}")) for s in LAYERS}
        half_kept = {s: Count(sem(f"first_half_copied{s}")) for s in LAYERS}
        x1b_ready = {s: Count(sem(f"x1_with_bias_ready{s}")) for s in LAYERS}
        stats_ready = {s: Count(sem(f"stats_ready{s}")) for s in (MLSTM, *LAYERS)}
        rstd_ready = {s: Count(sem(f"rstd_ready{s}")) for s in (MLSTM, *LAYERS)}
        nrm_ready = {s: Count(sem(f"normalised_ready{s}")) for s in (MLSTM, *LAYERS)}
        hn_ready = Count(sem("head_outputs_ready"))
        res_ready = {s: Count(sem(f"residual{s}_ready")) for s in LAYERS}
        cum_ready = Count(sem("split_cumulative_ready"))
        cum_act = Count(sem("cumulative_middle_ready"))
        mid_moved = Count(sem("cumulative_middle_moved"))
        bias_ready = Count(sem("source_bias_ready"))
        dec_ready = Count(sem("decays_ready"))
        dec_masked = Count(sem("decays_masked"))
        sq_ready = {s: Count(sem(f"squares_ready{s}")) for s in LAYERS}
        ss_ready = {s: Count(sem(f"sums_of_squares_ready{s}")) for s in LAYERS}
        prod_ready = {s: Count(sem(f"rotary_products_ready{s}")) for s in LAYERS}
        prod_free = [Count(sem(f"prod{j}_free")) for j in range(2)]
        qnorm_ready = {s: Count(sem(f"inverse_norms_of_q_ready{s}")) for s in LAYERS}
        rot_ready = {s: Count(sem(f"rotated_ready{s}")) for s in LAYERS}
        max_ready = {s: Count(sem(f"score_max_ready{s}")) for s in LAYERS}
        gelu_ready = {s: Count(sem(f"gelu_ready{s}")) for s in LAYERS}
        v_step = Count(sem("vector_step"))
        a_step = Count(sem("scalar_step"))
        g_step = Count(sem("gpsimd_step"))

        def rows(ap, n=P):
            return ap.rearrange("(b p) c -> p b c", p=n)

        n_q, n_k, n_v, n_o, n_w = (prob[1][:, j * HD:(j + 1) * HD] for j in range(5))
        w_raw = prob[1][:, 5 * HD:6 * HD].rearrange("p (b c) -> p b c", b=4)
        w1_n = prob[2][:, 0:2 * 2 * HID].rearrange("p (l n) -> p l n", l=DEPTH)
        tables = prob[2][:, 4 * HID:4 * HID + NT * 4 * D].rearrange("p (t n) -> p t n", t=NT)
        scales = prob[2][:, 4 * HID + NT * 4 * D:4 * HID + NT * 4 * D + DEPTH * 2 * D]\
            .rearrange("p (l w d) -> p l w d", l=DEPTH, w=2)
        n_i, n_f = nrm[0][0:H, 0, :], nrm[0][0:H, 1, :]
        lng_c = nrm[1][:, 0, 0:4]
        lnb_c = nrm[1][:, 0, 4:8]
        lb_c = nrm[1][:, 0, 8:8 + DEPTH]
        lg_c = nrm[1][:, 0, 16:16 + DEPTH]
        b1_n = nrm[1][:, 1, 0:6 * DEPTH].rearrange("p (l w b) -> p l w b", l=DEPTH, w=2)
        lnb_w = x1[1][:, :, :].rearrange("p t c -> p (t c)")
        lnb_w2 = x1[2][:, :, :].rearrange("p t c -> p (t c)")
        bo_n = work[0:1, 0:2, 0:SEQ]
        bo_r = work[0:1, 2:4, 0:SEQ]
        setup_g = [0]
        weight_loads = [(dst.rearrange("p (b c) -> p b c", b=4), rows(src))
                        for dst, src in ((n_q, Wq), (n_k, Wk), (n_v, Wv), (n_o, Wo))]
        weight_loads += [
            (n_w, W_out), (n_i, Wi), (n_f, Wf),
            (bi_c[:, :], bi.rearrange("(p o) -> p o", o=1)), (bf_c[FG:FG + H, :], bf.rearrange("(p o) -> p o", o=1)),
            (bo_n, bo.rearrange("(o a n) -> o a n", o=1, a=2)),
            (lng_c, lng.rearrange("(b p) -> p b", p=P)), (lnb_c, lnb.rearrange("(b p) -> p b", p=P)),
            (lb_c, lb.rearrange("l p -> p l")), (lg_c, lg.rearrange("l p -> p l")),
            (tables, rotary.rearrange("(t p) n -> p t n", p=P))]
        for l in range(DEPTH):
            weight_loads += [
                (wqkv_sb[:, l, :], wqkv[l, :, :]), (wo_sb[:, l, :, :], rows(wo[l, :, :])), (w1_n[:, l, :], w1[l, :, :]),
                (b2_sb[:, l, :], b2[l, :].partition_broadcast(P)),
                (scales[:, l, 0, :], qsc[l, :].partition_broadcast(P)),
                (scales[:, l, 1, :], ksc[l, :].partition_broadcast(P))]
            for b, (at, n) in enumerate(HB):
                weight_loads += [(w2_sb[0:n, l, b, :], w2[l, at:at + n, :])]
                for w in range(2):
                    a = w * HID + at
                    weight_loads += [(b1_n[0:n, l, w, b:b + 1], b1[l, a:a + n].rearrange("(p o) -> p o", o=1))]

        def load_weights(engine, loads):
            with nc.allow_non_contiguous_dma(reason="a few hundred words of biases, once"):
                for dst, src in loads:
                    engine.dma_start(dst, src).then_inc(load_s, 16)

        with nc.Block() as block:
            @block.sync
            def _(sp):
                load_weights(sp, weight_loads[0::2])

            @block.gpsimd
            def _(pool):
                g = nc.gpsimd
                n = [0]

                def link(ins):
                    n[0] += 1
                    ins.then_inc(set_g, 1)
                    pool.wait_ge(set_g, n[0])

                link(g.memset(ident[:, :], 0.0))
                link(g.affine_select(out=ident[:, :], in_=ident[:, :], compare_op=ALU.not_equal, fill=1.0,
                                     base=0, pattern=[[-1, P]], channel_multiplier=1))
                link(g.tensor_copy(ident_bf[:, :], ident[:, :]))
                link(g.memset(band0[:, :, :], 0.0))
                link(g.memset(band1[:, :, :], 0.0))
                link(g.affine_select(out=band0[:, :, :], in_=band0[:, :, :], compare_op=ALU.is_ge, fill=MASKED,
                                     base=0, pattern=[[0, 2], [-1, P]], channel_multiplier=1))
                link(g.affine_select(out=band0[:, :, :], in_=band0[:, :, :], compare_op=ALU.is_ge, fill=MASKED,
                                     base=WINDOW, pattern=[[0, 2], [1, P]], channel_multiplier=-1))
                link(g.affine_select(out=band1[:, :, :], in_=band1[:, :, :], compare_op=ALU.is_ge, fill=MASKED,
                                     base=P - WINDOW, pattern=[[0, 2], [-1, KEYS]], channel_multiplier=1))
                link(g.affine_select(out=band1[:, :, :], in_=band1[:, :, :], compare_op=ALU.is_ge, fill=MASKED,
                                     base=0, pattern=[[0, 2], [1, KEYS]], channel_multiplier=-1))
                link(g.memset(pick[:, :, :], 0.0))
                for part in range(3):
                    link(g.affine_select(out=pick[:, :, :], in_=pick[:, :, :], compare_op=ALU.not_equal, fill=1.0,
                                         base=-32 * part, pattern=[[-1, H], [0, P]], channel_multiplier=1))
                link(g.memset(ones_bf[:, :], 1.0))
                link(g.memset(minus_half[:, :], -0.5))
                link(g.memset(bo3[:, :], 0.0))
                for s in (MLSTM, *LAYERS):
                    link(g.memset(bd[s][:, :, :, :], 0.0))
                    link(g.memset(v[s][:, :, :, D:D + 1], 1.0))
                for s in LAYERS:
                    link(g.memset(sT[s][:, 0:1], 0.0))
                    link(g.memset(xs[s][:, :, :], 0.0))
                link(g.memset(cum3[:, :], 0.0))
                link(g.memset(gate_w[:, :], 0.0))
                setup_g[0] = n[0]

            @block.tensor
            def _(pe):
                pe.wait_ge(load_s, 16 * len(weight_loads))
                pe.wait_ge(set_g, setup_g[0])
                bank = [proj.banks[0], proj.banks[1], score.banks[0], score.banks[1], turn.banks[0]]
                for j, src in enumerate((n_q, n_k, n_v, n_o, n_w)):
                    for b in range(4):
                        last = nc.tensor.transpose(bank[j][:, b * P:(b + 1) * P], src[:, b * P:(b + 1) * P], ident[:, :])
                nc.tensor.transpose(turn.banks[1][:, 0:H], n_i, ident[0:H, 0:H])
                last = nc.tensor.transpose(turn.banks[1][:, H:2 * H], n_f, ident[0:H, 0:H])
                last.then_inc(set_p, 1)
                pe.wait_ge(set_d, 8)
                for b in range(4):
                    half = (lnb_w if b < 2 else lnb_w2)[:, (b % 2) * P:(b % 2 + 1) * P]
                    nc.tensor.matmul(acc.banks[0][:, 0:C], half, w_raw[:, b, :], start=(b == 0), stop=(b == 3))
                for l in range(DEPTH):
                    for w in range(2):
                        for b, (at, m) in enumerate(HB):
                            a = w * HID + at
                            last = nc.tensor.matmul(acc.banks[1][0:m, (l * 2 + w) * 3 + b:(l * 2 + w) * 3 + b + 1],
                                                    w1_n[:, l, a:a + m], lb_c[:, l:l + 1], start=True, stop=True)
                last.then_inc(set_p, 1)

            @block.scalar
            def _(act):
                load_weights(act, weight_loads[1::2])
                act.wait_ge(set_p, 1)
                for dst, src in ((wqT, proj.banks[0]), (wkT, proj.banks[1]), (wvT, score.banks[0]), (woT, score.banks[1])):
                    nc.scalar.activation(dst[:, :], src[:, :], ACT.Copy).then_inc(set_a, 1)

            @block.vector
            def _(dve):
                V = nc.vector
                n = [0]

                def link(ins):
                    n[0] += 1
                    ins.then_inc(set_d, 1)
                    dve.wait_ge(set_d, n[0])

                dve.wait_ge(set_p, 1)
                link(V.tensor_copy(gate_w[:, 0:H], turn.banks[1][:, 0:H]))
                link(V.tensor_copy(gate_w[:, FG:FG + H], turn.banks[1][:, H:2 * H]))
                link(V.tensor_copy(w_raw, turn.banks[0][:, :].rearrange("p (b c) -> p b c", b=4)))
                link(V.tensor_tensor(w_out[:, :, :], w_raw, lng_c.unsqueeze(2).broadcast_to([P, 4, C]), ALU.mult))
                for b in range(4):
                    half = (lnb_w if b < 2 else lnb_w2)[:, (b % 2) * P:(b % 2 + 1) * P]
                    link(V.tensor_copy(half, lnb_c[:, b:b + 1].broadcast_to([P, P])))
                for l in range(DEPTH):
                    link(V.tensor_scalar(w1_sb[:, l, :], w1_n[:, l, :], lg_c[:, l:l + 1], None, ALU.mult))
                for l in range(DEPTH):
                    for t in range(NT):
                        tab = tables[:, t, :].rearrange("p (w u d) -> p w u d", w=2, u=2)
                        sc = scales[:, l, :, :].unsqueeze(2).broadcast_to([P, 2, 2, D])
                        link(V.tensor_tensor(rot[:, l, t, :, :, :], tab, sc, ALU.mult))
                def halves(ap):
                    return ap.rearrange("o (a n) -> o a n", a=2)

                link(V.tensor_copy(halves(bo3[0:1, :]), bo_n))
                link(V.tensor_tensor(bo_r, bo_n, halves(bo3[0:1, :]), ALU.subtract))
                link(V.tensor_copy(halves(bo3[32:33, :]), bo_r))
                for a in range(2):
                    link(V.tensor_copy(mid_bf[0:1, :], bo_r[:, a, :]))
                    link(V.tensor_tensor(bo3[64:65, a * SEQ:(a + 1) * SEQ], bo_r[:, a, :], mid_bf[0:1, :], ALU.subtract))
                dve.wait_ge(set_p, 2)
                link(V.tensor_copy(out_bias[:, :], acc.banks[0][:, 0:C]))
                for l in range(DEPTH):
                    for b, (at, m) in enumerate(HB):
                        col = acc.banks[1][0:m, l * 6 + b:l * 6 + b + 4:3]
                        link(V.tensor_tensor(b1_c[0:m, l, :, b], b1_n[0:m, l, :, b], col, ALU.add))
                for s in LAYERS:
                    link(V.memset(prob1[s][:, :, 0:WINDOW], 0.0))

        SEQS = x.shape[0]
        FULL = SEQS - len(FIRST_TURNS)

        def walk(which, engine, stages, settle_turn):
            def turn_of(parts):
                for lane, name in schedule(parts, which):
                    stages[name](lane)
                settle_turn()

            for parts in FIRST_TURNS:
                turn_of(parts)
            with engine.Fori(0, FULL):
                turn_of(FULL_TURN)
            for parts in LAST_TURNS:
                turn_of(parts)

        xv = x.rearrange("b (t p) c -> b p t c", p=P)
        ov = out.rearrange("b (t p) c -> b p t c", p=P)

        with nc.Block() as block:
            @block.tensor
            def _(pe):
                T = nc.tensor
                at = {r: 0 for r in RINGS}

                class Use:

                    def __init__(self, ring, j):
                        self.tile, self.sem, self.value = ring.banks[j], ring.evacuated[j], ring.uses[j] + 1

                def claim(ring, to_act=False, to_dve=False):
                    j = at[ring] % 2
                    at[ring] += 1
                    pe.wait_ge(ring.evacuated[j], ring.uses[j] + 1)
                    ring.uses[j] += 1
                    if to_act:
                        ring.act_banks.append(j)
                    if to_dve:
                        ring.dve_banks.append(j)
                    return Use(ring, j)

                def wait_evacuated(uses):
                    for u in {u.sem.name: u for u in sorted(uses, key=lambda u: u.value)}.values():
                        pe.wait_ge(u.sem, u.value)

                made = {s: {} for s in (MLSTM, *LAYERS)}

                def turn_tile(s, src, ready, name):
                    use = claim(turn, to_act=True)
                    b = use.tile
                    pe.wait_ge(ready.sem, ready.next())
                    made[s][name] = [use]
                    for t in range(NT):
                        last = T.transpose(b[:, t * P:(t + 1) * P], src[:, t, :], ident[:, :])
                    last.then_inc(turn.to_act.sem, 1)

                def gate_products(s):
                    use = claim(turn, to_dve=True)
                    b = use.tile
                    wait_evacuated(made[s]["nT"])
                    made[s]["gates"] = [use]
                    T.matmul(b[0:FG + H, 0:SEQ], gate_w[:, :], nT[s][:, :], start=True, stop=True)\
                     .then_inc(turn.to_dve.sem, 1)

                def gates_turned(s):
                    use = claim(acc, to_dve=True)
                    b = use.tile
                    wait_evacuated(made[s]["gates"])
                    for t in range(NT):
                        last = T.transpose(b[:, t * H:(t + 1) * H], gi[:, t * P:(t + 1) * P], ident[0:H, 0:H])
                    last.then_inc(acc.to_dve.sem, 1)

                def mlstm_feature_heads(s, w, is_q):
                    if is_q:
                        made[s]["heads"] = []
                    for g2 in range(2):
                        use = claim(proj, to_act=is_q, to_dve=not is_q)
                        b = use.tile
                        made[s]["heads"].append(use)
                        for e in range(2):
                            p2 = 2 * g2 + e
                            last = T.matmul(b[:, e * SEQ:(e + 1) * SEQ], w[:, p2 * P:(p2 + 1) * P], nT[s][:, :],
                                            start=True, stop=True)
                        last.then_inc((proj.to_act if is_q else proj.to_dve).sem, 1)

                def mlstm_token_heads(s, w, gate):
                    if not gate:
                        made[s]["v"] = []
                    for t in range(NT):
                        use = claim(proj, to_act=True)
                        b = use.tile
                        made[s]["v"].append(use)
                        last = T.matmul(b[:, :], nT[s][:, t * P:(t + 1) * P], w[:, :], start=True, stop=not gate)
                        if gate:
                            last = T.matmul(b[:, :], ones_bf[:, :], bo3[:, :], start=False, stop=True)
                        last.then_inc(proj.to_act.sem, 1)

                def spread_gates(s, pairs):
                    if pairs[0] == 0:
                        pe.wait_ge(cum_ready.sem, cum_ready.next())
                        pe.wait_ge(mid_moved.sem, mid_moved.next())
                    for p2 in pairs:
                        use = claim(proj, to_act=True)
                        b = use.tile
                        for e in range(2):
                            last = T.matmul(b[:, e * SEQ:(e + 1) * SEQ], pick[:, 2 * p2 + e, :], cum3[:, :],
                                            start=True, stop=True)
                        last.then_inc(proj.to_act.sem, 1)

                def mlstm_scores0(s, pairs):
                    if pairs[0] == 0:
                        wait_evacuated(made[s]["heads"])
                        made[s]["weights"] = []
                    for p2 in pairs:
                        use = claim(score, to_dve=True)
                        b = use.tile
                        made[s]["weights"].append(use)
                        T.matmul(b[:, :].rearrange("p (e t) -> p e t", e=2), lin[s][:, p2, 0:P], bd[s][:, p2, :, :],
                                 start=True, stop=True).then_inc(score.to_dve.sem, 1)

                def mlstm_scores1(s):
                    for g2 in range(2):
                        use = claim(score, to_dve=True)
                        b = use.tile
                        made[s]["weights"].append(use)
                        for e in range(2):
                            p2 = 2 * g2 + e
                            last = T.matmul(b[:, e * SEQ:(e + 1) * SEQ].rearrange("p (e t) -> p e t", e=2),
                                            lin[s][:, p2, P:SEQ], bd[s][:, p2, :, P:SEQ], start=True, stop=True)
                        last.then_inc(score.to_dve.sem, 1)

                def mlstm_values(s, t, g2):
                    if t == 0 and g2 == 0:
                        wait_evacuated(made[s]["v"])
                    if t == 0:
                        wait_evacuated(made[s]["weights"][2 * g2:2 * g2 + 2])
                    use = claim(acc, to_dve=True)
                    b = use.tile
                    if t == 1:
                        wait_evacuated(made[s]["weights"][PAIRS + g2:PAIRS + g2 + 1])
                    for j in range(4):
                        h = 4 * g2 + j
                        o = b[:, j * (D + 1):(j + 1) * (D + 1)]
                        last = T.matmul(o, work[:, h, t * P:(t + 1) * P], v[s][:, 0, h, :], start=True, stop=t == 0)
                        if t == 1:
                            last = T.matmul(o, work[:, h, SEQ:DW], v[s][:, 1, h, :], start=False, stop=True)
                    last.then_inc(acc.to_dve.sem, 1)

                def features_T(s, src, ready, t):
                    if t == 0:
                        made[s]["hT"] = []
                    use = claim(turn, to_act=True)
                    b = use.tile
                    made[s]["hT"].append(use)
                    if ready is None:
                        wait_evacuated(made[s]["outputs"][t:t + 1])
                    elif t == 0:
                        pe.wait_ge(ready.sem, ready.next())
                    for k in range(4):
                        last = T.transpose(b[:, k * P:(k + 1) * P], src[:, t, k * P:(k + 1) * P], ident[:, :])
                    last.then_inc(turn.to_act.sem, 1)

                def outputs_T(s, t):
                    if s == MLSTM:
                        features_T(s, hs, hn_ready, t)
                    else:
                        features_T(s, o_sb[s], None, t)

                def from_heads(s, w):
                    use = claim(acc, to_dve=True)
                    b = use.tile
                    for t in range(NT):
                        wait_evacuated(made[s]["hT"][t:t + 1])
                        for k in range(4):
                            last = T.matmul(b[:, t * C:(t + 1) * C], hT[s][:, k, t * P:(t + 1) * P], w[:, k, :],
                                            start=(k == 0), stop=(k == 3))
                    last.then_inc(acc.to_dve.sem, 1)

                def attention_projection(s, t, w):
                    if t == 0 and w == 0:
                        wait_evacuated(made[s]["sT"])
                    use = claim(proj, to_act=True, to_dve=w < 2)
                    if w == 2:
                        made[s]["v"] = [use] if t == 0 else made[s]["v"] + [use]
                    T.matmul(use.tile[:, :], sT[s][:, t * P:(t + 1) * P], wqkv_sb[:, s - 1, w * HD:(w + 1) * HD],
                             start=True, stop=True).then_inc(proj.to_act.sem, 1)

                def rotated_T(s, t):
                    if t == 0:
                        wait_evacuated(made[s].get("hidden", []))
                        made[s]["heads"] = []
                    pe.wait_ge(rot_ready[s].sem, rot_ready[s].next())
                    for w in range(2):
                        use = claim(turn, to_act=True)
                        b = use.tile
                        made[s]["heads"].append(use)
                        flat = rotr[t][:, w, :, :].rearrange("p h d -> p (h d)")
                        for k in range(4):
                            last = T.transpose(b[:, k * P:(k + 1) * P], flat[:, k * P:(k + 1) * P], ident[:, :])
                        last.then_inc(turn.to_act.sem, 1)

                def attention_scores0(s, g2):
                    if g2 == 0:
                        wait_evacuated(made[s]["heads"][0:2])
                        made[s]["prob"] = []
                    use = claim(score, to_act=True, to_dve=True)
                    b = use.tile
                    made[s]["prob"].append(use)
                    for e in range(2):
                        p2 = 2 * g2 + e
                        o = b[:, e * SEQ:(e + 1) * SEQ].rearrange("p (e t) -> p e t", e=2)
                        T.matmul(o, lin[s][:, p2, 0:P], bd[s][:, p2, :, 0:P], start=True, stop=False)
                        last = T.matmul(o, ident_bf[:, :], band0[:, :, :], start=False, stop=True)
                    last.then_inc(score.to_dve.sem, 1)

                def attention_scores1(s, p2):
                    if p2 == 0:
                        wait_evacuated(made[s]["heads"])
                    use = claim(score, to_act=True, to_dve=True)
                    made[s]["prob"].append(use)
                    o = use.tile[:, 0:2 * KEYS].rearrange("p (e t) -> p e t", e=2)
                    T.matmul(o, lin[s][:, p2, P:SEQ], bd[s][:, p2, :, WINDOW:SEQ], start=True, stop=False)
                    T.matmul(o, ident_bf[:, :], band1[:, :, :], start=False, stop=True).then_inc(score.to_dve.sem, 1)

                def probs_turned(s, ks):
                    if ks[0] == 0:
                        made[s]["pt"] = []
                    for k in ks:
                        blk, h0 = k // 2, 4 * (k % 2)
                        src = prob0[s] if blk == 0 else prob1[s][:, :, (blk - 1) * P:blk * P]
                        if blk == 0:
                            wait_evacuated(made[s]["prob"][k:k + 1])
                        if blk == 1:
                            wait_evacuated(made[s]["prob"][2 + h0 // 2:4 + h0 // 2])
                        use = claim(turn, to_act=k % 2 == 0, to_dve=k % 2 == 1)
                        b = use.tile
                        made[s]["pt"].append(use)
                        for j in range(4):
                            last = T.transpose(b[:, j * P:(j + 1) * P], src[:, h0 + j, :], ident[:, :])
                        last.then_inc((turn.to_act if k % 2 == 0 else turn.to_dve).sem, 1)

                def attention_values(s, t):
                    if t == 0:
                        wait_evacuated(made[s]["v"])
                        made[s]["outputs"] = []
                    use = claim(acc, to_dve=True)
                    b = use.tile
                    made[s]["outputs"].append(use)
                    wait_evacuated(made[s]["pt"][0:2] if t == 0 else made[s]["pt"][2:6])
                    for h in range(H):
                        o = b[:, h * D:(h + 1) * D]
                        last = T.matmul(o, pt[:, t, h, :], v[s][:, 0, h, 0:D], start=True, stop=t == 0)
                        if t == 1:
                            last = T.matmul(o, pt[:, 2, h, :], v[s][:, 1, h, 0:D], start=False, stop=True)
                    last.then_inc(acc.to_dve.sem, 1)

                def mlp_up(s, k):
                    l = s - 1
                    a, m = HB[k]
                    if k == 0:
                        wait_evacuated(made[s]["nT"])
                        made[s]["hidden"] = []
                    use = claim(proj, to_act=True, to_dve=True)
                    b = use.tile
                    made[s]["hidden"].append(use)
                    T.matmul(b[0:m, 0:SEQ], w1_sb[:, l, HID + a:HID + a + m], nT[s][:, :], start=True, stop=True)
                    T.matmul(b[0:m, SEQ:2 * SEQ], w1_sb[:, l, a:a + m], nT[s][:, :], start=True, stop=True)\
                     .then_inc(proj.to_act.sem, 1)

                def mlp_down(s):
                    l = s - 1
                    hd = hid[s]
                    use = claim(acc, to_dve=True)
                    b = use.tile
                    wait_evacuated(made[s]["hidden"])
                    for t in range(NT):
                        for k, (a, m) in enumerate(HB):
                            last = T.matmul(b[:, t * C:(t + 1) * C], hd[0:m, k, t * P:(t + 1) * P], w2_sb[0:m, l, k, :],
                                            start=(k == 0), stop=(k == 2))
                    last.then_inc(acc.to_dve.sem, 1)

                for r in RINGS:
                    for c in r.evacuated:
                        pe.sem_inc(c, 1)

                def settle_turn():
                    settle(pe, [*nrm_ready.values(), *rot_ready.values(), *res_ready.values(),
                                hn_ready, cum_ready, mid_moved])
                    for r in RINGS:
                        for j in range(2):
                            if r.uses[j]:
                                pe.sem_inc(r.evacuated[j], -r.uses[j])
                                r.uses[j] = 0
                    for tiles in made.values():
                        for u in (u for uses in tiles.values() for u in uses):
                            u.value = 1

                walk(TENSOR, pe, {
                    "x_turn": lambda s: turn_tile(s, nrm[s], nrm_ready[s], "nT"),
                    "gates": gate_products,
                    "gate_bias": gates_turned,
                    "heads_q": lambda s: mlstm_feature_heads(s, wqT, True),
                    "heads_k": lambda s: mlstm_feature_heads(s, wkT, False),
                    "heads_v": lambda s: mlstm_token_heads(s, wvT, False),
                    "heads_o": lambda s: mlstm_token_heads(s, woT, True),
                    "decays0": lambda s: spread_gates(s, (0, 1)),
                    "decays1": lambda s: spread_gates(s, (2, 3)),
                    "weights0": lambda s: mlstm_scores0(s, (0, 1)),
                    "weights1": lambda s: mlstm_scores0(s, (2, 3)),
                    "weights2": mlstm_scores1,
                    "heads_out0": lambda s: mlstm_values(s, 0, 0),
                    "heads_out1": lambda s: mlstm_values(s, 0, 1),
                    "heads_out2": lambda s: mlstm_values(s, 1, 0),
                    "heads_out3": lambda s: mlstm_values(s, 1, 1),
                    "outputs0": lambda s: outputs_T(s, 0),
                    "outputs1": lambda s: outputs_T(s, 1),
                    "mlstm_project": lambda s: from_heads(s, w_out),
                    "layer_in": lambda s: turn_tile(s, xb[s], res_ready[s], "sT"),
                    "query0": lambda s: attention_projection(s, 0, 0),
                    "key0": lambda s: attention_projection(s, 0, 1),
                    "value0": lambda s: attention_projection(s, 0, 2),
                    "query1": lambda s: attention_projection(s, 1, 0),
                    "key1": lambda s: attention_projection(s, 1, 1),
                    "value1": lambda s: attention_projection(s, 1, 2),
                    "rotated0": lambda s: rotated_T(s, 0),
                    "rotated1": lambda s: rotated_T(s, 1),
                    "scores0": lambda s: attention_scores0(s, 0),
                    "scores1": lambda s: attention_scores0(s, 1),
                    "scores2": lambda s: attention_scores1(s, 0),
                    "scores3": lambda s: attention_scores1(s, 1),
                    "scores4": lambda s: attention_scores1(s, 2),
                    "scores5": lambda s: attention_scores1(s, 3),
                    "probs0": lambda s: probs_turned(s, (0, 1)),
                    "probs1": lambda s: probs_turned(s, (2, 3)),
                    "probs2": lambda s: probs_turned(s, (4, 5)),
                    "values0": lambda s: attention_values(s, 0),
                    "values1": lambda s: attention_values(s, 1),
                    "residual": lambda s: from_heads(s, wo_sb[:, s - 1, :, :]),
                    "mlp_in": lambda s: turn_tile(s, nrm[s], nrm_ready[s], "nT"),
                    "mlp_up0": lambda s: mlp_up(s, 0),
                    "mlp_up1": lambda s: mlp_up(s, 1),
                    "mlp_up2": lambda s: mlp_up(s, 2),
                    "mlp_down": mlp_down,
                }, settle_turn)

            @block.sync
            def _(sp):
                def load_x(n):
                    sp.dma_start(x_in[:, :, :], xv[bass.ds(n, 1), :, :, :].rearrange("o p t c -> p (o t) c"))\
                      .then_inc(x_loaded.sem, 16)

                def shift(s):
                    sp.wait_ge(x1_ready[s].sem, x1_ready[s].next())
                    sp.dma_start(xs[s][1:P, :, D:C], x1[s][0:P - 1, :, D:C]).then_inc(shifted[s].sem, 16)
                    sp.dma_start(xs[s][0:1, 1, D:C], x1[s][P - 1:P, 0, D:C]).then_inc(shifted[s].sem, 16)

                def turn_of(parts, n, more):
                    if "back2" in parts:
                        shift(2)
                    if "back1" in parts:
                        shift(1)
                    if "back2" in parts:
                        sp.wait_ge(y_ready.sem, y_ready.next())
                        sp.dma_start(ov[bass.ds(n, 1), :, :, :].rearrange("o p t c -> p (o t) c"), y[:, :, :])\
                          .then_inc(y_stored.sem, 16)
                        sp.wait_ge(y_stored.sem, y_stored.next(16))
                        sp.sem_inc(y_free.sem, 1)
                    if more is not None:
                        sp.wait_ge(x_free.sem, x_free.next())
                        load_x(more)
                    settle(sp, [x_free, *x1_ready.values(), y_ready, y_stored])

                load_x(0)
                sp.sem_inc(y_free.sem, 1)
                for n, parts in enumerate(FIRST_TURNS):
                    turn_of(parts, None, n + 1)
                lead = len(FIRST_TURNS)
                if FULL > 1:
                    with sp.Fori(0, FULL - 1) as i:
                        turn_of(FULL_TURN, i, i + lead + 1)
                turn_of(FULL_TURN, FULL - 1, None)
                for n, parts in enumerate(LAST_TURNS):
                    turn_of(parts, FULL + n, None)

            @block.gpsimd
            def _(pool):
                g = nc.gpsimd

                def link(ins):
                    ins.then_inc(g_step.sem, 1)
                    pool.wait_ge(g_step.sem, g_step.next())

                def inverse_std(s):
                    pool.wait_ge(stats_ready[s].sem, stats_ready[s].next())
                    link(g.tensor_scalar(veps[s][:, :], mv[s][:, :, 1], EPS, None, ALU.add))
                    g.tensor_tensor(rstd[s][:, :], veps[s][:, :], minus_half[:, 0:NT], ALU.pow)\
                     .then_inc(rstd_ready[s].sem, 1)

                def mask_decays(s, a):
                    pool.wait_ge(dec_ready.sem, dec_ready.next())
                    for t in range(NT):
                        part = work[:, a:a + 4, 0:P] if t == 0 else work[:, a:a + 4, SEQ:SEQ + P]
                        g.affine_select(out=part, in_=part, compare_op=ALU.is_ge, fill=0.0, base=0,
                                        pattern=[[0, 4], [1, P]], channel_multiplier=-1).then_inc(dec_masked.sem, 1)

                def rotate(s, t, w):
                    r = rotr[t]
                    pool.wait_ge(prod_ready[s].sem, prod_ready[s].next())
                    pr = prod[w]
                    for half in range(2):
                        a, b = half * 32, 32 - half * 32
                        g.tensor_tensor(r[:, w, :, a:a + 32], pr[:, 0, :, a:a + 32], pr[:, 1, :, b:b + 32],
                                        ALU.add).then_inc(g_step.sem, 1)
                        g_step.next()
                    pool.wait_ge(g_step.sem, g_step.seen)
                    pool.sem_inc(prod_free[w].sem, 1)

                def inverse_norms(s, t, w):
                    return g.tensor_tensor(rs[s][:, t, w, :], ss[s][:, t, w, :], minus_half[:, 0:H], ALU.pow)

                def scale_k(s, t):
                    r = rotr[t]
                    g.tensor_tensor(r[:, 1, :, :], r[:, 1, :, :],
                                    rs[s][:, t, 1, :].unsqueeze(2).broadcast_to([P, H, D]), ALU.mult)\
                     .then_inc(rot_ready[s].sem, 1)

                def mlp_inputs(s):
                    l = s - 1
                    pool.wait_ge(x1_pool[s].sem, x1_pool[s].next())
                    g.tensor_copy(xs[s][:, :, 0:D], x1[s][:, :, 0:D]).then_inc(half_kept[s].sem, 1)
                    if s == 2:
                        pool.wait_ge(y_free.sem, y_free.next())
                    g.tensor_tensor(x1b[s][:, :, :], x1[s][:, :, :],
                                    b2_sb[:, l, :].unsqueeze(1).broadcast_to([P, NT, C]), ALU.add)\
                     .then_inc(x1b_ready[s].sem, 1)

                def rotate_k(s, t):
                    rotate(s, t, 1)
                    pool.wait_ge(ss_ready[s].sem, ss_ready[s].next())
                    link(inverse_norms(s, t, 1))
                    scale_k(s, t)
                    inverse_norms(s, t, 0).then_inc(qnorm_ready[s].sem, 1)

                walk(GPSIMD, pool, {
                    "x_stats": inverse_std,
                    "decays0": lambda s: mask_decays(s, 0),
                    "decays1": lambda s: mask_decays(s, 4),
                    "heads_out3": inverse_std,
                    "mlstm_project": inverse_std,
                    "mlstm_residual": inverse_std,
                    "query0": lambda s: rotate(s, 0, 0),
                    "key0": lambda s: rotate_k(s, 0),
                    "query1": lambda s: rotate(s, 1, 0),
                    "key1": lambda s: rotate_k(s, 1),
                    "residual": mlp_inputs,
                    "shifted_stats": inverse_std,
                    "final_stats": inverse_std,
                }, lambda: settle(pool, [*stats_ready.values(), *prod_ready.values(), *ss_ready.values(), *x1_pool.values(),
                                  dec_ready, y_free, g_step]))

            @block.scalar
            def _(act):
                A = nc.scalar

                def bank(ring):
                    j = ring.act_banks.pop(0)
                    return ring.banks[j], ring.evacuated[j]

                def normal_T(s):
                    b, free = bank(turn)
                    act.wait_ge(turn.to_act.sem, turn.to_act.next())
                    ins = A.activation(nT[s][:, :], b[:, 0:SEQ], ACT.Copy)
                    ins.then_inc(free, 1)

                def move_middle(s):
                    act.wait_ge(cum_act.sem, cum_act.next())
                    A.activation(cum3[32:32 + H, :], mid_bf[:, :], ACT.Copy).then_inc(mid_moved.sem, 1)

                def mlstm_q(s):
                    for g2 in range(2):
                        b, free = bank(proj)
                        act.wait_ge(proj.to_act.sem, proj.to_act.next())
                        src = b[:, :].rearrange("p (a t) -> p a t", a=2)
                        for e in range(2):
                            ins = A.activation(bd[s][e * D:(e + 1) * D, 2 * g2:2 * g2 + 2, e, :],
                                               src[e * D:(e + 1) * D, :, :], ACT.Copy)
                        ins.then_inc(free, 1)

                def mlstm_v(s):
                    for t in range(NT):
                        b, free = bank(proj)
                        act.wait_ge(proj.to_act.sem, proj.to_act.next())
                        ins = A.activation(v[s][:, t, :, 0:D], b[:, :].rearrange("p (h d) -> p h d", h=H), ACT.Copy)
                        ins.then_inc(free, 1)

                def mlstm_gate(s):
                    for t in range(NT):
                        b, free = bank(proj)
                        act.wait_ge(proj.to_act.sem, proj.to_act.next())
                        ins = A.activation(th[:, t, :], b[:, :], ACT.Tanh, scale=0.5)
                        ins.then_inc(free, 1)

                def decays(s, pairs):
                    if pairs[0] == 0:
                        act.wait_ge(bias_ready.sem, bias_ready.next())
                    for p2 in pairs:
                        b, free = bank(proj)
                        act.wait_ge(proj.to_act.sem, proj.to_act.next())
                        src = b[:, :].rearrange("p (e t) -> p e t", e=2)
                        for e in range(2):
                            h = 2 * p2 + e
                            A.activation(work[:, h, 0:SEQ], src[:, e, :], ACT.Exp, bias=src_bias[:, 0, h:h + 1])
                            ins = A.activation(work[:, h, SEQ:DW], src[:, e, P:SEQ], ACT.Exp,
                                               bias=src_bias[:, 1, h:h + 1])
                        if p2 < pairs[-1]:
                            ins.then_inc(free, 1)
                    ins.then_inc(a_step.sem, 1)
                    act.wait_ge(a_step.sem, a_step.next())
                    act.sem_inc(free, 1)
                    act.sem_inc(dec_ready.sem, 1)

                def outputs_T(s, t):
                    b, free = bank(turn)
                    act.wait_ge(turn.to_act.sem, turn.to_act.next())
                    ins = A.activation(hT[s][:, :, t * P:(t + 1) * P], b[:, :].rearrange("p (b t) -> p b t", b=4), ACT.Copy)
                    ins.then_inc(free, 1)

                def shifted_T(s):
                    b, free = bank(turn)
                    act.wait_ge(turn.to_act.sem, turn.to_act.next())
                    A.activation(sT[s][0:D, :], b[0:D, 0:SEQ], ACT.Copy)
                    ins = A.activation(sT[s][D:C, 1:SEQ], b[D:C, 0:SEQ - 1], ACT.Copy)
                    ins.then_inc(free, 1)

                def squares(s, t, w):
                    b, free = bank(proj)
                    act.wait_ge(proj.to_act.sem, proj.to_act.next())
                    A.activation(sqr[t][:, w, :, :], b[:, :].rearrange("p (h d) -> p h d", h=H), ACT.Square)\
                     .then_inc(sq_ready[s].sem, 1)

                def attention_v(s, t):
                    b, free = bank(proj)
                    act.wait_ge(proj.to_act.sem, proj.to_act.next())
                    A.activation(v[s][:, t, :, 0:D], b[:, :].rearrange("p (h d) -> p h d", h=H), ACT.Copy)\
                     .then_inc(free, 1)

                def rotated_T(s, t):
                    b, free = bank(turn)
                    act.wait_ge(turn.to_act.sem, turn.to_act.next())
                    A.activation(lin[s][:, :, t * P:(t + 1) * P], b[:, :].rearrange("p (b t) -> p b t", b=4), ACT.Copy)\
                     .then_inc(free, 1)
                    b, free = bank(turn)
                    act.wait_ge(turn.to_act.sem, turn.to_act.next())
                    src = b[:, :].rearrange("p (b t) -> p b t", b=4)
                    for e in range(2):
                        ins = A.activation(bd[s][e * D:(e + 1) * D, :, e, t * P:(t + 1) * P], src[e * D:(e + 1) * D, :, :],
                                           ACT.Copy)
                    ins.then_inc(free, 1)

                def softmax0(s, g2):
                    b, free = bank(score)
                    act.wait_ge(max_ready[s].sem, max_ready[s].next())
                    for j in range(4):
                        h = 4 * g2 + j
                        ins = A.activation(prob0[s][:, h, :], b[:, j * P:(j + 1) * P], ACT.Exp,
                                           scale=rs[s][:, 0, 0, h:h + 1], bias=nbias[s][:, 0, h:h + 1],
                                           accum_out=rsum[s][:, 0, h:h + 1])
                    ins.then_inc(free, 1)

                def softmax1(s, p2):
                    b, free = bank(score)
                    act.wait_ge(max_ready[s].sem, max_ready[s].next())
                    for e in range(2):
                        h = 2 * p2 + e
                        ins = A.activation(prob1[s][:, h, WINDOW:SEQ], b[:, e * KEYS:(e + 1) * KEYS], ACT.Exp,
                                           scale=rs[s][:, 1, 0, h:h + 1], bias=nbias[s][:, 1, h:h + 1],
                                           accum_out=rsum[s][:, 1, h:h + 1])
                    ins.then_inc(free, 1)

                def probs_T(s, ks):
                    for k in ks:
                        if k % 2 == 0:
                            b, free = bank(turn)
                            act.wait_ge(turn.to_act.sem, turn.to_act.next())
                            ins = A.activation(pt[:, k // 2, 4 * (k % 2):4 * (k % 2) + 4, :],
                                               b[:, :].rearrange("p (h t) -> p h t", h=4), ACT.Copy)
                            ins.then_inc(free, 1)

                def gelu(s, k):
                    m = HB[k][1]
                    b, free = bank(proj)
                    act.wait_ge(proj.to_act.sem, proj.to_act.next())
                    A.activation(gel[s][0:m, k, :], b[0:m, 0:SEQ], ACT.Gelu,
                                 bias=b1_c[0:m, s - 1, 1, k:k + 1]).then_inc(gelu_ready[s].sem, 1)

                walk(SCALAR, act, {
                    "x_turn": normal_T,
                    "gates": move_middle,
                    "heads_q": mlstm_q,
                    "heads_v": mlstm_v,
                    "heads_o": mlstm_gate,
                    "decays0": lambda s: decays(s, (0, 1)),
                    "decays1": lambda s: decays(s, (2, 3)),
                    "outputs0": lambda s: outputs_T(s, 0),
                    "outputs1": lambda s: outputs_T(s, 1),
                    "layer_in": shifted_T,
                    "query0": lambda s: squares(s, 0, 0),
                    "key0": lambda s: squares(s, 0, 1),
                    "value0": lambda s: attention_v(s, 0),
                    "query1": lambda s: squares(s, 1, 0),
                    "key1": lambda s: squares(s, 1, 1),
                    "value1": lambda s: attention_v(s, 1),
                    "rotated0": lambda s: rotated_T(s, 0),
                    "rotated1": lambda s: rotated_T(s, 1),
                    "scores0": lambda s: softmax0(s, 0),
                    "scores1": lambda s: softmax0(s, 1),
                    "scores2": lambda s: softmax1(s, 0),
                    "scores3": lambda s: softmax1(s, 1),
                    "scores4": lambda s: softmax1(s, 2),
                    "scores5": lambda s: softmax1(s, 3),
                    "probs0": lambda s: probs_T(s, (0, 1)),
                    "probs1": lambda s: probs_T(s, (2, 3)),
                    "probs2": lambda s: probs_T(s, (4, 5)),
                    "mlp_in": normal_T,
                    "mlp_up0": lambda s: gelu(s, 0),
                    "mlp_up1": lambda s: gelu(s, 1),
                    "mlp_up2": lambda s: gelu(s, 2),
                }, lambda: settle(act, [r.to_act for r in RINGS] + [cum_act, bias_ready, *max_ready.values(), a_step]))

            @block.vector
            def _(dve):
                V = nc.vector

                def link(ins):
                    ins.then_inc(v_step.sem, 1)
                    dve.wait_ge(v_step.sem, v_step.next())

                def bank(ring):
                    j = ring.dve_banks.pop(0)
                    return ring.banks[j], ring.evacuated[j]

                def stats_of(s, src):
                    for t in range(NT):
                        ins = V.bn_stats(stats[s][:, t, :], src[:, t, :])
                        ins.then_inc(v_step.sem, 1)
                        v_step.next()
                    dve.wait_ge(v_step.sem, v_step.seen)
                    for t in range(NT):
                        ins = V.bn_aggr(mv[s][:, t, :], stats[s][:, t, :])
                        if t < NT - 1:
                            ins.then_inc(v_step.sem, 1)
                            v_step.next()
                    link(ins)
                    dve.sem_inc(stats_ready[s].sem, 1)

                def normalise(s, dst, src, ready, link_it=False):
                    dve.wait_ge(rstd_ready[s].sem, rstd_ready[s].next())
                    for t in range(NT):
                        ins = V.tensor_scalar(dst[:, t, :], src[:, t, :], mv[s][:, t, 0:1], rstd[s][:, t:t + 1],
                                              ALU.subtract, ALU.mult)
                        if ready is not None and t == NT - 1:
                            ins.then_inc(ready.sem, 1)
                        if link_it:
                            ins.then_inc(v_step.sem, 1)
                            v_step.next()
                    if link_it:
                        dve.wait_ge(v_step.sem, v_step.seen)

                def gates(s):
                    b, free = bank(turn)
                    dve.wait_ge(turn.to_dve.sem, turn.to_dve.next())
                    link(V.tensor_tensor_scan(cum, bf_c[FG:FG + H, 0:1].broadcast_to([H, SEQ]), b[FG:FG + H, 0:SEQ],
                                              0.0, ALU.add, ALU.add))
                    ins = V.scalar_tensor_tensor(gi, b[0:H, 0:SEQ], bi_c[:, 0:1], cum,
                                                 ALU.add, ALU.subtract)
                    ins.then_inc(free, 1)
                    link(V.tensor_copy(cum3[0:H, :], cum))
                    link(V.tensor_tensor(rest, cum, cum3[0:H, :], ALU.subtract))
                    link(V.tensor_copy(mid_bf[:, :], rest))
                    dve.sem_inc(cum_act.sem, 1)
                    V.tensor_tensor(cum3[64:64 + H, :], rest, mid_bf[:, :], ALU.subtract)\
                     .then_inc(cum_ready.sem, 1)

                def source_bias(s):
                    b, free = bank(acc)
                    dve.wait_ge(acc.to_dve.sem, acc.to_dve.next())
                    link(V.tensor_copy(src_bias[:, :, :], b[:, 0:NT * H].rearrange("p (t h) -> p t h", t=NT)))
                    dve.sem_inc(free, 1)
                    dve.sem_inc(bias_ready.sem, 1)

                def mlstm_k(s):
                    for g2 in range(2):
                        b, free = bank(proj)
                        dve.wait_ge(proj.to_dve.sem, proj.to_dve.next())
                        ins = V.tensor_scalar(lin[s][:, 2 * g2:2 * g2 + 2, :], b[:, :].rearrange("p (a t) -> p a t", a=2),
                                              D ** -0.5, None, ALU.mult)
                        ins.then_inc(free, 1)

                def weigh0(s, pairs):
                    dve.wait_ge(dec_masked.sem, dec_masked.next(NT))
                    for p2 in pairs:
                        b, free = bank(score)
                        dve.wait_ge(score.to_dve.sem, score.to_dve.next())
                        part = work[:, 2 * p2:2 * p2 + 2, 0:SEQ]
                        V.tensor_tensor(part, b[:, :].rearrange("p (e t) -> p e t", e=2), part, ALU.mult)\
                         .then_inc(free, 1)

                def weigh1(s):
                    for g2 in range(2):
                        b, free = bank(score)
                        dve.wait_ge(score.to_dve.sem, score.to_dve.next())
                        part = work[:, 4 * g2:4 * g2 + 4, SEQ:DW]
                        V.tensor_tensor(part, b[:, :].rearrange("p (e t) -> p e t", e=4), part, ALU.mult)\
                         .then_inc(free, 1)

                def head_outputs(s, t, g2):
                    b, free = bank(acc)
                    dve.wait_ge(acc.to_dve.sem, acc.to_dve.next())
                    src = b[:, 0:4 * (D + 1)].rearrange("p (h d) -> p h d", h=4)
                    rd = rden[:, t, 4 * g2:4 * g2 + 4]
                    o = hs[:, t, 256 * g2:256 * g2 + 256].rearrange("p (h d) -> p h d", h=4)
                    gate = th[:, t, 256 * g2:256 * g2 + 256].rearrange("p (h d) -> p h d", h=4)
                    link(V.tensor_scalar(rd, src[:, :, D], -1.0, 1.0, ALU.mult, ALU.max))
                    link(V.tensor_tensor(rd, src[:, :, D], rd, ALU.max))
                    V.scalar_tensor_tensor(o, gate, 1.0, src[:, :, 0:D], ALU.add, ALU.mult).then_inc(v_step.sem, 1)
                    v_step.next()
                    link(V.reciprocal(rd, rd))
                    dve.sem_inc(free, 1)
                    link(V.scalar_tensor_tensor(o, o, 0.5, rd.unsqueeze(2).broadcast_to([P, 4, D]), ALU.mult, ALU.mult))

                def project_out(s):
                    b, free = bank(acc)
                    dve.wait_ge(acc.to_dve.sem, acc.to_dve.next())
                    ins = V.tensor_tensor(x1[s][:, :, :], b[:, 0:SEQ].rearrange("p (t c) -> p t c", t=NT),
                                          out_bias[:, :].unsqueeze(1).broadcast_to([P, NT, C]), ALU.add)
                    link(ins)
                    dve.sem_inc(free, 1)
                    stats_of(s, x1[s])

                def mlstm_residual(s):
                    normalise(s, x1[s], x1[s], None, link_it=True)
                    ins = V.tensor_tensor(passed[0][:, :, :], x1[s][:, :, :], x_in[:, :, :], ALU.add)
                    link(ins)
                    dve.sem_inc(x_free.sem, 1)
                    stats_of(s, passed[0])

                def rotary_product(s, t, w):
                    b, free = bank(proj)
                    dve.wait_ge(sq_ready[s].sem, sq_ready[s].next())
                    dve.wait_ge(prod_free[w].sem, prod_free[w].next())
                    src = b[:, :].rearrange("p (h d) -> p h d", h=H).unsqueeze(1).broadcast_to([P, 2, H, D])
                    tab = rot[:, s - 1, t, w, :, :].unsqueeze(2).broadcast_to([P, 2, H, D])
                    V.tensor_tensor(prod[w][:, :, :, :], src, tab, ALU.mult).then_inc(v_step.sem, 1)
                    written = v_step.next()
                    if w == 1:
                        V.tensor_reduce(ss[s][:, t, :, :], sqr[t][:, :, :, :], axis=AXX, op=ALU.add)\
                         .then_inc(v_step.sem, 1)
                        v_step.next()
                    dve.wait_ge(v_step.sem, written)
                    dve.sem_inc(free, 1)
                    dve.sem_inc(prod_ready[s].sem, 1)
                    if w == 1:
                        dve.wait_ge(v_step.sem, v_step.seen)
                        V.tensor_scalar(ss[s][:, t, :, :], ss[s][:, t, :, :], 1e-24, None, ALU.max)\
                         .then_inc(ss_ready[s].sem, 1)

                def maxima(s, t, h, n, view):
                    if h == 0:
                        dve.wait_ge(qnorm_ready[s].sem, qnorm_ready[s].next())
                    dve.wait_ge(score.to_dve.sem, score.to_dve.next())
                    link(V.tensor_reduce(smax[s][:, t, h:h + n], view, axis=AXX, op=ALU.max))
                    V.scalar_tensor_tensor(nbias[s][:, t, h:h + n], smax[s][:, t, h:h + n], -1.0,
                                           rs[s][:, t, 0, h:h + n], ALU.mult, ALU.mult).then_inc(max_ready[s].sem, 1)

                def score_max0(s, g2):
                    b, _ = bank(score)
                    maxima(s, 0, 4 * g2, 4, b[:, :].rearrange("p (h t) -> p h t", h=4))

                def score_max1(s, p2):
                    b, _ = bank(score)
                    maxima(s, 1, 2 * p2, 2, b[:, 0:2 * KEYS].rearrange("p (h t) -> p h t", h=2))

                def probs_T(s, ks):
                    for k in ks:
                        if k % 2:
                            b, free = bank(turn)
                            dve.wait_ge(turn.to_dve.sem, turn.to_dve.next())
                            ins = V.tensor_copy(pt[:, k // 2, 4 * (k % 2):4 * (k % 2) + 4, :],
                                                b[:, :].rearrange("p (h t) -> p h t", h=4))
                            ins.then_inc(free, 1)

                def attention_out(s, t):
                    b, free = bank(acc)
                    dve.wait_ge(acc.to_dve.sem, acc.to_dve.next())
                    link(V.reciprocal(rinv[s][:, t, :], rsum[s][:, t, :]))
                    ins = V.tensor_tensor(o_sb[s][:, t, :].rearrange("p (h d) -> p h d", h=H),
                                          b[:, :].rearrange("p (h d) -> p h d", h=H),
                                          rinv[s][:, t, :].unsqueeze(2).broadcast_to([P, H, D]), ALU.mult)
                    ins.then_inc(free, 1)

                def attention_residual(s):
                    b, free = bank(acc)
                    dve.wait_ge(acc.to_dve.sem, acc.to_dve.next())
                    ins = V.tensor_tensor(x1[s][:, :, :], b[:, 0:SEQ].rearrange("p (t c) -> p t c", t=NT),
                                          xr[s][:, :, :], ALU.add)
                    link(ins)
                    dve.sem_inc(x1_ready[s].sem, 1)
                    dve.sem_inc(x1_pool[s].sem, 1)
                    dve.sem_inc(free, 1)

                def stats_of_shifted(s):
                    dve.wait_ge(half_kept[s].sem, half_kept[s].next())
                    dve.wait_ge(shifted[s].sem, shifted[s].next(32))
                    stats_of(s, xs[s])

                def hidden(s, k):
                    m = HB[k][1]
                    b, free = bank(proj)
                    dve.wait_ge(gelu_ready[s].sem, gelu_ready[s].next())
                    V.scalar_tensor_tensor(hid[s][0:m, k, :], b[0:m, SEQ:2 * SEQ], b1_c[0:m, s - 1, 0, k:k + 1],
                                           gel[s][0:m, k, :], ALU.add, ALU.mult).then_inc(free, 1)

                def mlp_residual(s):
                    b, free = bank(acc)
                    dve.wait_ge(acc.to_dve.sem, acc.to_dve.next())
                    dve.wait_ge(x1b_ready[s].sem, x1b_ready[s].next())
                    dst = xb[2] if s == 1 else x1[2]
                    link(V.tensor_tensor(dst[:, :, :], b[:, 0:SEQ].rearrange("p (t c) -> p t c", t=NT),
                                         x1b[s][:, :, :], ALU.add))
                    dve.sem_inc(free, 1)
                    if s == 1:
                        dve.sem_inc(res_ready[2].sem, 1)

                def pass_on(n):
                    link(V.tensor_copy(passed[n][:, :, :], passed[n - 1][:, :, :]))

                def keep(s):
                    link(V.tensor_copy(xr[s][:, :, :], xb[s][:, :, :]))

                def x_stats(s):
                    dve.wait_ge(x_loaded.sem, x_loaded.next(16))
                    stats_of(s, x_in)

                def last_head_outputs(s):
                    head_outputs(s, 1, 1)
                    stats_of(s, hs)

                def final(s):
                    normalise(s, x1[s], x1[s], None, link_it=True)
                    link(V.tensor_tensor(y[:, :, :], x1[s][:, :, :], passed[-1][:, :, :], ALU.add))
                    dve.sem_inc(y_ready.sem, 1)

                for c in prod_free:
                    dve.sem_inc(c.sem, 1)
                walk(VECTOR, dve, {
                    "x_stats": x_stats,
                    "x_norm": lambda s: normalise(s, nrm[s], x_in, nrm_ready[s]),
                    "gates": gates,
                    "gate_bias": source_bias,
                    "heads_k": mlstm_k,
                    "weights0": lambda s: weigh0(s, (0, 1)),
                    "weights1": lambda s: weigh0(s, (2, 3)),
                    "weights2": weigh1,
                    "heads_out0": lambda s: head_outputs(s, 0, 0),
                    "heads_out1": lambda s: head_outputs(s, 0, 1),
                    "heads_out2": lambda s: head_outputs(s, 1, 0),
                    "heads_out3": last_head_outputs,
                    "outputs_norm": lambda s: normalise(s, hs, hs, hn_ready),
                    "mlstm_project": project_out,
                    "mlstm_residual": mlstm_residual,
                    "mlstm_out": lambda s: normalise(s, xb[1], passed[0], res_ready[1]),
                    "pass_front": lambda s: pass_on(2 * s - 1),
                    "pass_back": lambda s: pass_on(2 * s),
                    "keep": keep,
                    "query0": lambda s: rotary_product(s, 0, 0),
                    "key0": lambda s: rotary_product(s, 0, 1),
                    "query1": lambda s: rotary_product(s, 1, 0),
                    "key1": lambda s: rotary_product(s, 1, 1),
                    "scores0": lambda s: score_max0(s, 0),
                    "scores1": lambda s: score_max0(s, 1),
                    "scores2": lambda s: score_max1(s, 0),
                    "scores3": lambda s: score_max1(s, 1),
                    "scores4": lambda s: score_max1(s, 2),
                    "scores5": lambda s: score_max1(s, 3),
                    "probs0": lambda s: probs_T(s, (0, 1)),
                    "probs1": lambda s: probs_T(s, (2, 3)),
                    "probs2": lambda s: probs_T(s, (4, 5)),
                    "values0": lambda s: attention_out(s, 0),
                    "values1": lambda s: attention_out(s, 1),
                    "residual": attention_residual,
                    "shifted_stats": stats_of_shifted,
                    "shifted_norm": lambda s: normalise(s, nrm[s], xs[s], nrm_ready[s]),
                    "mlp_up0": lambda s: hidden(s, 0),
                    "mlp_up1": lambda s: hidden(s, 1),
                    "mlp_up2": lambda s: hidden(s, 2),
                    "mlp_down": mlp_residual,
                    "final_stats": lambda s: stats_of(s, x1[s]),
                    "final": final,
                }, lambda: settle(dve, [r.to_dve for r in RINGS] + [x_loaded] + [*shifted.values()] + prod_free +
                                  [*rstd_ready.values(), *sq_ready.values(), *half_kept.values(), *gelu_ready.values(),
                                   *x1b_ready.values(), *qnorm_ready.values(), v_step, dec_masked]))


_INS = ["L0_attn_x", "L0_attn_Wq", "L0_attn_Wk", "L0_attn_Wv", "L0_attn_Wi", "L0_attn_bi", "L0_attn_Wf", "L0_attn_bf",
        "L0_attn_Wo", "L0_attn_bo", "L0_attn_W_out", "L0_attn_ln_g", "L0_attn_ln_b", "L0_ffn_wqkv", "L0_ffn_q_scale",
        "L0_ffn_k_scale", "L0_ffn_wo", "L0_ffn_ln_g", "L0_ffn_ln_b", "L0_ffn_w1", "L0_ffn_b1", "L0_ffn_w2", "L0_ffn_b2"]


def rotary_factors():
    import numpy as np

    half = np.arange(0, D, 2, dtype=np.float32)
    inv_freq = (np.float32(1.0) / np.float32(10000.0) ** (half / np.float32(D))).astype(np.float32)
    t = np.arange(SEQ, dtype=np.float32)
    freqs = np.concatenate([t[:, None] * inv_freq[None, :]] * 2, axis=-1)
    base = ((half + np.float32(0.4 * D)) / np.float32(1.4 * D)).astype(np.float32)
    power = ((t - SEQ // 2) / np.float32(WINDOW // 2)).astype(np.float32)
    scale = np.concatenate([base[None, :].astype(np.float64) ** power[:, None]] * 2, axis=-1)
    cos, sin = np.cos(freqs.astype(np.float64)), np.sin(freqs.astype(np.float64))
    sign = np.concatenate([np.ones(D // 2), -np.ones(D // 2)])
    q = np.stack([cos * scale, sin * scale * sign], axis=1) * 8.0
    k = np.stack([cos / scale, sin / scale * sign], axis=1)
    return np.ascontiguousarray(np.stack([q, k], axis=1).reshape(SEQ, 4 * D).astype(np.float32))


def kernel(**inputs):
    import numpy as _np
    import concourse.bacc as _bacc
    from concourse import mybir as _mybir
    from concourse.bass_utils import run_bass_kernel_spmd as _run

    nc = _bacc.Bacc("TRN2", target_bir_lowering=False, num_devices=1)
    arrays, args = {}, []
    for name in _INS + ["rotary"]:
        a = rotary_factors() if name == "rotary" else _np.ascontiguousarray(inputs[name])
        arrays[f"in_{name}_dram"] = a
        args.append(nc.dram_tensor(f"in_{name}_dram", a.shape, _mybir.dt.from_np(a.dtype), kind="ExternalInput").ap())
    shape = arrays["in_L0_attn_x_dram"].shape
    args.append(nc.dram_tensor("out_dram", shape, _mybir.dt.float32, kind="ExternalOutput").ap())
    block_kernel(nc, *args)
    r = _run(nc, [arrays], core_ids=[0])
    return r.results[0]["out_dram"]
```
